# Optimizing a Trainium2 kernel written in Bass

```python
import numpy as np
import jax
import jax.numpy as jnp

def _softmax(x, axis=-1):
    return jax.nn.softmax(x, axis=axis)

def _gelu(x):
    return jax.nn.gelu(x, approximate=True)

def _silu(x):
    return jax.nn.silu(x)

def _sigmoid(x):
    return jax.nn.sigmoid(x)

def _layernorm(x, axis=-1, eps=1e-05):
    m = jnp.mean(x, axis=axis, keepdims=True)
    v = jnp.var(x, axis=axis, keepdims=True)
    return (x - m) / jnp.sqrt(v + eps)

def _scatter_add(tgt, idx, src, axis=0):
    return tgt.at[idx].add(src)

def _segment_sum(src, seg, n):
    return jax.ops.segment_sum(src, seg, n)
kernel_name = 'mk_gnn_preln_d4_gnn_r32_513a4c'

def setup_inputs(seed: int=0):
    np.random.seed(seed)
    _w = jnp.asarray

    def _rec_inputs():
        import jax
        import jax.numpy as jnp
        _gk = jax.random.key(seed)
        x = -0.000202 + 1 * jax.random.normal(jax.random.fold_in(_gk, 1), (3125, 128), jnp.float32)
        _s = jax.random.randint(jax.random.fold_in(_gk, 2), (25000,), 0, 3125, jnp.int32)
        _d = jax.random.randint(jax.random.fold_in(_gk, 3), (25000,), 0, 3125, jnp.int32)
        _loop = jnp.arange(3125, dtype=jnp.int32)
        src = jnp.concatenate([_s, _d, _loop])
        dst = jnp.concatenate([_d, _s, _loop])
        _o = jnp.argsort(dst, stable=True)
        src = src[_o]
        dst = dst[_o]
        edge_attr_128 = -6.74381e-05 + 0.999835 * jax.random.normal(jax.random.fold_in(_gk, 11), (53125, 128), jnp.float32)
        return (x, src, dst, edge_attr_128)
    x, src, dst, edge_attr_128 = _rec_inputs()

    def _L0_gnn_setup():
        import jax, jax.numpy as jnp
        import numpy as np
        N_NODES = 50000
        N_EDGES = 625000
        D = 128
        SLOPE = 0.2
        key = jax.random.key(seed)
        ks = jax.random.split(key, 16)
        s = 1.0 / np.sqrt(D)
        inp = {'V': jax.random.normal(ks[0], (N_NODES, D), jnp.float32), 'E': jax.random.normal(ks[1], (N_EDGES, D), jnp.float32), 'edge_index': jax.random.randint(ks[2], (2, N_EDGES), 0, N_NODES, jnp.int64), 'Wq_w': jax.random.uniform(ks[3], (D, D), jnp.float32, -s, s), 'Wq_b': jax.random.uniform(ks[4], (D,), jnp.float32, -s, s), 'Wk_w': jax.random.uniform(ks[5], (D, D), jnp.float32, -s, s), 'Wk_b': jax.random.uniform(ks[6], (D,), jnp.float32, -s, s), 'Wv_w': jax.random.uniform(ks[7], (D, D), jnp.float32, -s, s), 'Wv_b': jax.random.uniform(ks[8], (D,), jnp.float32, -s, s), 'We_w': jax.random.uniform(ks[9], (D, D), jnp.float32, -s, s), 'We_b': jax.random.uniform(ks[10], (D,), jnp.float32, -s, s), 'a_w': jax.random.uniform(ks[11], (1, D), jnp.float32, -s, s), 'a_b': jax.random.uniform(ks[12], (1,), jnp.float32, -s, s)}
        return inp
    _L0_gnn_all = _L0_gnn_setup()
    _L0_gnn_in = {k: v for k, v in _L0_gnn_all.items() if k in ('Wq_w', 'Wq_b', 'Wk_w', 'Wk_b', 'Wv_w', 'Wv_b', 'We_w', 'We_b', 'a_w', 'a_b')}
    del _L0_gnn_all

    def _L1_gnn_setup():
        import jax, jax.numpy as jnp
        import numpy as np
        NEG_SLOPE = 0.2

        def gat_layer(x, src, dst, n, W, a_src, a_dst, b):
            h = x @ W
            al_s = h @ a_src
            al_d = h @ a_dst
            e = jax.nn.leaky_relu(al_s[src] + al_d[dst], NEG_SLOPE)
            m = jax.ops.segment_max(e, dst, num_segments=n)
            ex = jnp.exp(e - m[dst])
            z = jax.ops.segment_sum(ex, dst, num_segments=n)
            alpha = ex / z[dst]
            out = jax.ops.segment_sum(alpha[:, None] * h[src], dst, num_segments=n)
            return out + b
        key = jax.random.key(seed)
        N, E, D, L = (3125, 50000, 128, 3)
        ks = jax.random.split(key, 6)
        x = jax.random.normal(ks[0], (N, D), dtype=jnp.float32)
        edge_index = jax.random.randint(ks[1], (2, E), 0, N, dtype=jnp.int32)
        W = jax.random.normal(ks[2], (L, D, D), dtype=jnp.float32) / np.sqrt(D)
        a_src = jax.random.normal(ks[3], (L, D), dtype=jnp.float32) / np.sqrt(D)
        a_dst = jax.random.normal(ks[4], (L, D), dtype=jnp.float32) / np.sqrt(D)
        b = jnp.zeros((L, D), dtype=jnp.float32)
        return {'x': x, 'edge_index': edge_index, 'W': W, 'a_src': a_src, 'a_dst': a_dst, 'b': b}
    _L1_gnn_all = _L1_gnn_setup()
    _L1_gnn_in = {k: v for k, v in _L1_gnn_all.items() if k in ('W', 'a_src', 'a_dst', 'b')}
    del _L1_gnn_all

    def _L2_gnn_setup():
        import jax, jax.numpy as jnp
        import numpy as np
        N, D, DEG, DEPTH = (50000, 128, 32, 1)
        ALPHA = 0.5
        key = jax.random.key(seed)
        k1, k2, k3 = jax.random.split(key, 3)
        features = jax.random.normal(k1, (N, D), dtype=jnp.float32)
        rows = jnp.repeat(jnp.arange(N), DEG)
        offsets = jnp.arange(DEG) * (N // DEG)
        cols = (jnp.arange(N)[:, None] * 13 + offsets[None, :]) % N
        cols = jnp.sort(cols, axis=1).reshape(-1)
        adj_nei = jnp.stack([rows, cols], axis=0)
        bound = float(np.sqrt(6.0 / (D + 1)))
        high_atts = jax.random.uniform(k2, (DEPTH, D), minval=-bound, maxval=bound, dtype=jnp.float32)
        diff_atts = jax.random.uniform(k3, (DEPTH, D), minval=-bound, maxval=bound, dtype=jnp.float32)
        return {'features': features, 'adj_nei': adj_nei, 'high_atts': high_atts, 'diff_atts': diff_atts}
    _L2_gnn_all = _L2_gnn_setup()
    _L2_gnn_in = {k: v for k, v in _L2_gnn_all.items() if k in ('high_atts', 'diff_atts')}
    del _L2_gnn_all

    def _L3_gnn_setup():
        import jax, jax.numpy as jnp
        import numpy as np
        N_NODES = 3125
        N_EDGES = 50000
        D = 128
        N_LAYERS = 3
        BN_EPS = 1e-05
        key = jax.random.key(seed)
        ks = jax.random.split(key, 8)
        x = jax.random.normal(ks[0], (N_NODES, D), dtype=jnp.float32)
        edge_index = jax.random.randint(ks[1], (2, N_EDGES), 0, N_NODES, dtype=jnp.int64)
        scale = 1.0 / np.sqrt(D)
        W1 = jax.random.normal(ks[2], (N_LAYERS, D, D), dtype=jnp.float32) * scale
        b1 = jax.random.normal(ks[3], (N_LAYERS, D), dtype=jnp.float32) * 0.01
        gamma = jnp.ones((N_LAYERS, D), dtype=jnp.float32)
        beta = jnp.zeros((N_LAYERS, D), dtype=jnp.float32)
        bn_mean = jax.random.normal(ks[4], (N_LAYERS, D), dtype=jnp.float32) * 0.01
        bn_var = jax.random.uniform(ks[5], (N_LAYERS, D), dtype=jnp.float32, minval=0.5, maxval=1.5)
        W2 = jax.random.normal(ks[6], (N_LAYERS, D, D), dtype=jnp.float32) * scale
        b2 = jax.random.normal(ks[7], (N_LAYERS, D), dtype=jnp.float32) * 0.01
        return {'x': x, 'edge_index': edge_index, 'W1': W1, 'b1': b1, 'gamma': gamma, 'beta': beta, 'bn_mean': bn_mean, 'bn_var': bn_var, 'W2': W2, 'b2': b2}
    _L3_gnn_all = _L3_gnn_setup()
    _L3_gnn_in = {k: v for k, v in _L3_gnn_all.items() if k in ('W1', 'b1', 'gamma', 'beta', 'bn_mean', 'bn_var', 'W2', 'b2')}
    del _L3_gnn_all
    return {'x': x, 'src': src, 'dst': dst, 'edge_attr_128': edge_attr_128, 'L0_gnn_Wq_w': _L0_gnn_in['Wq_w'], 'L0_gnn_Wq_b': _L0_gnn_in['Wq_b'], 'L0_gnn_Wk_w': _L0_gnn_in['Wk_w'], 'L0_gnn_Wk_b': _L0_gnn_in['Wk_b'], 'L0_gnn_Wv_w': _L0_gnn_in['Wv_w'], 'L0_gnn_Wv_b': _L0_gnn_in['Wv_b'], 'L0_gnn_We_w': _L0_gnn_in['We_w'], 'L0_gnn_We_b': _L0_gnn_in['We_b'], 'L0_gnn_a_w': _L0_gnn_in['a_w'], 'L0_gnn_a_b': _L0_gnn_in['a_b'], 'L1_gnn_W': _L1_gnn_in['W'], 'L1_gnn_a_src': _L1_gnn_in['a_src'], 'L1_gnn_a_dst': _L1_gnn_in['a_dst'], 'L1_gnn_b': _L1_gnn_in['b'], 'L2_gnn_high_atts': _L2_gnn_in['high_atts'], 'L2_gnn_diff_atts': _L2_gnn_in['diff_atts'], 'L3_gnn_W1': _L3_gnn_in['W1'], 'L3_gnn_b1': _L3_gnn_in['b1'], 'L3_gnn_gamma': _L3_gnn_in['gamma'], 'L3_gnn_beta': _L3_gnn_in['beta'], 'L3_gnn_bn_mean': _L3_gnn_in['bn_mean'], 'L3_gnn_bn_var': _L3_gnn_in['bn_var'], 'L3_gnn_W2': _L3_gnn_in['W2'], 'L3_gnn_b2': _L3_gnn_in['b2']}

def reference(x, src, dst, edge_attr_128, L0_gnn_Wq_w, L0_gnn_Wq_b, L0_gnn_Wk_w, L0_gnn_Wk_b, L0_gnn_Wv_w, L0_gnn_Wv_b, L0_gnn_We_w, L0_gnn_We_b, L0_gnn_a_w, L0_gnn_a_b, L1_gnn_W, L1_gnn_a_src, L1_gnn_a_dst, L1_gnn_b, L2_gnn_high_atts, L2_gnn_diff_atts, L3_gnn_W1, L3_gnn_b1, L3_gnn_gamma, L3_gnn_beta, L3_gnn_bn_mean, L3_gnn_bn_var, L3_gnn_W2, L3_gnn_b2):
    import jax
    import jax.numpy as jnp

    def _L0_gnn_ref(V, E, edge_index, Wq_w, Wq_b, Wk_w, Wk_b, Wv_w, Wv_b, We_w, We_b, a_w, a_b):
        import jax, jax.numpy as jnp
        import numpy as np
        N_NODES = 50000
        N_EDGES = 625000
        D = 128
        SLOPE = 0.2
        src, dest = (edge_index[0], edge_index[1])
        n_nodes = V.shape[0]
        Q = V[src] @ Wq_w.T + Wq_b
        K = V[dest] @ Wk_w.T + Wk_b
        Vv = V[dest] @ Wv_w.T + Wv_b
        bias = E @ We_w.T + We_b
        z = jax.nn.leaky_relu(Q + K + bias, SLOPE)
        scores = z @ a_w.T + a_b
        m = jax.ops.segment_max(scores, dest, num_segments=n_nodes)
        e = jnp.exp(scores - m[dest])
        denom = jax.ops.segment_sum(e, dest, num_segments=n_nodes)
        alpha = e / denom[dest]
        H = jax.ops.segment_sum(alpha * Vv, dest, num_segments=n_nodes)
        return H

    def _L1_gnn_ref(x, edge_index, W, a_src, a_dst, b):
        import jax, jax.numpy as jnp
        import numpy as np
        NEG_SLOPE = 0.2

        def gat_layer(x, src, dst, n, W, a_src, a_dst, b):
            h = x @ W
            al_s = h @ a_src
            al_d = h @ a_dst
            e = jax.nn.leaky_relu(al_s[src] + al_d[dst], NEG_SLOPE)
            m = jax.ops.segment_max(e, dst, num_segments=n)
            ex = jnp.exp(e - m[dst])
            z = jax.ops.segment_sum(ex, dst, num_segments=n)
            alpha = ex / z[dst]
            out = jax.ops.segment_sum(alpha[:, None] * h[src], dst, num_segments=n)
            return out + b
        n = x.shape[0]
        loop = jnp.arange(n, dtype=edge_index.dtype)
        src = jnp.concatenate([edge_index[0], loop])
        dst = jnp.concatenate([edge_index[1], loop])
        h = x
        for l in range(W.shape[0]):
            h = gat_layer(h, src, dst, n, W[l], a_src[l], a_dst[l], b[l])
            h = jax.nn.relu(h)
        return h

    def _L2_gnn_ref(features, adj_nei, high_atts, diff_atts):
        import jax, jax.numpy as jnp
        import numpy as np
        N, D, DEG, DEPTH = (50000, 128, 32, 1)
        ALPHA = 0.5
        n = features.shape[0]
        rows = adj_nei[0]
        cols = adj_nei[1]
        x = jnp.tanh(features)
        for l in range(high_atts.shape[0]):
            neighs = x[cols]
            score = neighs @ high_atts[l] - ALPHA * (neighs @ diff_atts[l])
            m = jax.ops.segment_max(score, rows, num_segments=n, indices_are_sorted=True)
            e = jnp.exp(score - m[rows])
            s = jax.ops.segment_sum(e, rows, num_segments=n, indices_are_sorted=True)
            att = e / s[rows]
            out = jax.ops.segment_sum(neighs * att[:, None], rows, num_segments=n, indices_are_sorted=True)
            x = jnp.tanh(out)
        return x

    def _L3_gnn_ref(x, edge_index, W1, b1, gamma, beta, bn_mean, bn_var, W2, b2):
        import jax, jax.numpy as jnp
        import numpy as np
        N_NODES = 3125
        N_EDGES = 50000
        D = 128
        N_LAYERS = 3
        BN_EPS = 1e-05
        src = edge_index[0]
        dst = edge_index[1]
        n = x.shape[0]
        h = x
        for l in range(N_LAYERS):
            agg = jax.ops.segment_sum(h[src], dst, num_segments=n)
            z = h + agg
            z = z @ W1[l] + b1[l]
            z = (z - bn_mean[l]) * jax.lax.rsqrt(bn_var[l] + BN_EPS) * gamma[l] + beta[l]
            z = jax.nn.relu(z)
            h = jax.nn.relu(z @ W2[l] + b2[l])
        return h
    edge_index = jnp.stack([src, dst])
    h = jnp.maximum(_layernorm(x, axis=-1), 0.0)
    x = x + _L0_gnn_ref(h, edge_attr_128, edge_index, L0_gnn_Wq_w, L0_gnn_Wq_b, L0_gnn_Wk_w, L0_gnn_Wk_b, L0_gnn_Wv_w, L0_gnn_Wv_b, L0_gnn_We_w, L0_gnn_We_b, L0_gnn_a_w, L0_gnn_a_b)
    h = jnp.maximum(_layernorm(x, axis=-1), 0.0)
    x = x + _L1_gnn_ref(h, edge_index, L1_gnn_W, L1_gnn_a_src, L1_gnn_a_dst, L1_gnn_b)
    h = jnp.maximum(_layernorm(x, axis=-1), 0.0)
    x = x + _L2_gnn_ref(h, edge_index, L2_gnn_high_atts, L2_gnn_diff_atts)
    h = jnp.maximum(_layernorm(x, axis=-1), 0.0)
    x = x + _L3_gnn_ref(h, edge_index, L3_gnn_W1, L3_gnn_b1, L3_gnn_gamma, L3_gnn_beta, L3_gnn_bn_mean, L3_gnn_bn_var, L3_gnn_W2, L3_gnn_b2)
    return x

_drawn_inputs = setup_inputs


def setup_inputs(seed=0):
    import zlib

    import numpy as np

    out = dict(_drawn_inputs(seed))
    spreads = {'L1_gnn_b': (0.0, 0.1), 'L3_gnn_gamma': (1.0, 0.2), 'L3_gnn_beta': (0.0, 0.8)}
    factors = {'edge_attr_128': 200.0,
     'L0_gnn_Wq_w': 200.0,
     'L0_gnn_Wq_b': 200.0,
     'L0_gnn_Wk_w': 200.0,
     'L0_gnn_Wk_b': 200.0,
     'L0_gnn_We_w': 200.0,
     'L0_gnn_We_b': 200.0,
     'L0_gnn_a_w': 200.0,
     'L1_gnn_a_src': 4.917,
     'L1_gnn_a_dst': 200.0,
     'L2_gnn_high_atts': 4.963,
     'L2_gnn_diff_atts': 8.0,
     'L3_gnn_b1': 43.999,
     'L3_gnn_bn_mean': 56.105,
     'L3_gnn_b2': 26.749}
    for name, (base, spread) in spreads.items():
        noise = np.random.default_rng([zlib.crc32(name.encode()), seed]).standard_normal(out[name].shape)
        drawn = base * np.exp(spread * noise) if base else spread * noise
        out[name] = jnp.asarray(drawn.astype(out[name].dtype))
    for name, factor in factors.items():
        out[name] = (out[name] * factor).astype(out[name].dtype)
    return out
```

```python
import numpy as np
import concourse.bass as bass
from concourse import mybir
from contextlib import ExitStack

fp32 = mybir.dt.float32
bf16 = mybir.dt.bfloat16
fp16 = mybir.dt.float16
i32 = mybir.dt.int32
ALU = mybir.AluOpType
ACT = mybir.ActivationFunctionType
AX = mybir.AxisListType

N = 3125
E = 53125
D = 128
P = 128
NB = -(-N // P)
NP = NB * P
FULL = N // P
REST = N - FULL * P
GB = 5
NG = NB // GB
CHUNK = GB * P

EP = 125
ET = E // EP
GT = 5
EG = ET // GT

CT_TILES = 6
SUPER = P * CT_TILES
NSUP = -(-E // SUPER)
TAIL = E - (NSUP - 1) * SUPER
WIN = 56
GWIN = 50
SLOTS = 3

SLOPE = 0.2
EPS = 1e-5
BIG = 1e38
CLAMP = 1e30
TINY = 1e-30
SAFE_RANGE = 60.0


def build(nc, T, out, stop=99):
    ctx = ExitStack()
    with ctx:
        stage_sems = []

        def sem(name):
            stage_sems.append(nc.alloc_semaphore(name=name))
            return stage_sems[-1]

        def end_stage():
            nc.clear_and_free_semaphores(stage_sems)
            nc.all_engine_barrier()
            stage_sems.clear()

        def sb(scope, name, shape, dt):
            return scope.enter_context(nc.sbuf_tensor(name, shape, dt))

        def pb(scope, name, shape, dt=fp32):
            return scope.enter_context(nc.psum_tensor(name, shape, dt))

        q_table = nc.dram_tensor("q_table", (NP, D), fp32, kind="Internal").ap()
        k_table = nc.dram_tensor("k_table", (NP, D), fp32, kind="Internal").ap()
        k_parts = nc.dram_tensor("k_parts", (NP, 3, D), bf16, kind="Internal").ap()
        s_dram = nc.dram_tensor("s_dram", (NSUP * SUPER,), fp32, kind="Internal").ap()
        v_table = nc.dram_tensor("v_table", (NP, D), fp32, kind="Internal").ap()
        x_dram = nc.dram_tensor("x_dram", (NP, D), fp32, kind="Internal").ap()

        counts = sb(ctx, "counts", [P, NB, NP], bf16)
        ident = sb(ctx, "ident", [P, P], fp32)
        identb = sb(ctx, "identb", [P, P], bf16)
        scores = sb(ctx, "scores", [P, ET], fp32)

        class Chain:
            def __init__(self, name, engine):
                self.sem, self.engine, self.n = sem(name), engine, 0

            def __call__(self, ins):
                self.n += 1
                ins.then_inc(self.sem, 1)
                self.engine.wait_ge(self.sem, self.n)
                return ins

        def node_view(table):
            return table.rearrange("(b p) d -> p b d", p=P)

        def load_x(sp, dst, done):
            sp.dma_start(dst[:, 0:FULL, :], T["x"][0:FULL * P, :].rearrange("(b p) d -> p b d", p=P)).then_inc(done, 16)
            sp.dma_start(dst[0:REST, FULL, :], T["x"][FULL * P:N, :]).then_inc(done, 16)

        def layernorm_relu(step, dve, x, h, sq, st, tag, var_ready, std_ready):
            step(nc.vector.tensor_reduce(st[:, 0, :], x[:, :, :], AX.X, ALU.add))
            step(nc.vector.tensor_scalar(st[:, 1, :], st[:, 0, :], 1.0 / D, None, ALU.mult))
            step(nc.vector.tensor_tensor(h[:, :, :], x[:, :, :], st[:, 1, :].unsqueeze(2).broadcast_to([P, NB, D]), ALU.subtract))
            step(nc.vector.tensor_tensor(sq[:, :, :], h[:, :, :], h[:, :, :], ALU.mult))
            step(nc.vector.tensor_reduce(st[:, 2, :], sq[:, :, :], AX.X, ALU.add))
            nc.vector.tensor_scalar(st[:, 3, :], st[:, 2, :], 1.0 / D, EPS, ALU.mult, ALU.add).then_inc(var_ready, 1)
            dve.wait_ge(std_ready, 1)
            step(nc.vector.reciprocal(st[:, 1, :], st[:, 0, :]))
            step(nc.vector.tensor_tensor(h[:, :, :], h[:, :, :], st[:, 1, :].unsqueeze(2).broadcast_to([P, NB, D]), ALU.mult))

        def tables():
            with ExitStack() as s:
                xN = sb(s, "t_x", [P, NB, D], fp32)
                hN = sb(s, "t_h", [P, NB, D], fp32)
                st = sb(s, "t_st", [P, 4, NB], fp32)
                wraw = sb(s, "t_wraw", [P, 3, D], fp32)
                wT = sb(s, "t_wT", [P, 3, D], fp32)
                brow = sb(s, "t_brow", [P, 4, D], fp32)
                hT = sb(s, "t_hT", [P, CHUNK], fp32)
                kp = sb(s, "t_kp", [P, GB, 3, D], bf16)
                rest = sb(s, "t_rest", [P, GB, D], fp32)
                qkv = xN[:, 0:15, :].rearrange("p (t b) d -> p t b d", t=3)
                pT = pb(s, "t_pT", [P, 1024])
                pQ = pb(s, "t_pQ", [P, GB, 512])
                x_in, w_in, made, id_made = sem("t_x_in"), sem("t_w_in"), sem("t_made"), sem("t_id_made")
                pad_zero, h_ready, var_ready, std_ready = sem("t_pad"), sem("t_hready"), sem("t_var"), sem("t_std")
                kp_sb = sem("t_kp_sb")
                w_tr, w_sb, tr, tr_sb, mm, q_sb, q_out = (sem(f"t_{n}") for n in ("w_tr", "w_sb", "tr", "tr_sb", "mm", "q_sb", "q_out"))
                step = Chain("t_dve", nc.vector)
                with nc.Block() as block:
                    @block.sync
                    def _(sp):
                        sp.wait_ge(pad_zero, 1)
                        load_x(sp, xN, x_in)
                        for k, w in enumerate(("L0_gnn_Wq_w", "L0_gnn_Wk_w", "L0_gnn_Wv_w")):
                            sp.dma_start(wraw[:, k, :], T[w]).then_inc(w_in, 16)
                        for k, b in enumerate(("L0_gnn_Wq_b", "L0_gnn_Wk_b", "L0_gnn_Wv_b", "L0_gnn_We_b")):
                            sp.dma_start(brow[:, k, :], T[b].unsqueeze(0).broadcast_to([P, D])).then_inc(w_in, 16)
                        for g in range(NG):
                            sp.wait_ge(q_sb, g + 1)
                            for k, table in enumerate((q_table, k_table, v_table)):
                                sp.dma_start(node_view(table)[:, g * GB:(g + 1) * GB, :], qkv[:, k, :, :]).then_inc(q_out, 16)
                            sp.wait_ge(kp_sb, g + 1)
                            sp.dma_start(k_parts.rearrange("(b p) t d -> p b t d", p=P)[:, g * GB:(g + 1) * GB, :, :], kp[:, :, :, :]).then_inc(q_out, 16)
                        sp.wait_ge(q_out, 64 * NG)

                    @block.gpsimd
                    def _(pool):
                        nc.gpsimd.memset(ident[:, :], 0.0).then_inc(made, 1)
                        pool.wait_ge(made, 1)
                        nc.gpsimd.affine_select(out=ident[:, :], in_=ident[:, :], compare_op=ALU.not_equal, fill=1.0,
                                                base=0, pattern=[[-1, P]], channel_multiplier=1).then_inc(id_made, 1)
                        pool.wait_ge(id_made, 1)
                        nc.gpsimd.tensor_copy(identb[:, :], ident[:, :]).then_inc(id_made, 1)
                        nc.gpsimd.memset(counts[:, 0:NB // 2, :], 0.0).then_inc(made, 1)

                    @block.scalar
                    def _(act):
                        act.wait_ge(var_ready, 1)
                        nc.scalar.activation(st[:, 0, :], st[:, 3, :], ACT.Sqrt).then_inc(std_ready, 1)
                        act.wait_ge(w_tr, 3)
                        nc.scalar.activation(wT[:, :, :].rearrange("p t d -> p (t d)"), pQ[:, 0, 0:3 * D], ACT.Copy).then_inc(w_sb, 1)
                        for g in range(NG):
                            act.wait_ge(tr, GB * (g + 1))
                            if g:
                                act.wait_ge(mm, GB * g)
                            nc.scalar.activation(hT[:, :], pT[:, 0:CHUNK], ACT.Copy).then_inc(tr_sb, 1)

                    @block.vector
                    def _(dve):
                        nc.vector.memset(xN[:, FULL, :], 0.0).then_inc(pad_zero, 1)
                        nc.vector.memset(counts[:, NB // 2:NB, :], 0.0)
                        dve.wait_ge(w_in, 16 * 7)
                        step(nc.vector.tensor_tensor(brow[:, 1, :], brow[:, 1, :], brow[:, 3, :], ALU.add))
                        dve.wait_ge(x_in, 32)
                        layernorm_relu(step, dve, xN, hN, xN, st, "t", var_ready, std_ready)
                        nc.vector.tensor_scalar(hN[:, :, :], hN[:, :, :], 0.0, None, ALU.max).then_inc(h_ready, 1)
                        for g in range(NG):
                            dve.wait_ge(mm, GB * (g + 1))
                            if g:
                                dve.wait_ge(q_out, 64 * g)
                            nc.vector.tensor_tensor(
                                qkv[:, :, :, :].rearrange("p t b d -> p b t d"),
                                pQ[:, :, 0:3 * D].rearrange("p b (t d) -> p b t d", t=3),
                                brow[:, 0:3, :].unsqueeze(1).broadcast_to([P, GB, 3, D]), ALU.add).then_inc(q_sb, 1)
                            dve.wait_ge(q_sb, g + 1)
                            step(nc.vector.tensor_copy(kp[:, :, 0, :], qkv[:, 1, :, :]))
                            step(nc.vector.tensor_tensor(rest[:, :, :], qkv[:, 1, :, :], kp[:, :, 0, :], ALU.subtract))
                            step(nc.vector.tensor_copy(kp[:, :, 1, :], rest[:, :, :]))
                            step(nc.vector.tensor_tensor(rest[:, :, :], rest[:, :, :], kp[:, :, 1, :], ALU.subtract))
                            nc.vector.tensor_copy(kp[:, :, 2, :], rest[:, :, :]).then_inc(kp_sb, 1)

                    @block.tensor
                    def _(pe):
                        pe.wait_ge(id_made, 1)
                        pe.wait_ge(w_in, 16 * 7)
                        for k in range(3):
                            nc.tensor.transpose(pQ[:, 0, k * D:(k + 1) * D], wraw[:, k, :], ident[:, :]).then_inc(w_tr, 1)
                        pe.wait_ge(w_sb, 1)
                        pe.wait_ge(h_ready, 1)
                        for g in range(NG):
                            if g:
                                pe.wait_ge(tr_sb, g)
                            for k in range(GB):
                                nc.tensor.transpose(pT[:, k * P:(k + 1) * P], hN[:, g * GB + k, :], ident[:, :]).then_inc(tr, 1)
                            pe.wait_ge(tr_sb, g + 1)
                            if g:
                                pe.wait_ge(q_sb, g)
                            for k in range(GB):
                                nc.tensor.matmul(pQ[:, k, 0:3 * D], hT[:, k * P:(k + 1) * P],
                                                 wT[:, :, :].rearrange("p t d -> p (t d)"), start=True, stop=True).then_inc(mm, 1)

        def edges():
            HB = [(0, 9), (9, 18), (18, NB)]
            QT = CT_TILES // 2
            QW = QT * P
            NT = NSUP * CT_TILES
            IN_INC = 16 * 4
            with ExitStack() as s:
                iota = sb(s, "e_iota", [P, NB * WIN], fp16)
                key = sb(s, "e_key", [P, NSUP, CT_TILES], fp32)
                lo = sb(s, "e_lo", [P, NSUP, CT_TILES], fp32)
                src_i = sb(s, "e_srci", [P, NSUP, CT_TILES], i32)
                win_i = sb(s, "e_wi", [P, NSUP], i32)
                win_p = sb(s, "e_wp", [P, NSUP], fp32)
                part = sb(s, "e_part", [P, 1], fp32)
                key_oh = sb(s, "e_koh", [P, SLOTS, NB * WIN], bf16)
                lo_oh = sb(s, "e_loh", [P, SLOTS, P], bf16)
                e_in = sb(s, "e_e", [P, 2, CT_TILES, D], fp32)
                eT = sb(s, "e_eT", [P, 2, QW], fp32)
                win_f = eT[:, 1, QW - NSUP:QW]
                z = sb(s, "e_z", [P, 4, QT, D], fp32)
                dst_row = sb(s, "e_drow", [P, 2, SUPER], i32)
                dst_oh = sb(s, "e_doh", [P, 2, SUPER], bf16)
                k_win = sb(s, "e_kwin", [P, 2, 3, D], bf16)
                weT = sb(s, "e_weT", [P, D], fp32)
                a_row = sb(s, "e_a", [P, D], fp32)
                a_bias = sb(s, "e_ab", [P, 1], fp32)
                idx = sb(s, "e_idx", [P, 4, QT], i32)
                idk = sb(s, "e_idk", [P, 4, QT], i32)
                dots = sb(s, "e_dots", [P, CT_TILES], fp32)
                small = sb(s, "e_small", [P, 4], fp32)
                ones_row = sb(s, "e_ones", [1, P], fp32)
                flag = sb(s, "e_flag", [P, 1], i32)
                found = sb(s, "e_found", [P, NB * WIN], bf16)
                dst_i = sb(s, "e_dsti", [P, NSUP, CT_TILES], i32)
                dstf = z[:, 0:2, :, :].rearrange("p a t d -> p (a t d)")[:, 0:NT].rearrange("p (s j) -> p s j", s=NSUP)
                tmp = z[:, 2:4, :, :].rearrange("p a t d -> p (a t d)")[:, 0:NT].rearrange("p (s j) -> p s j", s=NSUP)
                pC = pb(s, "e_pC", [P, 1536])
                pT = [pb(s, f"e_pT{q}", [P, 512]) for q in range(2)]
                pZ = [pb(s, f"e_pZ{q}", [P, 512]) for q in range(2)]
                pS = pb(s, "e_pS", [P, 512])
                names = ("pad", "idx_in", "w_in", "const", "we_tr", "we_sb", "prep", "fl_t", "fl_r", "fl_b", "gate", "tr_done", "eT_ready",
                         "oh_ready", "oh_used", "doh_ready", "found", "stored", "mm_done", "z_copied", "dot_done", "idx_ready", "own", "score", "out",
                         "back")
                S = {n: sem(f"e_{n}") for n in names}
                in_ready = [sem(f"e_in_ready{p}") for p in range(2)]
                q_ready = [sem(f"e_q_ready{p}") for p in range(4)]
                k_ready = [sem(f"e_k_ready{p}") for p in range(4)]
                step = Chain("e_dve", nc.vector)
                full = NSUP - 1
                rows = TAIL // CT_TILES
                left = TAIL - rows * CT_TILES
                e_rows = T["edge_attr_128"]
                e_view = e_rows[0:full * SUPER, :].rearrange("(s p j) d -> p s j d", p=P, j=CT_TILES)
                s_view = s_dram[0:NSUP * SUPER].rearrange("(s p j) -> p s j", p=P, j=CT_TILES)

                with nc.Block() as block:
                    @block.sync
                    def _(sp):
                        sp.wait_ge(S["pad"], 2)
                        for name, to in (("src", src_i), ("dst", dst_i)):
                            v = T[name]
                            m = full * SUPER
                            sp.dma_start(to[:, 0:full, :], v[0:m].rearrange("(s p j) -> p s j", p=P, j=CT_TILES)).then_inc(S["idx_in"], 16)
                            sp.dma_start(to[0:rows, full, :], v[m:m + rows * CT_TILES].rearrange("(p j) -> p j", j=CT_TILES)).then_inc(S["idx_in"], 16)
                            sp.dma_start(to[rows:rows + 1, full, 0:left], v[m + rows * CT_TILES:E].unsqueeze(0)).then_inc(S["idx_in"], 16)
                        sp.dma_start(win_i[:, :], T["dst"][0:full * SUPER + 1:SUPER].unsqueeze(0).broadcast_to([P, NSUP]),
                                     allow_slow_non_contiguous=True).then_inc(S["idx_in"], 16)
                        sp.dma_start(weT[:, :], T["L0_gnn_We_w"]).then_inc(S["w_in"], 16)
                        sp.dma_start(a_row[:, :], T["L0_gnn_a_w"].broadcast_to([P, D])).then_inc(S["w_in"], 16)
                        sp.dma_start(a_bias[:, :], T["L0_gnn_a_b"].unsqueeze(0).broadcast_to([P, 1])).then_inc(S["w_in"], 16)

                        def load_window(i, par):
                            at = sp.value_load(win_i[0:1, bass.ds(i, 1)], min_val=0, max_val=NP - WIN)
                            sp.dma_start(k_win[0:WIN, par, :, :], k_parts[bass.ds(at, WIN), :, :]).then_inc(in_ready[par], 16)

                        def load(i, par):
                            sp.wait_ge(S["mm_done"], i * 2 + 2)
                            for p0, p1 in ((0, P // 2), (P // 2, P)):
                                sp.dma_start(e_in[p0:p1, par, :, :], e_view[p0:p1, bass.ds(i, 1), :, :].squeeze(1)).then_inc(in_ready[par], 16)
                            sp.dma_start(dst_row[0:WIN, par, :], T["dst"][bass.ds(i * SUPER, SUPER)].unsqueeze(0).broadcast_to([WIN, SUPER])
                                         ).then_inc(in_ready[par], 16)
                            load_window(i, par)

                        def load_tail(i, par):
                            sp.wait_ge(S["mm_done"], i * 2 + 2)
                            m = i * SUPER
                            sp.dma_start(e_in[0:rows, par, :, :], e_rows[m:m + rows * CT_TILES, :].rearrange("(p j) d -> p j d", j=CT_TILES)
                                         ).then_inc(in_ready[par], 16)
                            sp.dma_start(e_in[rows:rows + 1, par, 0:left, :], e_rows[m + rows * CT_TILES:E, :].unsqueeze(0)).then_inc(in_ready[par], 16)
                            sp.dma_start(dst_row[0:WIN, par, 0:TAIL], T["dst"][m:E].unsqueeze(0).broadcast_to([WIN, TAIL])).then_inc(in_ready[par], 16)
                            load_window(i, par)

                        def store_scores(i):
                            sp.wait_ge(S["score"], i + 2)
                            sp.dma_start(s_view[:, bass.ds(i, 1), :].squeeze(1), scores[:, bass.ds(i * CT_TILES, CT_TILES)]).then_inc(S["out"], 16)

                        sp.wait_ge(S["prep"], 1)
                        for i in range(4):
                            load(i, i % 2)
                        with sp.Fori(2, NSUP // 2 - 1) as h:
                            for par in range(2):
                                load(h * 2 + par, par)
                                store_scores(h * 2 + par - 4)
                        load(NSUP - 2, 0)
                        load_tail(NSUP - 1, 1)
                        for i in range(NSUP - 6, NSUP):
                            store_scores(i)
                        sp.wait_ge(S["out"], 16 * NSUP)
                        sp.dma_start(scores[0:EP, :], s_dram[0:E].rearrange("(p j) -> p j", p=EP)).then_inc(S["back"], 16)

                    @block.gpsimd
                    def _(pool):
                        nc.gpsimd.iota(iota[:, :], pattern=[[1, NB * WIN]], base=0, channel_multiplier=0,
                                       allow_small_or_imprecise_dtypes=True).then_inc(S["const"], 1)
                        nc.gpsimd.iota(part[:, :], pattern=[[1, 1]], base=0, channel_multiplier=1,
                                       allow_small_or_imprecise_dtypes=True).then_inc(S["const"], 1)
                        nc.gpsimd.memset(ones_row[:, :], 1.0).then_inc(S["const"], 1)
                        pool.wait_ge(S["prep"], 2)

                        def gather(h, par, q, general):
                            i, g, slot = h * 2 + par, h * 4 + (par * 2 + q), par * 2 + q
                            pool.wait_ge(S["z_copied"], g + 3)
                            if general:
                                nc.gpsimd.tensor_copy(idk[:, slot, :], dst_i[:, bass.ds(i, 1), q * QT:(q + 1) * QT].squeeze(1))
                            nc.gpsimd.tensor_copy(idx[:, slot, :], src_i[:, bass.ds(i, 1), q * QT:(q + 1) * QT].squeeze(1)).then_inc(S["idx_ready"], 1)
                            pool.wait_ge(S["idx_ready"], g + 1)
                            pool.sem_inc(S["gate"], 1)
                            for k in range(QT):
                                nc.gpsimd.indirect_dma_start(out=z[:, slot, k, :], out_offset=None, in_=q_table,
                                                             in_offset=bass.IndirectOffsetOnAxis(ap=idx[:, slot, k:k + 1], axis=0),
                                                             compute_op=ALU.add).then_inc(q_ready[slot], 16)
                            if general:
                                pool.wait_ge(q_ready[slot], h * (16 * QT) + 16 * QT)
                                pool.sem_inc(S["gate"], 1)
                                for k in range(QT):
                                    nc.gpsimd.indirect_dma_start(out=z[:, slot, k, :], out_offset=None, in_=k_table,
                                                                 in_offset=bass.IndirectOffsetOnAxis(ap=idk[:, slot, k:k + 1], axis=0),
                                                                 compute_op=ALU.add).then_inc(k_ready[slot], 16)

                        def gathers(general):
                            with pool.Fori(0, NSUP // 2) as h:
                                for par in range(2):
                                    for q in range(2):
                                        gather(h, par, q, general)

                        general = pool.value_load(flag[0:1, 0:1], min_val=0, max_val=1)
                        with pool.If(general > 0):
                            gathers(True)
                        with pool.If(general < 1):
                            gathers(False)

                    @block.scalar
                    def _(act):
                        act.wait_ge(S["we_tr"], 1)
                        nc.scalar.activation(weT[:, :], pT[0][:, 0:D], ACT.Copy).then_inc(S["we_sb"], 1)
                        act.sem_inc(S["eT_ready"], 2)
                        act.sem_inc(S["z_copied"], 2)
                        act.sem_inc(S["found"], 1)
                        with act.Fori(0, NSUP // 2) as h:
                            for n in range(4):
                                g, q = h * 4 + n, n % 2
                                act.wait_ge(S["tr_done"], g + 1)
                                act.wait_ge(S["mm_done"], g + 3)
                                nc.scalar.activation(eT[:, q, :], pT[q][:, 0:QW], ACT.Copy).then_inc(S["eT_ready"], 1)
                                if q == 1:
                                    i = h * 2 + n // 2
                                    act.wait_ge(S["oh_used"], i * CT_TILES + CT_TILES + SLOTS)
                                    act.wait_ge(S["stored"], i + 1)
                                    for a, (b0, b1) in enumerate(HB):
                                        ins = nc.scalar.activation(found[:, b0 * WIN:b1 * WIN], pC[:, a * 512:a * 512 + (b1 - b0) * WIN], ACT.Copy)
                                    ins.then_inc(S["found"], 1)
                                act.wait_ge(S["mm_done"], g + 5)
                                act.wait_ge(S["dot_done"], g + 1)
                                nc.scalar.activation(z[:, n, :, :].rearrange("p t d -> p (t d)"), pZ[q][:, 0:QW], ACT.Copy).then_inc(S["z_copied"], 1)

                    @block.vector
                    def _(dve):
                        nc.vector.memset(src_i[:, full, :], 0).then_inc(S["pad"], 1)
                        nc.vector.memset(dst_i[:, full, :], NP - 1).then_inc(S["pad"], 1)
                        dve.wait_ge(S["idx_in"], 16 * 7)
                        dve.wait_ge(S["const"], 2)
                        step(nc.vector.tensor_copy(win_f, win_i[:, :]))
                        step(nc.vector.tensor_scalar(win_f, win_f, float(NP - WIN), None, ALU.min))
                        nc.vector.tensor_copy(win_i[:, :], win_f).then_inc(S["prep"], 1)
                        step(nc.vector.tensor_scalar(win_p[:, :], win_f, part[:, 0:1], None, ALU.add))
                        step(nc.vector.tensor_copy(dstf, dst_i[:, :, :]))
                        step(nc.vector.tensor_scalar(tmp.bitcast(i32), src_i[:, :, :], P - 1, None, ALU.bitwise_and))
                        step(nc.vector.tensor_copy(lo[:, :, :], tmp.bitcast(i32)))
                        step(nc.vector.tensor_copy(key[:, :, :], src_i[:, :, :]))
                        step(nc.vector.tensor_tensor(key[:, :, :], key[:, :, :], lo[:, :, :], ALU.subtract))
                        step(nc.vector.tensor_scalar(key[:, :, :], key[:, :, :], WIN / P, 1.0, ALU.mult, ALU.add))
                        step(nc.vector.tensor_tensor(tmp, dstf, win_f.unsqueeze(2).broadcast_to([P, NSUP, CT_TILES]), ALU.subtract))
                        step(nc.vector.tensor_tensor(key[:, :, :], key[:, :, :], tmp, ALU.add))
                        good = eT[:, :, :].rearrange("p a n -> p (a n)")[:, 0:NT].rearrange("p (s j) -> p s j", s=NSUP)
                        step(nc.vector.tensor_scalar(good, tmp, float(WIN), None, ALU.is_lt))
                        step(nc.vector.tensor_scalar(tmp, tmp, 0.0, None, ALU.is_ge))
                        step(nc.vector.tensor_tensor(good, good, tmp, ALU.mult))
                        step(nc.vector.tensor_scalar(dstf, dstf, float(N), None, ALU.is_lt))
                        step(nc.vector.tensor_tensor(good, good, dstf, ALU.mult))
                        step(nc.vector.tensor_tensor(key[:, :, :], key[:, :, :], good, ALU.mult))
                        step(nc.vector.tensor_scalar(key[:, :, :], key[:, :, :], 1.0, None, ALU.subtract))
                        step(nc.vector.tensor_tensor(dstf, dstf, good, ALU.subtract))
                        nc.vector.tensor_reduce(small[:, 0:1], dstf.rearrange("p s j -> p (s j)"), AX.X, ALU.max).then_inc(S["fl_r"], 1)
                        dve.wait_ge(S["fl_t"], 1)
                        nc.vector.tensor_reduce(small[0:1, 1:2], pS[0:1, 0:P], AX.X, ALU.max).then_inc(S["fl_r"], 1)
                        dve.wait_ge(S["fl_b"], 1)
                        step(nc.vector.tensor_copy(flag[:, :], pS[:, P:P + 1]))
                        nc.vector.scalar_tensor_tensor(win_p[:, :], flag[:, 0:1].broadcast_to([P, NSUP]), -2.0 * NP, win_p[:, :],
                                                       ALU.mult, ALU.add).then_inc(S["prep"], 1)
                        dve.wait_ge(S["prep"], 2)
                        dve.sem_inc(S["dot_done"], 4)
                        dve.sem_inc(S["stored"], 1)
                        dve.sem_inc(S["score"], 1)

                        def edge_loop(general):
                            def make_dst_oh(h, par):
                                i = h * 2 + par
                                dve.wait_ge(in_ready[par], h * IN_INC + IN_INC)
                                dve.wait_ge(S["mm_done"], i * 2 + 2)
                                nc.vector.tensor_scalar(dst_oh[0:WIN, par, :], dst_row[0:WIN, par, :], win_p[0:WIN, bass.ds(i, 1)], None,
                                                        ALU.is_equal).then_inc(S["doh_ready"], 1)

                            def make_oh(i, n):
                                dve.wait_ge(S["oh_used"], i * CT_TILES + n + 1)
                                nc.vector.tensor_scalar(lo_oh[:, n % SLOTS, :], iota[:, 0:P], lo[:, bass.ds(i, 1), n:n + 1].squeeze(1), None, ALU.is_equal)
                                nc.vector.tensor_scalar(key_oh[:, n % SLOTS, :], iota[:, :], key[:, bass.ds(i, 1), n:n + 1].squeeze(1), None,
                                                        ALU.is_equal).then_inc(S["oh_ready"], 1)

                            def store(i):
                                at = dve.value_load(win_i[0:1, bass.ds(i, 1)], min_val=0, max_val=NP - WIN)
                                dve.wait_ge(S["found"], i + 2)
                                dve.wait_ge(S["stored"], i + 1)
                                v = counts[:, :, bass.ds(at, WIN)]
                                nc.vector.tensor_tensor(v, v, found[:, :].rearrange("p (b w) -> p b w", w=WIN), ALU.add).then_inc(S["stored"], 1)

                            def dot(h, par, q):
                                i, g, slot = h * 2 + par, h * 4 + (par * 2 + q), par * 2 + q
                                ready = k_ready if general else q_ready
                                dve.wait_ge(ready[slot], h * (16 * QT) + 16 * QT)
                                v = z[:, slot, :, :].rearrange("p t d -> p (t d)")
                                nc.vector.scalar_tensor_tensor(v, v, SLOPE, v, ALU.mult, ALU.max).then_inc(S["own"], 1)
                                dve.wait_ge(S["own"], g + 1)
                                if q == 0:
                                    dve.wait_ge(S["score"], i + 1)
                                for k in range(QT):
                                    n = q * QT + k
                                    ins = nc.vector.tensor_tensor_reduce(out=z[:, slot, k, :], in0=z[:, slot, k, :], in1=a_row[:, :], scale=1.0,
                                                                         scalar=0.0, op0=ALU.mult, op1=ALU.add, accum_out=dots[:, n:n + 1])
                                ins.then_inc(S["dot_done"], 1)

                            def copy_scores(i):
                                dve.wait_ge(S["dot_done"], i * 2 + 6)
                                nc.vector.tensor_copy(scores[:, bass.ds(i * CT_TILES, CT_TILES)], dots[:, :]).then_inc(S["score"], 1)

                            def supertile(h, par, early=False):
                                i = h * 2 + par
                                before = (h, 0) if par else (h - 1, 1)
                                make_dst_oh(h, par)
                                for n in range(CT_TILES):
                                    make_oh(i, n)
                                    if n == 2 and not (early and par == 0):
                                        store(i - 1)
                                    if n == 3 and not early:
                                        dot(h - 1, par, 1)
                                        copy_scores(i - 2)
                                    if n == 5 and not (early and par == 0):
                                        dot(*before, 0)

                            supertile(0, 0, early=True)
                            supertile(0, 1, early=True)
                            with dve.Fori(1, NSUP // 2) as h:
                                supertile(h, 0)
                                supertile(h, 1)
                            store(NSUP - 1)
                            dot(NSUP // 2 - 1, 0, 1)
                            copy_scores(NSUP - 2)
                            dot(NSUP // 2 - 1, 1, 0)
                            dot(NSUP // 2 - 1, 1, 1)
                            copy_scores(NSUP - 1)

                        general = dve.value_load(flag[0:1, 0:1], min_val=0, max_val=1)
                        with dve.If(general > 0):
                            edge_loop(True)
                        with dve.If(general < 1):
                            edge_loop(False)
                        dve.wait_ge(S["back"], 16)
                        nc.vector.tensor_scalar(scores[0:EP, :], scores[0:EP, :], a_bias[0:EP, 0:1], None, ALU.add)

                    @block.tensor
                    def _(pe):
                        pe.sem_inc(S["mm_done"], 4)
                        pe.sem_inc(S["oh_used"], SLOTS)
                        pe.wait_ge(S["w_in"], 48)
                        nc.tensor.transpose(pT[0][:, 0:D], weT[:, :], ident[:, :]).then_inc(S["we_tr"], 1)
                        pe.wait_ge(S["we_sb"], 1)
                        pe.wait_ge(S["const"], 3)
                        pe.wait_ge(S["fl_r"], 1)
                        nc.tensor.transpose(pS[0:1, 0:P], small[:, 0:1], ident[:, :]).then_inc(S["fl_t"], 1)
                        pe.wait_ge(S["fl_r"], 2)
                        nc.tensor.matmul(pS[:, P:P + 1], ones_row[0:1, :], small[0:1, 1:2], start=True, stop=True).then_inc(S["fl_b"], 1)

                        def group(h, par, q):
                            i, g = h * 2 + par, h * 4 + (par * 2 + q)
                            if q == 0:
                                pe.wait_ge(in_ready[par], h * IN_INC + IN_INC)
                            pe.wait_ge(S["eT_ready"], g + 1)
                            for k in range(QT):
                                ins = nc.tensor.transpose(pT[q][:, k * P:(k + 1) * P], e_in[:, par, q * QT + k, :], ident[:, :])
                            ins.then_inc(S["tr_done"], 1)
                            if q == 0:
                                pe.wait_ge(S["found"], i + 1)
                            for n in range(q * QT, (q + 1) * QT):
                                pe.wait_ge(S["oh_ready"], i * CT_TILES + n + 1)
                                for a, (b0, b1) in enumerate(HB):
                                    ins = nc.tensor.matmul(pC[:, a * 512:a * 512 + (b1 - b0) * WIN], lo_oh[:, n % SLOTS, :],
                                                           key_oh[:, n % SLOTS, b0 * WIN:b1 * WIN], start=(n == 0), stop=(n == CT_TILES - 1), skip_group_check=True)
                                ins.then_inc(S["oh_used"], 1)
                            pe.wait_ge(S["eT_ready"], g + 3)
                            pe.wait_ge(S["doh_ready"], i + 1)
                            pe.wait_ge(S["z_copied"], g + 1)
                            for k in range(QT):
                                nc.tensor.matmul(pZ[q][:, k * P:(k + 1) * P], eT[:, q, k * P:(k + 1) * P], weT[:, :], start=(k == 0), stop=False,
                                                 skip_group_check=True)
                            for k in range(QT):
                                n = q * QT + k
                                for t in range(3):
                                    ins = nc.tensor.matmul(pZ[q][:, k * P:(k + 1) * P], dst_oh[0:WIN, par, n:n + (P - 1) * CT_TILES + 1:CT_TILES],
                                                           k_win[0:WIN, par, t, :], start=False, stop=(t == 2), skip_group_check=True)
                            ins.then_inc(S["mm_done"], 1)

                        with pe.Fori(0, NSUP // 2) as h:
                            for par in range(2):
                                for q in range(2):
                                    group(h, par, q)
                end_stage()
                general_counts(flag, iota, key, lo, src_i, dst_i, z, e_in, dst_oh, key_oh, lo_oh, small, pC, HB)

        def general_counts(flag, iota, key, lo, src_i, dst_i, z, e_in, zeros, key_oh, lo_oh, small, pC, HB):
            NT = NSUP * CT_TILES
            hi, dstf, rel, good = (t[:, 2 * (k % 2):2 * (k % 2) + 2].rearrange("p a t d -> p (a t d)")[:, 0:NT] if t is z else
                                   t[:, k % 2, :, :].rearrange("p t d -> p (t d)")[:, 0:NT] for k, t in enumerate((z, z, e_in, e_in)))
            keys, los, srcs, dsts = (t[:, :, :].rearrange("p s j -> p (s j)") for t in (key, lo, src_i, dst_i))
            start = small[:, 2:3]
            zero = zeros[:, 0, :]
            S = {n: sem(f"c_{n}") for n in ("made", "used", "zeroed", "stored", "own")}
            step = Chain("c_dve", nc.vector)
            STEPS = 7
            GROUPS = NT // SLOTS
            with nc.Block() as block:
                @block.vector
                def _(dve):
                    with dve.If(dve.value_load(flag[0:1, 0:1], min_val=0, max_val=1) > 0):
                        nc.vector.memset(zero, 0.0).then_inc(S["zeroed"], 1)
                        nc.vector.memset(start, 0.0)
                        step(nc.vector.tensor_copy(hi, srcs))
                        step(nc.vector.tensor_tensor(hi, hi, los, ALU.subtract))
                        step(nc.vector.tensor_scalar(hi, hi, GWIN / P, 1.0, ALU.mult, ALU.add))
                        step(nc.vector.tensor_copy(dstf, dsts))
                        step(nc.vector.tensor_scalar(rel, dstf, float(N), None, ALU.is_lt))
                        step(nc.vector.scalar_tensor_tensor(dstf, dstf, 1.0, rel, ALU.add, ALU.mult))
                        step(nc.vector.tensor_scalar(dstf, dstf, 1.0, None, ALU.subtract))
                        dve.sem_inc(S["used"], 1)
                        dve.sem_inc(S["own"], 1)
                        with dve.Fori(0, NP // GWIN) as w:
                            def own(n, ins):
                                ins.then_inc(S["own"], 1)
                                dve.wait_ge(S["own"], w * STEPS + n + 1)

                            dve.wait_ge(S["own"], w * STEPS + 1)
                            own(1, nc.vector.tensor_scalar(rel, dstf, start, None, ALU.subtract))
                            own(2, nc.vector.tensor_scalar(good, rel, float(GWIN), None, ALU.is_lt))
                            own(3, nc.vector.scalar_tensor_tensor(keys, rel, 0.0, good, ALU.is_ge, ALU.mult))
                            own(4, nc.vector.tensor_tensor(good, rel, hi, ALU.add))
                            own(5, nc.vector.tensor_tensor(keys, keys, good, ALU.mult))
                            own(6, nc.vector.tensor_scalar(keys, keys, 1.0, None, ALU.subtract))
                            nc.vector.tensor_scalar(start, start, float(GWIN), None, ALU.add).then_inc(S["own"], 1)
                            with dve.Fori(0, GROUPS) as t:
                                dve.wait_ge(S["used"], w * GROUPS + t + 1)
                                for n in range(SLOTS):
                                    nc.vector.tensor_scalar(lo_oh[:, n, :], iota[:, 0:P], los[:, bass.ds(t * SLOTS + n, 1)], None, ALU.is_equal)
                                    ins = nc.vector.tensor_scalar(key_oh[:, n, 0:NB * GWIN], iota[:, 0:NB * GWIN], keys[:, bass.ds(t * SLOTS + n, 1)], None, ALU.is_equal)
                                ins.then_inc(S["made"], 1)
                            dve.wait_ge(S["used"], w * GROUPS + GROUPS + 1)
                            for a, (b0, b1) in enumerate(HB):
                                ins = nc.vector.tensor_copy(counts[:, b0:b1, bass.ds(w * GWIN, GWIN)],
                                                            pC[:, a * 512:a * 512 + (b1 - b0) * GWIN].rearrange("p (b w) -> p b w", w=GWIN))
                            ins.then_inc(S["stored"], 1)

                @block.tensor
                def _(pe):
                    with pe.If(pe.value_load(flag[0:1, 0:1], min_val=0, max_val=1) > 0):
                        pe.wait_ge(S["zeroed"], 1)
                        pe.sem_inc(S["stored"], 1)
                        with pe.Fori(0, NP // GWIN) as w:
                            pe.wait_ge(S["stored"], w + 1)
                            for a, (b0, b1) in enumerate(HB):
                                nc.tensor.matmul(pC[:, a * 512:a * 512 + (b1 - b0) * GWIN], zero[:, 0:P], zero[:, 0:(b1 - b0) * GWIN], start=True, stop=False,
                                                 skip_group_check=True)
                            with pe.Fori(0, GROUPS) as t:
                                pe.wait_ge(S["made"], w * GROUPS + t + 1)
                                for n in range(SLOTS):
                                    for a, (b0, b1) in enumerate(HB):
                                        ins = nc.tensor.matmul(pC[:, a * 512:a * 512 + (b1 - b0) * GWIN], lo_oh[:, n, :],
                                                               key_oh[:, n, b0 * GWIN:b1 * GWIN], start=False, stop=True, skip_group_check=True)
                                ins.then_inc(S["used"], 1)

        def edge_softmax(hN):
            HC = 25
            LS = 5
            with ExitStack() as s:
                dst_i = sb(s, "s_dst_i", [P, ET + 2], i32)
                dstF = sb(s, "s_dstF", [P, ET + 2], fp32)
                link = sb(s, "s_link", [P, ET + 1], fp32)
                pen = sb(s, "s_pen", [P, ET + 1], fp32)
                fwd = sb(s, "s_fwd", [P, ET], fp32)
                bwd = sb(s, "s_bwd", [P, ET], fp32)
                col = sb(s, "s_col", [P, 4], fp32)
                carry = sb(s, "s_carry", [P, 2], fp32)
                row = sb(s, "s_row", [1, 4, P], fp32)
                rowc = sb(s, "s_rowc", [1, 2, P + 1], fp32)
                lo = sb(s, "s_lo", [P, ET], fp32)
                hi = sb(s, "s_hi", [P, ET], fp32)
                iota = sb(s, "s_iota", [P, P], fp16)
                iota25 = sb(s, "s_iota25", [P, NB], fp32)
                alpha = sb(s, "s_alpha", [P, 3, ET], bf16)
                lo_oh = sb(s, "s_lo_oh", [P, 2, LS, P], bf16)
                hi_oh = sb(s, "s_hi_oh", [P, 2, HC, NB], bf16)
                hi_al = sb(s, "s_hi_al", [P, 2, HC, 3, NB], bf16)
                zero = sb(s, "s_zero", [P, P], bf16)
                nodes = sb(s, "s_nodes", [P, 3, NB], fp32)
                parts = sb(s, "s_parts", [3 * NB, P], fp32)
                pR = pb(s, "s_pR", [P, 512])
                pN = pb(s, "s_pN", [P, 512])
                pX = pb(s, "s_pX", [P, 512])
                idx_in, const, row_t, col_t = sem("s_idx_in"), sem("s_const"), sem("s_row_t"), sem("s_col_t")
                row_ready, rc_ready, c_ready = sem("s_row_ready"), sem("s_rc"), sem("s_c")
                hi_ready, lo_ready, hist = sem("s_hi_ready"), sem("s_lo_ready"), sem("s_hist")
                own, pad, zeroed, turned = sem("s_own"), sem("s_pad"), sem("s_zeroed"), sem("s_turned")
                step = Chain("s_dve", nc.vector)
                passes = [(0, "max"), (1, "max"), (0, "sum"), (1, "sum")]

                with nc.Block() as block:
                    @block.sync
                    def _(sp):
                        sp.wait_ge(pad, 1)
                        sp.dma_start(dst_i[0:EP, 1:ET + 1], T["dst"].rearrange("(p j) -> p j", p=EP)).then_inc(idx_in, 16)
                        sp.dma_start(dst_i[1:EP, 0:1], T["dst"][ET - 1:E - ET:ET].unsqueeze(1), allow_slow_non_contiguous=True).then_inc(idx_in, 16)
                        sp.dma_start(dst_i[0:EP - 1, ET + 1:ET + 2], T["dst"][ET:E:ET].unsqueeze(1), allow_slow_non_contiguous=True).then_inc(idx_in, 16)

                    @block.gpsimd
                    def _(pool):
                        nc.gpsimd.iota(iota[:, :], pattern=[[1, P]], base=0, channel_multiplier=0,
                                       allow_small_or_imprecise_dtypes=True).then_inc(const, 1)
                        nc.gpsimd.iota(iota25[:, :], pattern=[[1, NB]], base=0, channel_multiplier=0,
                                       allow_small_or_imprecise_dtypes=True).then_inc(const, 1)

                        def weigh(i, par):
                            v = slice(0, EP)
                            pool.wait_ge(own, i + 1)
                            for k in range(3):
                                ins = nc.gpsimd.tensor_tensor(hi_al[v, par, :, k, :], hi_oh[v, par, :, :],
                                                              alpha[v, k, bass.ds(i * HC, HC)].unsqueeze(2).broadcast_to([EP, HC, NB]), ALU.mult)
                            ins.then_inc(hi_ready, 1)

                        weigh(0, 0)
                        with pool.Fori(0, ET // HC // 2) as i:
                            for par in range(2):
                                pool.wait_ge(hist, i * (2 * HC // LS) + par * (HC // LS) + 2)
                                weigh(i * 2 + par + 1, 1 - par)

                    @block.vector
                    def _(dve):
                        nc.vector.memset(zero[:, :], 0.0).then_inc(zeroed, 1)
                        nc.vector.memset(dst_i[:, :], -1).then_inc(pad, 1)
                        dve.wait_ge(idx_in, 48)
                        v = slice(0, EP)
                        step(nc.vector.tensor_copy(dstF[v, :], dst_i[v, :]))
                        step(nc.vector.tensor_tensor(link[v, :], dstF[v, 0:ET + 1], dstF[v, 1:ET + 2], ALU.is_equal))
                        step(nc.vector.tensor_scalar(pen[v, :], link[v, :], BIG, BIG, ALU.mult, ALU.subtract))
                        step(nc.vector.tensor_reduce(col[v, 1:2], link[v, 0:ET], AX.X, ALU.min))
                        step(nc.vector.tensor_reduce(col[v, 2:3], link[v, 1:ET + 1], AX.X, ALU.min))
                        val = scores
                        for n, (back, kind) in enumerate(passes):
                            o = bwd if back else fwd
                            data = val[v, 0:ET]
                            gate = (pen if kind == "max" else link)[v, 1:ET + 1] if back else (pen if kind == "max" else link)[v, 0:ET]
                            dest = o[v, :]
                            if back:
                                data, gate, dest = data[:, ::-1], gate[:, ::-1], dest[:, ::-1]
                            ops = (ALU.add, ALU.max) if kind == "max" else (ALU.mult, ALU.add)
                            start = -BIG if kind == "max" else 0.0
                            step(nc.vector.tensor_tensor_scan(dest, gate, data, start, *ops))
                            step(nc.vector.tensor_copy(col[v, 0:1], o[v, 0:1] if back else o[v, ET - 1:ET]))
                            step(nc.vector.tensor_copy(col[v, 3:4], col[v, 2:3] if back else col[v, 1:2]))
                            nc.vector.tensor_scalar(col[v, 3:4], col[v, 3:4], BIG if kind == "max" else 1.0,
                                                    BIG if kind == "max" else 0.0, ALU.mult, ALU.subtract).then_inc(row_ready, 1)
                            dve.wait_ge(row_t, 2 * (n + 1))
                            step(nc.vector.tensor_copy(row[0:1, 0, v], pR[0:1, 0:EP]))
                            step(nc.vector.tensor_copy(row[0:1, 1, v], pR[0:1, P:P + EP]))
                            step(nc.vector.memset(rowc[0:1, 0, :], start))
                            rd, rg, ro = row[0:1, 0, v], row[0:1, 1, v], (rowc[0:1, 0, 0:EP] if back else rowc[0:1, 0, 1:EP + 1])
                            if back:
                                rd, rg, ro = rd[:, ::-1], rg[:, ::-1], ro[:, ::-1]
                            step(nc.vector.tensor_tensor_scan(ro, rg, rd, start, *ops))
                            nc.vector.tensor_copy(rowc[0:1, 1, v], rowc[0:1, 0, 1:EP + 1] if back else rowc[0:1, 0, 0:EP]).then_inc(rc_ready, 1)
                            dve.wait_ge(col_t, n + 1)
                            step(nc.vector.tensor_copy(carry[v, 0:1], pR[v, 2 * P:2 * P + 1]))
                            step(nc.vector.tensor_tensor_scan(dest, gate, data, carry[v, 0:1], *ops))
                            if n == 1:
                                step(nc.vector.tensor_tensor(fwd[v, :], fwd[v, :], bwd[v, :], ALU.max))
                                nc.vector.tensor_tensor(scores[v, :], scores[v, :], fwd[v, :], ALU.subtract).then_inc(c_ready, 1)
                                dve.wait_ge(c_ready, 2)
                        step(nc.vector.tensor_tensor(fwd[v, :], fwd[v, :], bwd[v, :], ALU.add))
                        step(nc.vector.tensor_tensor(fwd[v, :], fwd[v, :], scores[v, :], ALU.subtract))
                        step(nc.vector.reciprocal(bwd[v, :], fwd[v, :]))
                        step(nc.vector.tensor_tensor(fwd[v, :], scores[v, :], bwd[v, :], ALU.mult))
                        for k in range(3):
                            step(nc.vector.tensor_copy(alpha[v, k, :], fwd[v, :]))
                            if k < 2:
                                step(nc.vector.tensor_tensor(fwd[v, :], fwd[v, :], alpha[v, k, :], ALU.subtract))
                        step(nc.vector.tensor_scalar(dst_i[v, :], dst_i[v, :], P - 1, None, ALU.bitwise_and))
                        step(nc.vector.tensor_copy(lo[v, :], dst_i[v, 1:ET + 1]))
                        step(nc.vector.tensor_tensor(hi[v, :], dstF[v, 1:ET + 1], lo[v, :], ALU.subtract))
                        step(nc.vector.tensor_scalar(hi[v, :], hi[v, :], 1.0 / P, None, ALU.mult))
                        dve.wait_ge(const, 2)
                        def make_hi(i, par):
                            nc.vector.tensor_tensor(hi_oh[v, par, :, :], hi[v, bass.ds(i * HC, HC)].unsqueeze(2).broadcast_to([EP, HC, NB]),
                                                    iota25[v, :].unsqueeze(1).broadcast_to([EP, HC, NB]), ALU.is_equal).then_inc(own, 1)

                        def make_lo(i, u0):
                            for u in range(HC // LS):
                                dve.wait_ge(hist, i * (HC // LS) + u + 1)
                                for j in range(u * LS, (u + 1) * LS):
                                    ins = nc.vector.tensor_scalar(lo_oh[v, (u0 + u) % 2, j % LS, :], iota[v, :], lo[v, bass.ds(i * HC + j, 1)], None, ALU.is_equal)
                                ins.then_inc(lo_ready, 1)

                        make_hi(0, 0)
                        with dve.Fori(0, ET // HC // 2) as i:
                            for par in range(2):
                                dve.wait_ge(hi_ready, i * 2 + par + 1)
                                make_hi(i * 2 + par + 1, 1 - par)
                                make_lo(i * 2 + par, par * (HC // LS))
                        make_lo(ET // HC - 1, 0)
                        dve.wait_ge(hist, ET // LS + 2)
                        nc.vector.tensor_copy(parts[:, :], pN[0:3 * NB, 0:P]).then_inc(own, 1)
                        dve.wait_ge(turned, 1)
                        step(nc.vector.tensor_copy(nodes[:, :, :], pX[:, 0:3 * NB].rearrange("p (k b) -> p k b", k=3)))
                        step(nc.vector.tensor_tensor(nodes[:, 0, :], nodes[:, 0, :], nodes[:, 1, :], ALU.add))
                        step(nc.vector.tensor_tensor(alpha_sum[:, :], nodes[:, 0, :], nodes[:, 2, :], ALU.add))

                    @block.scalar
                    def _(act):
                        act.wait_ge(c_ready, 1)
                        nc.scalar.activation(scores[0:EP, :], scores[0:EP, :], ACT.Exp).then_inc(c_ready, 1)

                    @block.tensor
                    def _(pe):
                        v = slice(0, EP)
                        for n in range(4):
                            pe.wait_ge(row_ready, n + 1)
                            nc.tensor.transpose(pR[0:1, 0:EP], col[v, 0:1], ident[v, v]).then_inc(row_t, 1)
                            nc.tensor.transpose(pR[0:1, P:P + EP], col[v, 3:4], ident[v, v]).then_inc(row_t, 1)
                            pe.wait_ge(rc_ready, n + 1)
                            nc.tensor.transpose(pR[v, 2 * P:2 * P + 1], rowc[0:1, 1, v], ident[0:1, 0:1]).then_inc(col_t, 1)
                        pe.wait_ge(zeroed, 1)
                        nc.tensor.matmul(pN[0:3 * NB, 0:P], zero[:, 0:3 * NB], zero[:, :], start=True, stop=False, skip_group_check=True).then_inc(hist, 2)

                        def products(i, par):
                            for j in range(HC):
                                if j == 0:
                                    pe.wait_ge(hi_ready, i + 1)
                                if j % LS == 0:
                                    pe.wait_ge(lo_ready, i * (HC // LS) + j // LS + 1)
                                ins = nc.tensor.matmul(pN[0:3 * NB, 0:P], hi_al[v, par, j, :, :].rearrange("p k b -> p (k b)"),
                                                       lo_oh[v, (par * (HC // LS) + j // LS) % 2, j % LS, :], start=False, stop=True, skip_group_check=True)
                                if j % LS == LS - 1:
                                    ins.then_inc(hist, 1)

                        with pe.Fori(0, ET // HC // 2) as i:
                            products(i * 2, 0)
                            products(i * 2 + 1, 1)
                        products(ET // HC - 1, 0)
                        pe.wait_ge(own, ET // HC + 1)
                        nc.tensor.transpose(pX[:, 0:3 * NB], parts[:, :], ident[0:3 * NB, 0:3 * NB]).then_inc(turned, 1)

        def residual(tag, hN, first=False, last=False, loops=None):
            with ExitStack() as s:
                xN = sb(s, f"{tag}_x", [P, NB, D], fp32)
                vN = sb(s, f"{tag}_v", [P, NB, D], fp32)
                st = sb(s, f"{tag}_st", [P, 4, NB], fp32)
                pad, x_in, x_new, x_out = (sem(f"{tag}_{n}") for n in ("pad", "x_in", "x_new", "x_out"))
                var_ready, std_ready = sem(f"{tag}_var"), sem(f"{tag}_std")
                step = Chain(f"{tag}_dve", nc.vector)
                flat = counts[:, :, :].rearrange("p b n -> p (b n)")
                own_block = NP + P
                with nc.Block() as block:
                    @block.sync
                    def _(sp):
                        if first:
                            sp.wait_ge(pad, 1)
                            load_x(sp, xN, x_in)
                            sp.dma_start(vN[:, :, :], node_view(v_table)).then_inc(x_in, 16)
                        else:
                            sp.dma_start(xN[:, :, :], node_view(x_dram)).then_inc(x_in, 16)
                        sp.wait_ge(x_new, 1)
                        if last:
                            sp.dma_start(out[0:FULL * P, :].rearrange("(b p) d -> p b d", p=P), xN[:, 0:FULL, :]).then_inc(x_out, 16)
                            sp.dma_start(out[FULL * P:N, :], xN[0:REST, FULL, :]).then_inc(x_out, 16)
                            sp.wait_ge(x_out, 32)
                        else:
                            sp.dma_start(node_view(x_dram), xN[:, :, :]).then_inc(x_out, 16)
                            sp.wait_ge(x_out, 16)

                    @block.scalar
                    def _(act):
                        if not last:
                            act.wait_ge(var_ready, 1)
                            nc.scalar.activation(st[:, 0, :], st[:, 3, :], ACT.Sqrt).then_inc(std_ready, 1)

                    @block.vector
                    def _(dve):
                        if loops is not None:
                            v = flat[:, 0:(NB - 1) * own_block].rearrange("p (b n) -> p b n", n=own_block)[:, :, 0:P]
                            nc.vector.tensor_tensor(v, v, identb[:, :].unsqueeze(1).broadcast_to([P, NB - 1, P]), loops)
                            v = flat[:, (NB - 1) * own_block:NB * NP]
                            nc.vector.tensor_tensor(v, v, identb[:, :], loops)
                        if first:
                            nc.vector.memset(xN[:, FULL, :], 0.0).then_inc(pad, 1)
                            dve.wait_ge(x_in, 48)
                            step(nc.vector.tensor_tensor(vN[:, :, :], vN[:, :, :], alpha_sum[:, :].unsqueeze(2).broadcast_to([P, NB, D]), ALU.mult))
                            add = vN
                        else:
                            dve.wait_ge(x_in, 16)
                            add = hN
                        nc.vector.tensor_tensor(xN[:, :, :], xN[:, :, :], add[:, :, :], ALU.add).then_inc(x_new, 1)
                        dve.wait_ge(x_new, 1)
                        if not last:
                            layernorm_relu(step, dve, xN, hN, vN, st, tag, var_ready, std_ready)
                            nc.vector.tensor_scalar(hN[:, :, :], hN[:, :, :], 0.0, None, ALU.max)

        def bank_of(k, w):
            return k * w if k < 3 else 512 + (k - 3) * w

        def logit_range(step, dve, logit, rng, neg, S, pR, flag):
            step(nc.vector.tensor_reduce(rng[:, 0:1], logit, AX.X, ALU.max))
            step(nc.vector.tensor_scalar(neg, logit, -1.0, None, ALU.mult))
            nc.vector.tensor_reduce(rng[:, 1:2], neg, AX.X, ALU.max).then_inc(S["rng_r"], 1)
            dve.wait_ge(S["rng_t"], 1)
            nc.vector.tensor_reduce(rng[0:1, 2:4], pR[0:1, 0:2 * P].rearrange("p (t n) -> p t n", t=2), AX.X, ALU.max).then_inc(S["rng_s"], 1)
            dve.wait_ge(S["rng_b"], 1)
            step(nc.vector.tensor_copy(rng[:, 4:6], pR[:, 2 * P:2 * P + 2]))
            step(nc.vector.tensor_tensor(rng[:, 6:7], rng[:, 4:5], rng[:, 5:6], ALU.add))
            step(nc.vector.tensor_scalar(flag[:, :], rng[:, 6:7], SAFE_RANGE, None, ALU.is_gt))
            step(nc.vector.tensor_scalar(rng[:, 6:7], rng[:, 6:7], TINY, 2.0, ALU.max, ALU.mult))
            step(nc.vector.reciprocal(rng[:, 7:8], rng[:, 6:7]))

        def logit_range_pe(pe, rng, ones, S, pR):
            pe.wait_ge(S["rng_r"], 1)
            for t in range(2):
                ins = nc.tensor.transpose(pR[0:1, t * P:(t + 1) * P], rng[:, t:t + 1], ident[:, :])
            ins.then_inc(S["rng_t"], 1)
            pe.wait_ge(S["rng_s"], 1)
            nc.tensor.matmul(pR[:, 2 * P:2 * P + 2], ones[0:1, :], rng[0:1, 2:4], start=True, stop=True).then_inc(S["rng_b"], 1)

        def gat(layer, hN):
            tag = f"g{layer}"
            wide = D + 2
            with ExitStack() as s:
                val = sb(s, f"{tag}_val", [P, NB, D + 1], fp32)
                acc = sb(s, f"{tag}_acc", [P, NP], fp32)
                e2 = sb(s, f"{tag}_e2", [P, 2, CHUNK], fp32)
                w_ext = sb(s, f"{tag}_w", [P, wide], fp32)
                a_col = sb(s, f"{tag}_a", [P, 2], fp32)
                b_row = sb(s, f"{tag}_b", [P, D], fp32)
                ones = sb(s, f"{tag}_ones", [P, P], fp32)
                al = sb(s, f"{tag}_al", [P, 2, NB], fp32)
                al2 = sb(s, f"{tag}_al2", [P, NB], fp32)
                ap = sb(s, f"{tag}_ap", [P, NB], fp32)
                amax = sb(s, f"{tag}_amax", [P, NB], fp32)
                m = sb(s, f"{tag}_m", [P, NB], fp32)
                R = sb(s, f"{tag}_R", [P, 2, NB + GB], fp32)
                rng = sb(s, f"{tag}_rng", [P, 8], fp32)
                flag = sb(s, f"{tag}_flag", [P, 1], i32)
                z = sb(s, f"{tag}_z", [P, GB], fp32)
                rz = sb(s, f"{tag}_rz", [P, GB], fp32)
                hT = acc[:, 0:2 * CHUNK].rearrange("p (t n) -> p t n", t=2)
                wT = acc[:, 2 * CHUNK:2 * CHUNK + D]
                diag = acc[:, 0:2 * CHUNK].rearrange("p (t b m) -> p t b m", t=2, b=GB)
                e1 = acc[:, 2 * CHUNK:(2 + SLOTS) * CHUNK].rearrange("p (t n) -> p t n", t=SLOTS)
                pR = pb(s, f"{tag}_pR", [P, 2, 1536])
                pO = pb(s, f"{tag}_pO", [P, 1024])

                S = {n: sem(f"{tag}_{n}") for n in ("w_in", "const", "w_tr", "w_sb", "wa", "wa_sb", "tr", "tr_sb", "lin", "lin_sb",
                                                     "rng_r", "rng_t", "rng_s", "rng_b")}
                step = Chain(f"{tag}_dve", nc.vector)

                def result(g, k):
                    o = k * wide if k < 3 else (k - 3) * wide
                    bank = (pO[:, 0:512] if k < 3 else pO[:, 512:1024]) if g % 2 == 0 else (pR[:, 0, 1024:1536] if k < 3 else pR[:, 1, 1024:1536])
                    return bank, o

                with nc.Block() as block:
                    @block.sync
                    def _(sp):
                        sp.dma_start(w_ext[:, 0:D], T["L1_gnn_W"][layer, :, :]).then_inc(S["w_in"], 16)
                        sp.dma_start(a_col[:, 0:1], T["L1_gnn_a_src"][layer, :].unsqueeze(1)).then_inc(S["w_in"], 16)
                        sp.dma_start(a_col[:, 1:2], T["L1_gnn_a_dst"][layer, :].unsqueeze(1)).then_inc(S["w_in"], 16)
                        sp.dma_start(b_row[:, :], T["L1_gnn_b"][layer, :].unsqueeze(0).broadcast_to([P, D])).then_inc(S["w_in"], 16)

                    @block.gpsimd
                    def _(pool):
                        nc.gpsimd.memset(ones[:, :], 1.0).then_inc(S["const"], 1)
                        nc.gpsimd.memset(val[:, :, D:D + 1], 1.0).then_inc(S["const"], 1)
                        nc.gpsimd.memset(R[:, :, NB:NB + GB], 0.0).then_inc(S["const"], 1)

                    @block.scalar
                    def _(act):
                        def copy_hT(g):
                            act.wait_ge(S["tr"], g + 1)
                            if g >= 2:
                                act.wait_ge(S["lin"], g - 1)
                            nc.scalar.activation(hT[:, g % 2, :], pR[:, g % 2, 0:CHUNK], ACT.Copy).then_inc(S["tr_sb"], 1)

                        copy_hT(0)
                        copy_hT(1)
                        act.wait_ge(S["w_tr"], 1)
                        nc.scalar.activation(wT, pO[:, 0:D], ACT.Copy).then_inc(S["w_sb"], 1)
                        act.wait_ge(S["wa"], 1)
                        nc.scalar.activation(w_ext[:, D:D + 2], pO[:, 0:2], ACT.Copy).then_inc(S["wa_sb"], 1)
                        for g in range(2, NG):
                            copy_hT(g)

                    @block.vector
                    def _(dve):
                        for g in range(NG):
                            dve.wait_ge(S["lin"], g + 1)
                            for k0, k1 in ((0, 3), (3, GB)):
                                bank, _o = result(g, k0)
                                o = bank[:, 0:(k1 - k0) * wide].rearrange("p (b w) -> p b w", w=wide)
                                nc.vector.tensor_copy(val[:, g * GB + k0:g * GB + k1, 0:D], o[:, :, 0:D])
                                ins = nc.vector.tensor_copy(al[:, :, g * GB + k0:g * GB + k1], o[:, :, D:D + 2].rearrange("p b t -> p t b"))
                            ins.then_inc(S["lin_sb"], 1)
                        dve.wait_ge(S["lin_sb"], NG)
                        step(nc.vector.tensor_scalar(al2[:, :], al[:, 0, :], SLOPE, None, ALU.mult))
                        logit_range(step, dve, al[:, 0, :], rng, ap[:, :], S, pR[:, 0, :], flag)
                        nc.vector.tensor_copy(amax[:, :], rng[:, 4:5].broadcast_to([P, NB]))

                    @block.tensor
                    def _(pe):
                        def turn(g):
                            if g >= 2:
                                pe.wait_ge(S["tr_sb"], g - 1)
                            for k in range(GB):
                                ins = nc.tensor.transpose(pR[:, g % 2, k * P:(k + 1) * P], hN[:, g * GB + k, :], ident[:, :])
                            ins.then_inc(S["tr"], 1)

                        turn(0)
                        turn(1)
                        pe.wait_ge(S["w_in"], 64)
                        nc.tensor.transpose(pO[:, 0:D], w_ext[:, 0:D], ident[:, :]).then_inc(S["w_tr"], 1)
                        pe.wait_ge(S["w_sb"], 1)
                        nc.tensor.matmul(pO[:, 0:2], wT, a_col[:, :], start=True, stop=True).then_inc(S["wa"], 1)
                        pe.wait_ge(S["wa_sb"], 1)
                        for g in range(NG):
                            pe.wait_ge(S["tr_sb"], g + 1)
                            if g >= 2:
                                pe.wait_ge(S["lin_sb"], g - 1)
                            for k in range(GB):
                                bank, o = result(g, k)
                                ins = nc.tensor.matmul(bank[:, o:o + wide], hT[:, g % 2, k * P:(k + 1) * P], w_ext[:, :], start=True, stop=True)
                            ins.then_inc(S["lin"], 1)
                            if g + 2 < NG:
                                turn(g + 2)
                        pe.wait_ge(S["const"], 3)
                        logit_range_pe(pe, rng, ones, S, pR[:, 0, :])
                end_stage()

                destination_maxima(tag, acc, ap, al, amax, rng, pR, flag)

                end_stage()

                S = {n: sem(f"{tag}m_{n}") for n in ("diag", "r_ready", "e_ready", "m_done", "p_ready", "p_used", "o_free", "z_own", "relu")}
                step = Chain(f"{tag}m_dve", nc.vector)

                with nc.Block() as block:
                    @block.scalar
                    def _(act):
                        def exponentials(c, par):
                            for b in range(NB):
                                if b == 0:
                                    act.wait_ge(S["r_ready"], c + 1)
                                last = b - SLOTS + NB if b >= SLOTS else max(x for x in range(NB) if x % SLOTS == b % SLOTS)
                                act.wait_ge(S["p_used"], c * NB + last + 1)
                                nc.scalar.activation(e1[:, b % SLOTS, :], pR[:, par, 0:CHUNK], ACT.Exp, bias=al[:, 0, b:b + 1])
                                act.wait_ge(S["m_done"], c * NB + (b + 1 if b >= 2 else 2 - b))
                                nc.scalar.activation(e2[:, b % 2, :], pR[:, par, CHUNK:2 * CHUNK], ACT.Exp, bias=al2[:, b:b + 1]).then_inc(S["e_ready"], 1)

                        exponentials(0, 0)
                        with act.Fori(0, NG // 2) as i:
                            exponentials(i * 2 + 1, 1)
                            exponentials(i * 2 + 2, 0)

                    @block.vector
                    def _(dve):
                        step(nc.vector.tensor_tensor(amax[:, :], amax[:, :], al[:, 1, :], ALU.add))
                        step(nc.vector.scalar_tensor_tensor(m[:, :], amax[:, :], SLOPE, amax[:, :], ALU.mult, ALU.max))
                        step(nc.vector.tensor_tensor(R[:, 0, 0:NB], al[:, 1, :], m[:, :], ALU.subtract))
                        step(nc.vector.scalar_tensor_tensor(R[:, 1, 0:NB], al[:, 1, :], SLOPE, m[:, :], ALU.mult, ALU.subtract))
                        dve.sem_inc(S["m_done"], 2)

                        def make_diag(c):
                            for t in range(2):
                                ins = nc.vector.tensor_tensor(diag[:, t, :, :], ident[:, :].unsqueeze(1).broadcast_to([P, GB, P]),
                                                              R[:, t, bass.ds(c * GB, GB)].unsqueeze(2).broadcast_to([P, GB, P]), ALU.mult)
                            ins.then_inc(S["diag"], 1)

                        def weights(c, b):
                            dve.wait_ge(S["e_ready"], c * NB + b + 1)
                            v = e1[:, b % SLOTS, :]
                            nc.vector.tensor_tensor(v, v, e2[:, b % 2, :], ALU.max).then_inc(S["m_done"], 1)
                            dve.wait_ge(S["m_done"], c * NB + b + 3)
                            nc.vector.scalar_tensor_tensor(v, v, CLAMP, counts[:, b, bass.ds(c * CHUNK, CHUNK)], ALU.min, ALU.mult).then_inc(S["p_ready"], 1)

                        def normalise(c):
                            dve.wait_ge(S["p_used"], c * NB + NB)
                            for k0, k1 in ((0, 3), (3, GB)):
                                o = pO[:, bank_of(k0, D + 1):bank_of(k0, D + 1) + (k1 - k0) * (D + 1)].rearrange("p (b w) -> p b w", w=D + 1)
                                ins = nc.vector.tensor_scalar(z[:, k0:k1].unsqueeze(2), o[:, :, D:D + 1], TINY, None, ALU.max)
                            ins.then_inc(S["z_own"], 1)
                            dve.wait_ge(S["z_own"], c * 2 - 1)
                            nc.vector.reciprocal(rz[:, :], z[:, :]).then_inc(S["z_own"], 1)
                            dve.wait_ge(S["z_own"], c * 2)
                            for k in range(GB):
                                o = pO[:, bank_of(k, D + 1):bank_of(k, D + 1) + D]
                                ins = nc.vector.scalar_tensor_tensor(hN[:, bass.ds((c - 1) * GB + k, 1), :].squeeze(1), o, rz[:, k:k + 1], b_row[:, :],
                                                                     ALU.mult, ALU.add)
                            ins.then_inc(S["o_free"], 1)

                        def relu(c):
                            v = hN[:, bass.ds((c - 1) * GB, GB), :]
                            nc.vector.tensor_scalar(v, v, 0.0, None, ALU.max).then_inc(S["relu"], 1)

                        make_diag(0)
                        for b in range(NB):
                            weights(0, b)
                            if b == 12:
                                make_diag(1)
                        with dve.Fori(1, NG) as c:
                            for b in range(NB):
                                weights(c, b)
                                if b == 1:
                                    normalise(c)
                                if b == 3:
                                    dve.wait_ge(S["o_free"], c)
                                    relu(c)
                                if b == 12:
                                    dve.wait_ge(S["r_ready"], c + 1)
                                    make_diag(c + 1)
                        normalise(NG)
                        dve.wait_ge(S["o_free"], NG)
                        relu(NG)

                    @block.tensor
                    def _(pe):
                        def spread(c, par):
                            pe.wait_ge(S["diag"], c + 1)
                            bank = pR[:, par, :]
                            d = diag[:, :, :, :].rearrange("p t b m -> p (t b m)")
                            for a, z0 in ((0, 512), (512, 1024), (1024, 2 * CHUNK)):
                                ins = nc.tensor.matmul(bank[:, a:z0], ones[:, :], d[:, a:z0], start=True, stop=True)
                            ins.then_inc(S["r_ready"], 1)

                        def products(c, b):
                            pe.wait_ge(S["p_ready"], c * NB + b + 1)
                            for k in range(GB):
                                ins = nc.tensor.matmul(pO[:, bank_of(k, D + 1):bank_of(k, D + 1) + D + 1], e1[:, b % SLOTS, k * P:(k + 1) * P],
                                                       val[:, b, :], start=(b == 0 and k in (0, 3)), stop=(b == NB - 1), skip_group_check=True)
                            ins.then_inc(S["p_used"], 1)

                        pe.sem_inc(S["p_used"], NB)
                        spread(0, 0)
                        for b in range(NB):
                            products(0, b)
                            if b == 14:
                                spread(1, 1)
                        with pe.Fori(0, NG // 2) as i:
                            for c, par in ((i * 2 + 1, 0), (i * 2 + 2, 1)):
                                pe.wait_ge(S["o_free"], c)
                                for b in range(NB):
                                    products(c, b)
                                    if b == 14:
                                        spread(c + 1, par)

        def destination_maxima(tag, acc, ap, al, amax, rng, pR, flag):
            S = {n: sem(f"{tag}x_{n}") for n in ("own", "ready", "turned", "reduced")}
            step = Chain(f"{tag}x_dve", nc.vector)
            with nc.Block() as block:
                @block.vector
                def _(dve):
                    with dve.If(dve.value_load(flag[0:1, 0:1], min_val=0, max_val=1) > 0):
                        step(nc.vector.tensor_scalar(ap[:, :], al[:, 0, :], rng[:, 5:6], rng[:, 7:8], ALU.add, ALU.mult))
                        step(nc.vector.tensor_scalar(ap[:, :], ap[:, :], 0.5, None, ALU.add))
                        nc.vector.memset(acc[:, :], 0.0).then_inc(S["own"], 1)
                        with dve.Fori(0, NB) as b:
                            dve.wait_ge(S["own"], b + 1)
                            nc.vector.scalar_tensor_tensor(acc[:, :], counts[:, bass.ds(b, 1), :].squeeze(1), ap[:, bass.ds(b, 1)],
                                                           acc[:, :], ALU.min, ALU.max).then_inc(S["own"], 1)
                        for g in range(NG):
                            dve.wait_ge(S["turned"], g + 1)
                            nc.vector.tensor_reduce(amax[:, g * GB:(g + 1) * GB], pR[:, 0, 0:CHUNK].rearrange("p (b n) -> p b n", b=GB), AX.X,
                                                    ALU.max).then_inc(S["reduced"], 1)
                        dve.wait_ge(S["reduced"], NG)
                        step(nc.vector.tensor_scalar(amax[:, :], amax[:, :], 0.5, rng[:, 6:7], ALU.subtract, ALU.mult))
                        step(nc.vector.tensor_scalar(amax[:, :], amax[:, :], rng[:, 5:6], None, ALU.subtract))

                @block.tensor
                def _(pe):
                    with pe.If(pe.value_load(flag[0:1, 0:1], min_val=0, max_val=1) > 0):
                        pe.wait_ge(S["own"], NB + 1)
                        for g in range(NG):
                            if g:
                                pe.wait_ge(S["reduced"], g)
                            for k in range(GB):
                                ins = nc.tensor.transpose(pR[:, 0, k * P:(k + 1) * P], acc[:, (g * GB + k) * P:(g * GB + k + 1) * P], ident[:, :])
                            ins.then_inc(S["turned"], 1)

        def local_attention(hN):
            tag = "l2"
            WD = D + 1
            with ExitStack() as s:
                val = sb(s, f"{tag}_val", [P, NB, WD], fp32)
                space = sb(s, f"{tag}_space", [P, (3 * NB * WD + 1) // 2], fp32)
                acc = space[:, 0:NP]
                parts = space[:, :].bitcast(bf16)[:, 0:3 * NB * WD].rearrange("p (b t w) -> p b t w", b=NB, t=3)
                turn = sb(s, f"{tag}_turn", [P, 3, CHUNK], bf16)
                e2 = space[:, NP:NP + CHUNK]
                turn32 = turn[:, :, :].rearrange("p t n -> p (t n)").bitcast(fp32)
                ones = turn32[:, 0:P]
                w_row = turn32[:, P:3 * P].rearrange("p (t d) -> p t d", t=2)
                al = sb(s, f"{tag}_al", [P, NB], fp32)
                A = sb(s, f"{tag}_A", [P, NB], fp32)
                ap = sb(s, f"{tag}_ap", [P, NB], fp32)
                amax = sb(s, f"{tag}_amax", [P, NB], fp32)
                rng = sb(s, f"{tag}_rng", [P, 8], fp32)
                flag = sb(s, f"{tag}_flag", [P, 1], i32)
                fin = scores[:, 0:2 * (WD + 2)].rearrange("p (t w) -> p t w", t=2)
                pA = pb(s, f"{tag}_pA", [P, 1024])
                pB = pb(s, f"{tag}_pB", [P, 1024])
                pC = pb(s, f"{tag}_pC", [P, 1024])
                pO = pb(s, f"{tag}_pO", [P, 1024])
                S = {n: sem(f"{tag}_{n}") for n in ("w_in", "const", "tanh", "rng_r", "rng_t", "rng_s", "rng_b")}
                step = Chain(f"{tag}_dve", nc.vector)
                a3 = space[:, 0:NP].rearrange("p (b d) -> p b d", b=NB)
                with nc.Block() as block:
                    @block.sync
                    def _(sp):
                        sp.dma_start(w_row[:, 0, :], T["L2_gnn_high_atts"].broadcast_to([P, D])).then_inc(S["w_in"], 16)
                        sp.dma_start(w_row[:, 1, :], T["L2_gnn_diff_atts"].broadcast_to([P, D])).then_inc(S["w_in"], 16)

                    @block.gpsimd
                    def _(pool):
                        nc.gpsimd.memset(ones[:, :], 1.0).then_inc(S["const"], 1)
                        nc.gpsimd.memset(val[:, :, D:WD], 1.0)

                    @block.scalar
                    def _(act):
                        nc.scalar.activation(val[:, :, 0:D], hN[:, :, :], ACT.Tanh).then_inc(S["tanh"], 1)

                    @block.vector
                    def _(dve):
                        dve.wait_ge(S["w_in"], 32)
                        step(nc.vector.scalar_tensor_tensor(w_row[:, 0, :], w_row[:, 1, :], -0.5, w_row[:, 0, :], ALU.mult, ALU.add))
                        dve.wait_ge(S["tanh"], 1)
                        step(nc.vector.tensor_tensor(a3, val[:, :, 0:D], w_row[:, 0, :].unsqueeze(1).broadcast_to([P, NB, D]), ALU.mult))
                        step(nc.vector.tensor_reduce(al[:, :], a3, AX.X, ALU.add))
                        logit_range(step, dve, al[:, :], rng, ap[:, :], S, pC[:, :], flag)

                    @block.tensor
                    def _(pe):
                        pe.wait_ge(S["const"], 1)
                        logit_range_pe(pe, rng, ones, S, pC[:, :])
                end_stage()
                one_shift(hN, tag, val, parts, turn, fin, al, A, rng, flag, (pA, pB, pC), pO)
                end_stage()
                own_shifts(hN, tag, val, acc, e2, ones, al, ap, amax, rng, flag, pA, pB, pC, pO)

        def one_shift(hN, tag, val, parts, turn, fin, al, A, rng, flag, pTurn, pO):
            WD = D + 1
            U = NG
            S = {n: sem(f"{tag}f_{n}") for n in ("A", "w", "turned", "copied", "used", "read", "own", "done")}
            step = Chain(f"{tag}f_dve", nc.vector)
            with nc.Block() as block:
                @block.scalar
                def _(act):
                    with act.If(act.value_load(flag[0:1, 0:1], min_val=0, max_val=1) < 1):
                        act.wait_ge(S["A"], 1)
                        nc.scalar.activation(A[:, :], al[:, :], ACT.Exp).then_inc(S["A"], 1)
                        act.sem_inc(S["copied"], 2)

                        def copies(b):
                            for g in range(U):
                                act.wait_ge(S["turned"], b * U + g + 1)
                                act.wait_ge(S["used"], b * U + g + 1)
                                nc.scalar.activation(turn[:, g % 3, :], pTurn[g % 3][:, 0:CHUNK], ACT.Copy).then_inc(S["copied"], 1)

                        with act.Fori(0, NB) as b:
                            copies(b)
                        for g in range(NG):
                            act.wait_ge(S["done"], (g + 1) * GB)
                            v = hN[:, g * GB:(g + 1) * GB, :]
                            nc.scalar.activation(v, v, ACT.Tanh)

                @block.vector
                def _(dve):
                    with dve.If(dve.value_load(flag[0:1, 0:1], min_val=0, max_val=1) < 1):
                        nc.vector.tensor_scalar(al[:, :], al[:, :], rng[:, 4:5], None, ALU.subtract).then_inc(S["A"], 1)
                        dve.sem_inc(S["read"], 2)
                        dve.wait_ge(S["A"], 2)
                        for g in range(NG):
                            v = val[:, g * GB:(g + 1) * GB, :]
                            step(nc.vector.tensor_tensor(v, v, A[:, g * GB:(g + 1) * GB].unsqueeze(2).broadcast_to([P, GB, WD]), ALU.mult))
                            for t in range(3):
                                o = parts[:, g * GB:(g + 1) * GB, t, :]
                                ins = nc.vector.tensor_copy(o, v)
                                if t < 2:
                                    step(ins)
                                    step(nc.vector.tensor_tensor(v, v, o, ALU.subtract))
                            ins.then_inc(S["w"], 1)

                        def finish(b, par):
                            def own(n, ins):
                                ins.then_inc(S["own"], 1)
                                dve.wait_ge(S["own"], b * 4 + n)

                            dve.wait_ge(S["used"], b * U + U + 2)
                            o = pO[:, par * 512:par * 512 + 3 * WD].rearrange("p (t w) -> p t w", t=3)
                            t = fin[:, par, :]
                            own(1, nc.vector.tensor_reduce(t[:, 0:WD], o.rearrange("p t w -> p w t"), AX.X, ALU.add))
                            own(2, nc.vector.tensor_scalar(t[:, WD:WD + 1], t[:, D:WD], TINY, None, ALU.max))
                            own(3, nc.vector.reciprocal(t[:, WD + 1:WD + 2], t[:, WD:WD + 1]))
                            dve.sem_inc(S["read"], 1)
                            own(4, nc.vector.tensor_scalar(hN[:, bass.ds(b, 1), :].squeeze(1), t[:, 0:D], t[:, WD + 1:WD + 2], None, ALU.mult))
                            dve.sem_inc(S["done"], 1)

                        with dve.Fori(0, NB // 2) as i:
                            finish(i * 2, 0)
                            finish(i * 2 + 1, 1)
                        finish(NB - 1, 0)

                @block.tensor
                def _(pe):
                    with pe.If(pe.value_load(flag[0:1, 0:1], min_val=0, max_val=1) < 1):
                        pe.sem_inc(S["used"], 2)

                        def turned(b, g):
                            pe.wait_ge(S["copied"], b * U + g + 1)
                            for k in range(GB):
                                c = g * GB + k
                                src = counts[:, b, c * P:(c + 1) * P] if isinstance(b, int) else counts[:, bass.ds(b, 1), c * P:(c + 1) * P].squeeze(1)
                                ins = nc.tensor.matmul(pTurn[g % 3][:, k * P:(k + 1) * P], src, identb[:, :], start=True, stop=True)
                            ins.then_inc(S["turned"], 1)

                        def sources(b, par, last=False):
                            for g in range(U):
                                if g + 1 < U:
                                    turned(b, g + 1)
                                elif not last:
                                    turned(b + 1, 0)
                                if g == 0:
                                    pe.wait_ge(S["read"], b + 1)
                                pe.wait_ge(S["w"], g + 1)
                                pe.wait_ge(S["copied"], b * U + g + 3)
                                for k in range(GB):
                                    ins = nc.tensor.matmul(pO[:, par * 512:par * 512 + 3 * WD], turn[:, g % 3, k * P:(k + 1) * P],
                                                           parts[:, g * GB + k, :, :].rearrange("p t w -> p (t w)"), start=(g == 0 and k == 0),
                                                           stop=(g == U - 1 and k == GB - 1), skip_group_check=True)
                                ins.then_inc(S["used"], 1)

                        turned(0, 0)
                        with pe.Fori(0, NB // 2) as i:
                            sources(i * 2, 0)
                            sources(i * 2 + 1, 1)
                        sources(NB - 1, 0, last=True)

        def own_shifts(hN, tag, val, acc, e2, ones, al, ap, amax, rng, flag, pA, pB, pC, pO):
            e1 = acc[:, 2 * CHUNK:(2 + SLOTS) * CHUNK].rearrange("p (t n) -> p t n", t=SLOTS)
            diag = acc[:, 0:CHUNK].rearrange("p (b m) -> p b m", b=GB)
            z, rz = ap[:, 0:GB], ap[:, GB:2 * GB]
            S = {n: sem(f"{tag}o_{n}") for n in ("acc_ready", "acc_t", "acc_m", "diag_ready", "r_ready", "e_ready", "p_ready", "p_used",
                                                  "o_free", "c_ready", "c_used", "tanh")}
            step = Chain(f"{tag}o_dve", nc.vector)
            with nc.Block() as block:
                @block.scalar
                def _(act):
                    with act.If(act.value_load(flag[0:1, 0:1], min_val=0, max_val=1) > 0):
                        act.sem_inc(S["e_ready"], 1)
                        act.sem_inc(S["tanh"], 1)
                        with act.Fori(0, NG) as c:
                            for b in range(NB):
                                if b == 0:
                                    act.wait_ge(S["r_ready"], c + 1)
                                last = b - SLOTS + NB if b >= SLOTS else max(x for x in range(NB) if x % SLOTS == b % SLOTS)
                                act.wait_ge(S["p_used"], c * NB + last + 1)
                                nc.scalar.activation(e1[:, b % SLOTS, :], pA[:, 0:CHUNK], ACT.Exp, bias=al[:, b:b + 1]).then_inc(S["e_ready"], 1)
                            act.wait_ge(S["o_free"], c + 2)
                            nc.scalar.activation(hN[:, bass.ds(c * GB, GB), :], e2[:, :].rearrange("p (b d) -> p b d", b=GB), ACT.Tanh).then_inc(S["tanh"], 1)

                @block.vector
                def _(dve):
                    with dve.If(dve.value_load(flag[0:1, 0:1], min_val=0, max_val=1) > 0):
                        step(nc.vector.tensor_scalar(ap[:, :], al[:, :], rng[:, 5:6], rng[:, 7:8], ALU.add, ALU.mult))
                        step(nc.vector.tensor_scalar(ap[:, :], ap[:, :], 0.5, None, ALU.add))
                        step(nc.vector.memset(acc, 0.0))
                        dve.sem_inc(S["c_used"], 1)
                        with dve.Fori(0, NB) as b:
                            for c in range(NG):
                                dve.wait_ge(S["c_ready"], b * NG + c + 1)
                                dve.wait_ge(S["c_used"], b * NG + c + 1)
                                v = acc[:, c * CHUNK:(c + 1) * CHUNK]
                                nc.vector.scalar_tensor_tensor(v, (pO if c % 2 else pC)[:, 0:CHUNK], ap[:, bass.ds(b, 1)], v,
                                                               ALU.min, ALU.max).then_inc(S["c_used"], 1)
                        dve.wait_ge(S["c_used"], NB * NG + 1)
                        dve.sem_inc(S["acc_ready"], 1)
                        for g in range(NG):
                            dve.wait_ge(S["acc_t"], g + 1)
                            nc.vector.tensor_reduce(amax[:, g * GB:(g + 1) * GB], pA[:, 0:CHUNK].rearrange("p (b n) -> p b n", b=GB), AX.X,
                                                    ALU.max).then_inc(S["acc_m"], 1)
                        dve.wait_ge(S["acc_m"], NG)
                        step(nc.vector.tensor_scalar(amax[:, :], amax[:, :], 0.5, rng[:, 6:7], ALU.subtract, ALU.mult))
                        step(nc.vector.tensor_scalar(amax[:, :], amax[:, :], rng[:, 5:6], -1.0, ALU.subtract, ALU.mult))
                        dve.sem_inc(S["o_free"], 1)
                        with dve.Fori(0, NG) as c:
                            nc.vector.tensor_tensor(diag, ident[:, :].unsqueeze(1).broadcast_to([P, GB, P]),
                                                    amax[:, bass.ds(c * GB, GB)].unsqueeze(2).broadcast_to([P, GB, P]), ALU.mult).then_inc(S["diag_ready"], 1)
                            for b in range(NB):
                                dve.wait_ge(S["e_ready"], c * NB + b + 2)
                                v = e1[:, b % SLOTS, :]
                                dve.wait_ge(S["c_ready"], c * NB + (NB * NG + b + 1))
                                nc.vector.scalar_tensor_tensor(v, v, CLAMP, (pB if b % 2 else pC)[:, 0:CHUNK], ALU.min, ALU.mult).then_inc(S["p_ready"], 1)
                            dve.wait_ge(S["p_used"], c * NB + 2 * NB)
                            dve.wait_ge(S["tanh"], c + 1)
                            for k0, k1 in ((0, 3), (3, GB)):
                                o = pO[:, bank_of(k0, D + 1):bank_of(k0, D + 1) + (k1 - k0) * (D + 1)].rearrange("p (b w) -> p b w", w=D + 1)
                                nc.vector.tensor_scalar(z[:, k0:k1].unsqueeze(2), o[:, :, D:D + 1], TINY, None, ALU.max).then_inc(S["acc_m"], 1)
                            dve.wait_ge(S["acc_m"], c * 3 + NG + 2)
                            nc.vector.reciprocal(rz, z).then_inc(S["acc_m"], 1)
                            dve.wait_ge(S["acc_m"], c * 3 + NG + 3)
                            for k in range(GB):
                                o = pO[:, bank_of(k, D + 1):bank_of(k, D + 1) + D]
                                ins = nc.vector.tensor_scalar(e2[:, k * D:(k + 1) * D], o, rz[:, k:k + 1], None, ALU.mult)
                            ins.then_inc(S["o_free"], 1)

                @block.tensor
                def _(pe):
                    with pe.If(pe.value_load(flag[0:1, 0:1], min_val=0, max_val=1) > 0):
                        def turned(b, c, bank):
                            for k in range(GB):
                                src = (counts[:, c * GB + k, bass.ds(b * P, P)] if isinstance(c, int) else
                                       counts[:, bass.ds(c * GB + k, 1), b * P:(b + 1) * P].squeeze(1))
                                ins = nc.tensor.matmul(bank[:, k * P:(k + 1) * P], src, identb[:, :], start=True, stop=True)
                            ins.then_inc(S["c_ready"], 1)

                        with pe.Fori(0, NB) as b:
                            for c in range(NG):
                                pe.wait_ge(S["c_used"], b * NG + (c if c >= 1 else 1))
                                turned(b, c, pO if c % 2 else pC)
                        pe.wait_ge(S["acc_ready"], 1)
                        for g in range(NG):
                            if g:
                                pe.wait_ge(S["acc_m"], g)
                            for k in range(GB):
                                ins = nc.tensor.transpose(pA[:, k * P:(k + 1) * P], acc[:, (g * GB + k) * P:(g * GB + k + 1) * P], ident[:, :])
                            ins.then_inc(S["acc_t"], 1)
                        pe.sem_inc(S["p_used"], NB)
                        with pe.Fori(0, NG) as c:
                            pe.wait_ge(S["diag_ready"], c + 1)
                            pe.wait_ge(S["e_ready"], c * NB + 1)
                            nc.tensor.matmul(pA[:, 0:512], ones[:, :], diag[:, 0:4, :].rearrange("p b m -> p (b m)"), start=True, stop=True)
                            nc.tensor.matmul(pA[:, 512:CHUNK], ones[:, :], diag[:, 4, :], start=True, stop=True).then_inc(S["r_ready"], 1)
                            pe.wait_ge(S["o_free"], c + 1)
                            for b in range(NB):
                                if b == 0:
                                    turned(0, c, pC)
                                else:
                                    pe.wait_ge(S["p_ready"], c * NB + b)
                                if b + 1 < NB:
                                    turned(b + 1, c, pC if b % 2 else pB)
                                pe.wait_ge(S["p_ready"], c * NB + b + 1)
                                for k in range(GB):
                                    ins = nc.tensor.matmul(pO[:, bank_of(k, D + 1):bank_of(k, D + 1) + D + 1], e1[:, b % SLOTS, k * P:(k + 1) * P],
                                                           val[:, b, :], start=(b == 0 and k in (0, 3)), stop=(b == NB - 1), skip_group_check=True)
                                ins.then_inc(S["p_used"], 1)

        def gin(hN):
            L = 3
            W = 400
            names_ = ("b1", "bn_mean", "bn_var", "gamma", "beta", "b2")
            B1, MEAN, VAR, GAMMA, BETA, B2 = (slice(L * k, L * k + L) for k in range(6))
            with ExitStack() as s:
                hT = sb(s, "i_hT", [P, NP], fp32)
                parts = sb(s, "i_parts", [P, NB, 3, D], bf16)
                w = sb(s, "i_w", [P, L, 2, D], fp32)
                rows = hT[0:6 * L, 0:D]
                cols = sb(s, "i_cols", [P, 6 * L], fp32)
                t1 = sb(s, "i_t1", [P, W], fp32)
                pZ = [pb(s, f"i_pZ{k}", [P, 512]) for k in range(2)]
                pM = [pb(s, f"i_pM{k}", [P, 512]) for k in range(2)]
                pT = pb(s, "i_pT", [P, 1024])
                names = ("in", "cols_t", "cols_c", "sd", "sd_d", "tr", "tr_used", "h_split", "agg", "z_ready", "m1", "m1_act", "m2", "h_new", "bn")
                S = {n: sem(f"i_{n}") for n in names}
                step = Chain("i_dve", nc.vector)
                flat = hN[:, :, :].rearrange("p b d -> p (b d)")
                with nc.Block() as block:
                    @block.sync
                    def _(sp):
                        for k, n in enumerate(names_):
                            sp.dma_start(rows[L * k:L * k + L, :], T[f"L3_gnn_{n}"]).then_inc(S["in"], 16)
                        sp.dma_start(w[:, :, 0, :], T["L3_gnn_W1"].rearrange("l i o -> i l o")).then_inc(S["in"], 16)
                        sp.dma_start(w[:, :, 1, :], T["L3_gnn_W2"].rearrange("l i o -> i l o")).then_inc(S["in"], 16)

                    @block.tensor
                    def _(pe):
                        pe.wait_ge(S["in"], 16 * 8)
                        nc.tensor.transpose(pT[:, 0:6 * L], rows, ident[0:6 * L, 0:6 * L]).then_inc(S["cols_t"], 1)
                        pe.wait_ge(S["cols_c"], 1)
                        for g in range(NG):
                            if g:
                                pe.wait_ge(S["tr_used"], g)
                            for k in range(GB):
                                ins = nc.tensor.transpose(pT[:, k * P:(k + 1) * P], hN[:, g * GB + k, :], ident[:, :])
                            ins.then_inc(S["tr"], 1)
                        for l in range(L):
                            def aggregate(c, k, l=l, between={}):
                                for b in range(NB):
                                    for t in range(3):
                                        ins = nc.tensor.matmul(pZ[k][:, 0:W], parts[:, b, t, :], counts[:, b, bass.ds(c * W, W)],
                                                               start=(b == 0 and t == 0), stop=(b == NB - 1 and t == 2), skip_group_check=True)
                                    if b in between:
                                        between[b]()
                                ins.then_inc(S["agg"], 1)

                            def first_product(c, k, n, l=l):
                                pe.wait_ge(S["z_ready"], n)
                                nc.tensor.matmul(pM[0][:, 0:W], w[:, l, 0, :], hT[:, bass.ds(c * W, W)], start=True, stop=True).then_inc(S["m1"], 1)

                            def second_product(n, l=l):
                                pe.wait_ge(S["m1_act"], n)
                                nc.tensor.matmul(pM[1][:, 0:W], w[:, l, 1, :], t1[:, :], start=True, stop=True).then_inc(S["m2"], 1)

                            pe.wait_ge(S["h_split"], l + 1)
                            base = l * (NP // W)
                            with pe.Fori(0, NP // W // 2) as i:
                                aggregate(i * 2, 0)
                                aggregate(i * 2 + 1, 1, between={5: lambda: first_product(i * 2, 0, i * 2 + base + 1),
                                                                 10: lambda: second_product(i * 2 + base + 1)})
                                first_product(i * 2 + 1, 1, i * 2 + base + 2)
                                second_product(i * 2 + base + 2)
                            pe.wait_ge(S["h_new"], base + NP // W)
                            for g in range(NG):
                                pe.wait_ge(S["tr_used"], (l + 1) * NG + g)
                                for k in range(GB):
                                    ins = nc.tensor.transpose(pT[:, k * P:(k + 1) * P], hT[:, (g * GB + k) * P:(g * GB + k + 1) * P], ident[:, :])
                                ins.then_inc(S["tr"], 1)

                    @block.scalar
                    def _(act):
                        act.wait_ge(S["sd"], 1)
                        nc.scalar.activation(cols[:, VAR], cols[:, VAR], ACT.Sqrt).then_inc(S["sd_d"], 1)
                        act.wait_ge(S["bn"], 1)
                        for l in range(L):
                            base = l * (NP // W)
                            with act.Fori(0, NP // W // 2) as i:
                                for k in range(2):
                                    n = i * 2 + (base + k + 1)
                                    act.wait_ge(S["m1"], n)
                                    nc.scalar.activation(t1[:, :], pM[0][:, 0:W], ACT.Relu, bias=cols[:, BETA][:, l:l + 1],
                                                         scale=cols[:, GAMMA][:, l:l + 1]).then_inc(S["m1_act"], 1)
                                    act.wait_ge(S["m2"], n)
                                    nc.scalar.activation(hT[:, bass.ds(i * (2 * W) + k * W, W)], pM[1][:, 0:W], ACT.Relu,
                                                         bias=cols[:, B2][:, l:l + 1]).then_inc(S["h_new"], 1)

                    @block.vector
                    def _(dve):
                        dve.wait_ge(S["cols_t"], 1)
                        nc.vector.tensor_copy(cols[:, :], pT[:, 0:6 * L]).then_inc(S["cols_c"], 1)
                        dve.wait_ge(S["cols_c"], 1)
                        nc.vector.tensor_scalar(cols[:, VAR], cols[:, VAR], EPS, None, ALU.add).then_inc(S["sd"], 1)
                        dve.wait_ge(S["sd_d"], 1)
                        step(nc.vector.reciprocal(cols[:, VAR], cols[:, VAR]))
                        step(nc.vector.tensor_tensor(cols[:, GAMMA], cols[:, GAMMA], cols[:, VAR], ALU.mult))
                        step(nc.vector.tensor_tensor(cols[:, B1], cols[:, B1], cols[:, MEAN], ALU.subtract))
                        step(nc.vector.tensor_tensor(cols[:, B1], cols[:, B1], cols[:, GAMMA], ALU.mult))
                        nc.vector.tensor_tensor(cols[:, BETA], cols[:, BETA], cols[:, B1], ALU.add).then_inc(S["bn"], 1)
                        for g in range(NG):
                            dve.wait_ge(S["tr"], g + 1)
                            nc.vector.tensor_copy(hT[:, g * CHUNK:(g + 1) * CHUNK], pT[:, 0:CHUNK]).then_inc(S["tr_used"], 1)
                        for l in range(L):
                            base = l * (NP // W)
                            for t in range(3):
                                o = parts[:, :, t, :]
                                ins = nc.vector.tensor_copy(o, hN[:, :, :])
                                if t < 2:
                                    step(ins)
                                    step(nc.vector.tensor_tensor(hN[:, :, :], hN[:, :, :], o, ALU.subtract))
                            ins.then_inc(S["h_split"], 1)
                            with dve.Fori(0, NP // W // 2) as i:
                                for k in range(2):
                                    v = hT[:, bass.ds(i * (2 * W) + k * W, W)]
                                    dve.wait_ge(S["agg"], i * 2 + (base + k + 1))
                                    nc.vector.tensor_tensor(v, pZ[k][:, 0:W], v, ALU.add).then_inc(S["z_ready"], 1)
                            for g in range(NG):
                                dve.wait_ge(S["tr"], (l + 1) * NG + g + 1)
                                nc.vector.tensor_copy(flat[:, g * CHUNK:(g + 1) * CHUNK], pT[:, 0:CHUNK]).then_inc(S["tr_used"], 1)
                            dve.wait_ge(S["tr_used"], (l + 2) * NG)


        tables()
        end_stage()
        if stop >= 2:
            edges()
            end_stage()
        alpha_sum = sb(ctx, "alpha_sum", [P, NB], fp32)
        hN = sb(ctx, "hN", [P, NB, D], fp32)
        stages = [lambda: edge_softmax(hN), lambda: residual("r0", hN, first=True, loops=ALU.add),
                  lambda: gat(0, hN), lambda: gat(1, hN), lambda: gat(2, hN),
                  lambda: residual("r1", hN, loops=ALU.subtract), lambda: local_attention(hN), lambda: residual("r2", hN),
                  lambda: gin(hN), lambda: residual("r3", hN, last=True)]
        for stage in stages[0:max(0, stop - 2)]:
            stage()
            end_stage()


_INS = ['x', 'src', 'dst', 'edge_attr_128', 'L0_gnn_Wq_w', 'L0_gnn_Wq_b', 'L0_gnn_Wk_w', 'L0_gnn_Wk_b', 'L0_gnn_Wv_w',
        'L0_gnn_Wv_b', 'L0_gnn_We_w', 'L0_gnn_We_b', 'L0_gnn_a_w', 'L0_gnn_a_b', 'L1_gnn_W', 'L1_gnn_a_src',
        'L1_gnn_a_dst', 'L1_gnn_b', 'L2_gnn_high_atts', 'L2_gnn_diff_atts', 'L3_gnn_W1', 'L3_gnn_b1', 'L3_gnn_gamma',
        'L3_gnn_beta', 'L3_gnn_bn_mean', 'L3_gnn_bn_var', 'L3_gnn_W2', 'L3_gnn_b2']


def kernel(**inputs):
    import concourse.bacc as bacc
    from concourse.bass_utils import run_bass_kernel_spmd

    nc = bacc.Bacc("TRN2", target_bir_lowering=False, num_devices=1)
    arrays, aps = {}, {}
    for name in _INS:
        a = np.ascontiguousarray(inputs[name])
        arrays[f"in_{name}"] = a
        aps[name] = nc.dram_tensor(f"in_{name}", a.shape, mybir.dt.from_np(a.dtype), kind="ExternalInput").ap()
    out = nc.dram_tensor("out_x", (N, D), fp32, kind="ExternalOutput").ap()
    build(nc, aps, out)
    r = run_bass_kernel_spmd(nc, [arrays], core_ids=[0])
    return r.results[0]["out_x"]
```

```python
import numpy as np
import concourse.bass as bass
from concourse import mybir
from contextlib import ExitStack

fp32 = mybir.dt.float32
bf16 = mybir.dt.bfloat16
fp16 = mybir.dt.float16
i32 = mybir.dt.int32
ALU = mybir.AluOpType
ACT = mybir.ActivationFunctionType
AX = mybir.AxisListType

N = 3125
E = 53125
D = 128
P = 128
NB = -(-N // P)
NP = NB * P
FULL = N // P
REST = N - FULL * P
GB = 5
NG = NB // GB
CHUNK = GB * P

EP = 125
ET = E // EP

CT_TILES = 6
SUPER = P * CT_TILES
NSUP = -(-E // SUPER)
TAIL = E - (NSUP - 1) * SUPER
WIN = 56
GWIN = 50
SLOTS = 3

SLOPE = 0.2
EPS = 1e-5
BIG = 1e38
CLAMP = 1e30
TINY = 1e-30
SAFE_RANGE = 60.0


def build(nc, T, out, stop=99):
    ctx = ExitStack()
    with ctx:
        stage_sems = []

        def sem(name):
            stage_sems.append(nc.alloc_semaphore(name=name))
            return stage_sems[-1]

        def end_stage():
            nc.clear_and_free_semaphores(stage_sems)
            nc.all_engine_barrier()
            stage_sems.clear()

        def sb(scope, name, shape, dt):
            return scope.enter_context(nc.sbuf_tensor(name, shape, dt))

        def pb(scope, name, shape, dt=fp32):
            return scope.enter_context(nc.psum_tensor(name, shape, dt))

        q_table = nc.dram_tensor("q_table", (NP, D), fp32, kind="Internal").ap()
        k_table = nc.dram_tensor("k_table", (NP, D), fp32, kind="Internal").ap()
        k_parts = nc.dram_tensor("k_parts", (NP, 3, D), bf16, kind="Internal").ap()
        s_dram = nc.dram_tensor("s_dram", (NSUP * SUPER,), fp32, kind="Internal").ap()
        v_table = nc.dram_tensor("v_table", (NP, D), fp32, kind="Internal").ap()
        x_dram = nc.dram_tensor("x_dram", (NP, D), fp32, kind="Internal").ap()

        counts = sb(ctx, "counts", [P, NB, NP], bf16)
        ident = sb(ctx, "ident", [P, P], fp32)
        identb = sb(ctx, "identb", [P, P], bf16)
        scores = sb(ctx, "scores", [P, ET], fp32)

        class Chain:
            def __init__(self, name, engine):
                self.sem, self.engine, self.n = sem(name), engine, 0

            def __call__(self, ins):
                self.n += 1
                ins.then_inc(self.sem, 1)
                self.engine.wait_ge(self.sem, self.n)
                return ins

        def node_view(table):
            return table.rearrange("(b p) d -> p b d", p=P)

        def load_x(sp, dst, done):
            sp.dma_start(dst[:, 0:FULL, :], T["x"][0:FULL * P, :].rearrange("(b p) d -> p b d", p=P)).then_inc(done, 16)
            sp.dma_start(dst[0:REST, FULL, :], T["x"][FULL * P:N, :]).then_inc(done, 16)

        HALVES = ((0, 13), (13, NB))

        def layernorm_relu(step, dve, x, h, sq, st, done, last):
            step(nc.vector.tensor_reduce(st[:, 0, :], x[:, :, :], AX.X, ALU.add))
            step(nc.vector.tensor_scalar(st[:, 1, :], st[:, 0, :], 1.0 / D, None, ALU.mult))
            for b0, b1 in HALVES:
                nc.vector.tensor_tensor(h[:, b0:b1, :], x[:, b0:b1, :], st[:, 1, b0:b1].unsqueeze(2).broadcast_to([P, b1 - b0, D]),
                                        ALU.subtract).then_inc(done["centred"], 1)
            for n, (b0, b1) in enumerate(HALVES):
                dve.wait_ge(done["squared"], n + 1)
                step(nc.vector.tensor_reduce(st[:, 2, b0:b1], sq[:, b0:b1, :], AX.X, ALU.add))
            nc.vector.tensor_scalar(st[:, 3, :], st[:, 2, :], 1.0 / D, EPS, ALU.mult, ALU.add).then_inc(done["var_ready"], 1)
            dve.wait_ge(done["std_ready"], 1)
            step(nc.vector.reciprocal(st[:, 1, :], st[:, 0, :]))
            dve.wait_ge(done["centred"], 2)
            for b0, b1 in HALVES:
                ins = nc.vector.scalar_tensor_tensor(h[:, b0:b1, :], h[:, b0:b1, :], 0.0, st[:, 1, b0:b1].unsqueeze(2).broadcast_to([P, b1 - b0, D]),
                                                     ALU.max, ALU.mult)
                if last is not None:
                    ins.then_inc(last, 1)

        def square_and_root(act, h, sq, st, done):
            for n, (b0, b1) in enumerate(HALVES):
                act.wait_ge(done["centred"], n + 1)
                nc.scalar.activation(sq[:, b0:b1, :], h[:, b0:b1, :], ACT.Square).then_inc(done["squared"], 1)
            act.wait_ge(done["var_ready"], 1)
            nc.scalar.activation(st[:, 0, :], st[:, 3, :], ACT.Sqrt).then_inc(done["std_ready"], 1)

        def norm_sems(tag):
            return {n: sem(f"{tag}_{n}") for n in ("centred", "squared", "var_ready", "std_ready")}

        def tables(src_i, dst_i, win_i):
            with ExitStack() as s:
                xN = sb(s, "t_x", [P, NB, D], fp32)
                hN = sb(s, "t_h", [P, NB, D], fp32)
                st = sb(s, "t_st", [P, 4, NB], fp32)
                wraw = sb(s, "t_wraw", [P, 3, D], fp32)
                wT = sb(s, "t_wT", [P, 3, D], fp32)
                brow = sb(s, "t_brow", [P, 4, D], fp32)
                hT = sb(s, "t_hT", [P, CHUNK], fp32)
                kp = sb(s, "t_kp", [P, GB, 3, D], bf16)
                rest = xN[:, 3 * GB:4 * GB, :]
                second = sb(s, "t_qkv", [P, 3, GB, D], fp32)
                slots = (xN[:, 0:3 * GB, :].rearrange("p (t b) d -> p t b d", t=3), second[:, :, :, :])
                pT = pb(s, "t_pT", [P, 1024])
                pQ = pb(s, "t_pQ", [P, GB, 512])
                x_in, w_in, made, id_made = sem("t_x_in"), sem("t_w_in"), sem("t_made"), sem("t_id_made")
                pad_zero, h_ready, norm = sem("t_pad"), sem("t_hready"), norm_sems("t")
                edge_pad, idx_in = sem("t_edge_pad"), sem("t_idx_in")
                full = NSUP - 1
                rows = TAIL // CT_TILES
                left = TAIL - rows * CT_TILES
                kp_out, part_sb, rest_sb = sem("t_kp_out"), sem("t_part"), sem("t_rest")
                ZERO_POOL = 17
                w_tr, w_sb, tr, tr_sb, mm, q_sb = (sem(f"t_{n}") for n in ("w_tr", "w_sb", "tr", "tr_sb", "mm", "q_sb"))
                q_out = [sem(f"t_q_out{k}") for k in range(2)]
                step = Chain("t_dve", nc.vector)
                with nc.Block() as block:
                    @block.sync
                    def _(sp):
                        sp.wait_ge(pad_zero, 1)
                        load_x(sp, xN, x_in)
                        for k, w in enumerate(("L0_gnn_Wq_w", "L0_gnn_Wk_w", "L0_gnn_Wv_w")):
                            sp.dma_start(wraw[:, k, :], T[w]).then_inc(w_in, 16)
                        for k, b in enumerate(("L0_gnn_Wq_b", "L0_gnn_Wk_b", "L0_gnn_Wv_b", "L0_gnn_We_b")):
                            sp.dma_start(brow[:, k, :], T[b].unsqueeze(0).broadcast_to([P, D])).then_inc(w_in, 16)
                        sp.wait_ge(edge_pad, 2)
                        for name, to in (("src", src_i), ("dst", dst_i)):
                            v = T[name]
                            m = full * SUPER
                            sp.dma_start(to[:, 0:full, :], v[0:m].rearrange("(s p j) -> p s j", p=P, j=CT_TILES)).then_inc(idx_in, 16)
                            sp.dma_start(to[0:rows, full, :], v[m:m + rows * CT_TILES].rearrange("(p j) -> p j", j=CT_TILES)).then_inc(idx_in, 16)
                            sp.dma_start(to[rows:rows + 1, full, 0:left], v[m + rows * CT_TILES:E].unsqueeze(0)).then_inc(idx_in, 16)
                        sp.dma_start(win_i[:, :], T["dst"][0:full * SUPER + 1:SUPER].unsqueeze(0).broadcast_to([P, NSUP]),
                                     allow_slow_non_contiguous=True).then_inc(idx_in, 16)
                        for g in range(NG):
                            sp.wait_ge(q_sb, g + 1)
                            for k, table in enumerate((q_table, k_table, v_table)):
                                sp.dma_start(node_view(table)[:, g * GB:(g + 1) * GB, :], slots[g % 2][:, k, :, :]).then_inc(q_out[g % 2], 16)
                            sp.wait_ge(part_sb, 3 * g + 3)
                            sp.dma_start(k_parts.rearrange("(b p) t d -> p b t d", p=P)[:, g * GB:(g + 1) * GB, :, :], kp[:, :, :, :]).then_inc(kp_out, 16)
                        sp.wait_ge(kp_out, 16 * NG)
                        sp.wait_ge(idx_in, 16 * 7)
                        for k in range(2):
                            sp.wait_ge(q_out[k], 48 * ((NG + 1 - k) // 2))

                    @block.gpsimd
                    def _(pool):
                        nc.gpsimd.memset(ident[:, :], 0.0).then_inc(made, 1)
                        pool.wait_ge(made, 1)
                        nc.gpsimd.affine_select(out=ident[:, :], in_=ident[:, :], compare_op=ALU.not_equal, fill=1.0,
                                                base=0, pattern=[[-1, P]], channel_multiplier=1).then_inc(id_made, 1)
                        pool.wait_ge(id_made, 1)
                        nc.gpsimd.tensor_copy(identb[:, :], ident[:, :]).then_inc(id_made, 1)
                        nc.gpsimd.memset(counts[:, 0:ZERO_POOL, :], 0.0)

                    @block.scalar
                    def _(act):
                        square_and_root(act, hN, xN, st, norm)
                        act.wait_ge(w_tr, 3)
                        nc.scalar.activation(wT[:, :, :].rearrange("p t d -> p (t d)"), pQ[:, 0, 0:3 * D], ACT.Copy).then_inc(w_sb, 1)

                        def split(g):
                            act.wait_ge(q_sb, g + 1)
                            if g:
                                act.wait_ge(kp_out, 16 * g)
                            for t, source in enumerate((slots[g % 2][:, 1, :, :], rest[:, :, :], rest[:, :, :])):
                                if t:
                                    act.wait_ge(rest_sb, 2 * g + t)
                                nc.scalar.activation(kp[:, :, t, :], source, ACT.Copy).then_inc(part_sb, 1)

                        for g in range(NG):
                            act.wait_ge(tr, GB * (g + 1))
                            if g:
                                act.wait_ge(mm, GB * g)
                            nc.scalar.activation(hT[:, :], pT[:, 0:CHUNK], ACT.Copy).then_inc(tr_sb, 1)
                            if g:
                                split(g - 1)
                        split(NG - 1)

                    @block.vector
                    def _(dve):
                        nc.vector.memset(xN[:, FULL, :], 0.0).then_inc(pad_zero, 1)
                        nc.vector.memset(src_i[:, full, :], 0).then_inc(edge_pad, 1)
                        nc.vector.memset(dst_i[:, full, :], NP - 1).then_inc(edge_pad, 1)
                        clear = np.linspace(ZERO_POOL, NB, NG + 2).astype(int).tolist()
                        nc.vector.memset(counts[:, clear[0]:clear[1], :], 0.0)
                        dve.wait_ge(w_in, 16 * 7)
                        step(nc.vector.tensor_tensor(brow[:, 1, :], brow[:, 1, :], brow[:, 3, :], ALU.add))
                        dve.wait_ge(x_in, 32)
                        layernorm_relu(step, dve, xN, hN, xN, st, norm, h_ready)
                        for g in range(NG):
                            nc.vector.memset(counts[:, clear[g + 1]:clear[g + 2], :], 0.0)
                            dve.wait_ge(mm, GB * (g + 1))
                            if g >= 2:
                                dve.wait_ge(q_out[g % 2], 48 * (g // 2))
                            nc.vector.tensor_tensor(
                                slots[g % 2].rearrange("p t b d -> p b t d"),
                                pQ[:, :, 0:3 * D].rearrange("p b (t d) -> p b t d", t=3),
                                brow[:, 0:3, :].unsqueeze(1).broadcast_to([P, GB, 3, D]), ALU.add).then_inc(q_sb, 1)
                            for t, source in ((0, slots[g % 2][:, 1, :, :]), (1, rest[:, :, :])):
                                dve.wait_ge(part_sb, 3 * g + t + 1)
                                nc.vector.tensor_tensor(rest[:, :, :], source, kp[:, :, t, :], ALU.subtract).then_inc(rest_sb, 1)

                    @block.tensor
                    def _(pe):
                        pe.wait_ge(id_made, 1)
                        pe.wait_ge(w_in, 16 * 7)
                        for k in range(3):
                            nc.tensor.transpose(pQ[:, 0, k * D:(k + 1) * D], wraw[:, k, :], ident[:, :]).then_inc(w_tr, 1)
                        pe.wait_ge(w_sb, 1)
                        pe.wait_ge(h_ready, 2)
                        for g in range(NG):
                            if g:
                                pe.wait_ge(tr_sb, g)
                            for k in range(GB):
                                nc.tensor.transpose(pT[:, k * P:(k + 1) * P], hN[:, g * GB + k, :], ident[:, :]).then_inc(tr, 1)
                            pe.wait_ge(tr_sb, g + 1)
                            if g:
                                pe.wait_ge(q_sb, g)
                            for k in range(GB):
                                nc.tensor.matmul(pQ[:, k, 0:3 * D], hT[:, k * P:(k + 1) * P],
                                                 wT[:, :, :].rearrange("p t d -> p (t d)"), start=True, stop=True).then_inc(mm, 1)

        def edges(src_i, dst_i, win_i):
            HB = [(0, 9), (9, 18), (18, NB)]
            QT = CT_TILES // 2
            QW = QT * P
            NT = NSUP * CT_TILES
            IN_INC = 16 * 4
            with ExitStack() as s:
                iota = sb(s, "e_iota", [P, NB * WIN], fp16)
                key = sb(s, "e_key", [P, NSUP, CT_TILES], fp32)
                lo = sb(s, "e_lo", [P, NSUP, CT_TILES], fp32)
                win_p = sb(s, "e_wp", [P, NSUP], fp32)
                part = sb(s, "e_part", [P, 1], fp32)
                key_oh = sb(s, "e_koh", [P, SLOTS, NB * WIN], bf16)
                lo_oh = sb(s, "e_loh", [P, SLOTS, P], bf16)
                e_in = sb(s, "e_e", [P, 2, CT_TILES, D], fp32)
                eT = sb(s, "e_eT", [P, 2, QW], fp32)
                win_f = eT[:, 1, QW - NSUP:QW]
                z = sb(s, "e_z", [P, 4, QT, D], fp32)
                dst_row = sb(s, "e_drow", [P, 2, SUPER], i32)
                dst_oh = sb(s, "e_doh", [P, 2, SUPER], bf16)
                k_win = sb(s, "e_kwin", [P, 2, 3, D], bf16)
                weT = sb(s, "e_weT", [P, D], fp32)
                a_row = sb(s, "e_a", [P, D], fp32)
                a_bias = sb(s, "e_ab", [P, 1], fp32)
                idx = sb(s, "e_idx", [P, 4, QT], i32)
                idk = sb(s, "e_idk", [P, 4, QT], i32)
                dots = sb(s, "e_dots", [P, CT_TILES], fp32)
                small = sb(s, "e_small", [P, 4], fp32)
                ones_row = sb(s, "e_ones", [1, P], fp32)
                flag = sb(s, "e_flag", [P, 1], i32)
                found = sb(s, "e_found", [P, NB * WIN], bf16)
                dstf = z[:, 0:2, :, :].rearrange("p a t d -> p (a t d)")[:, 0:NT].rearrange("p (s j) -> p s j", s=NSUP)
                tmp = z[:, 2:4, :, :].rearrange("p a t d -> p (a t d)")[:, 0:NT].rearrange("p (s j) -> p s j", s=NSUP)
                pC = pb(s, "e_pC", [P, 1536])
                pT = [pb(s, f"e_pT{q}", [P, 512]) for q in range(2)]
                pZ = [pb(s, f"e_pZ{q}", [P, 512]) for q in range(2)]
                pS = pb(s, "e_pS", [P, 512])
                names = ("w_in", "const", "we_tr", "we_sb", "prep", "fl_t", "fl_r", "fl_b", "gate", "tr_done", "eT_ready",
                         "oh_ready", "oh_used", "doh_ready", "found", "stored", "mm_done", "z_copied", "dot_done", "idx_ready", "own", "score", "out",
                         "back")
                S = {n: sem(f"e_{n}") for n in names}
                in_ready = [sem(f"e_in_ready{p}") for p in range(2)]
                q_ready = [sem(f"e_q_ready{p}") for p in range(4)]
                k_ready = [sem(f"e_k_ready{p}") for p in range(4)]
                step = Chain("e_dve", nc.vector)
                full = NSUP - 1
                rows = TAIL // CT_TILES
                left = TAIL - rows * CT_TILES
                e_rows = T["edge_attr_128"]
                e_view = e_rows[0:full * SUPER, :].rearrange("(s p j) d -> p s j d", p=P, j=CT_TILES)
                s_view = s_dram[0:NSUP * SUPER].rearrange("(s p j) -> p s j", p=P, j=CT_TILES)

                with nc.Block() as block:
                    @block.sync
                    def _(sp):
                        sp.dma_start(weT[:, :], T["L0_gnn_We_w"]).then_inc(S["w_in"], 16)
                        sp.dma_start(a_row[:, :], T["L0_gnn_a_w"].broadcast_to([P, D])).then_inc(S["w_in"], 16)
                        sp.dma_start(a_bias[:, :], T["L0_gnn_a_b"].unsqueeze(0).broadcast_to([P, 1])).then_inc(S["w_in"], 16)

                        def load_window(i, par):
                            at = sp.value_load(win_i[0:1, bass.ds(i, 1)], min_val=0, max_val=NP - WIN)
                            sp.dma_start(k_win[0:WIN, par, :, :], k_parts[bass.ds(at, WIN), :, :]).then_inc(in_ready[par], 16)

                        def load(i, par):
                            sp.wait_ge(S["mm_done"], i * 2 + 2)
                            for p0, p1 in ((0, P // 2), (P // 2, P)):
                                sp.dma_start(e_in[p0:p1, par, :, :], e_view[p0:p1, bass.ds(i, 1), :, :].squeeze(1)).then_inc(in_ready[par], 16)
                            sp.dma_start(dst_row[0:WIN, par, :], T["dst"][bass.ds(i * SUPER, SUPER)].unsqueeze(0).broadcast_to([WIN, SUPER])
                                         ).then_inc(in_ready[par], 16)
                            load_window(i, par)

                        def load_tail(i, par):
                            sp.wait_ge(S["mm_done"], i * 2 + 2)
                            m = i * SUPER
                            sp.dma_start(e_in[0:rows, par, :, :], e_rows[m:m + rows * CT_TILES, :].rearrange("(p j) d -> p j d", j=CT_TILES)
                                         ).then_inc(in_ready[par], 16)
                            sp.dma_start(e_in[rows:rows + 1, par, 0:left, :], e_rows[m + rows * CT_TILES:E, :].unsqueeze(0)).then_inc(in_ready[par], 16)
                            sp.dma_start(dst_row[0:WIN, par, 0:TAIL], T["dst"][m:E].unsqueeze(0).broadcast_to([WIN, TAIL])).then_inc(in_ready[par], 16)
                            load_window(i, par)

                        def store_scores(i):
                            sp.wait_ge(S["score"], i + 2)
                            sp.dma_start(s_view[:, bass.ds(i, 1), :].squeeze(1), scores[:, bass.ds(i * CT_TILES, CT_TILES)]).then_inc(S["out"], 16)

                        sp.wait_ge(S["prep"], 1)
                        for i in range(4):
                            load(i, i % 2)
                        with sp.Fori(2, NSUP // 2 - 1) as h:
                            for par in range(2):
                                load(h * 2 + par, par)
                                store_scores(h * 2 + par - 4)
                        load(NSUP - 2, 0)
                        load_tail(NSUP - 1, 1)
                        for i in range(NSUP - 6, NSUP):
                            store_scores(i)
                        sp.wait_ge(S["out"], 16 * NSUP)
                        sp.dma_start(scores[0:EP, :], s_dram[0:E].rearrange("(p j) -> p j", p=EP)).then_inc(S["back"], 16)

                    @block.gpsimd
                    def _(pool):
                        nc.gpsimd.iota(iota[:, :], pattern=[[1, NB * WIN]], base=0, channel_multiplier=0,
                                       allow_small_or_imprecise_dtypes=True).then_inc(S["const"], 1)
                        nc.gpsimd.iota(part[:, :], pattern=[[1, 1]], base=0, channel_multiplier=1,
                                       allow_small_or_imprecise_dtypes=True).then_inc(S["const"], 1)
                        nc.gpsimd.memset(ones_row[:, :], 1.0).then_inc(S["const"], 1)
                        pool.wait_ge(S["prep"], 2)

                        def gather(h, par, q, general):
                            i, g, slot = h * 2 + par, h * 4 + (par * 2 + q), par * 2 + q
                            pool.wait_ge(S["z_copied"], g + 3)
                            if general:
                                nc.gpsimd.tensor_copy(idk[:, slot, :], dst_i[:, bass.ds(i, 1), q * QT:(q + 1) * QT].squeeze(1))
                            nc.gpsimd.tensor_copy(idx[:, slot, :], src_i[:, bass.ds(i, 1), q * QT:(q + 1) * QT].squeeze(1)).then_inc(S["idx_ready"], 1)
                            pool.wait_ge(S["idx_ready"], g + 1)
                            pool.sem_inc(S["gate"], 1)
                            for k in range(QT):
                                nc.gpsimd.indirect_dma_start(out=z[:, slot, k, :], out_offset=None, in_=q_table,
                                                             in_offset=bass.IndirectOffsetOnAxis(ap=idx[:, slot, k:k + 1], axis=0),
                                                             compute_op=ALU.add).then_inc(q_ready[slot], 16)
                            if general:
                                pool.wait_ge(q_ready[slot], h * (16 * QT) + 16 * QT)
                                pool.sem_inc(S["gate"], 1)
                                for k in range(QT):
                                    nc.gpsimd.indirect_dma_start(out=z[:, slot, k, :], out_offset=None, in_=k_table,
                                                                 in_offset=bass.IndirectOffsetOnAxis(ap=idk[:, slot, k:k + 1], axis=0),
                                                                 compute_op=ALU.add).then_inc(k_ready[slot], 16)

                        def gathers(general):
                            with pool.Fori(0, NSUP // 2) as h:
                                for par in range(2):
                                    for q in range(2):
                                        gather(h, par, q, general)

                        general = pool.value_load(flag[0:1, 0:1], min_val=0, max_val=1)
                        with pool.If(general > 0):
                            gathers(True)
                        with pool.If(general < 1):
                            gathers(False)

                    @block.scalar
                    def _(act):
                        act.wait_ge(S["we_tr"], 1)
                        nc.scalar.activation(weT[:, :], pT[0][:, 0:D], ACT.Copy).then_inc(S["we_sb"], 1)
                        act.sem_inc(S["eT_ready"], 2)
                        act.sem_inc(S["z_copied"], 2)
                        act.sem_inc(S["found"], 1)
                        with act.Fori(0, NSUP // 2) as h:
                            for n in range(4):
                                g, q = h * 4 + n, n % 2
                                act.wait_ge(S["tr_done"], g + 1)
                                act.wait_ge(S["mm_done"], g + 3)
                                nc.scalar.activation(eT[:, q, :], pT[q][:, 0:QW], ACT.Copy).then_inc(S["eT_ready"], 1)
                                if q == 1:
                                    i = h * 2 + n // 2
                                    act.wait_ge(S["oh_used"], i * CT_TILES + CT_TILES + SLOTS)
                                    act.wait_ge(S["stored"], i + 1)
                                    for a, (b0, b1) in enumerate(HB):
                                        ins = nc.scalar.activation(found[:, b0 * WIN:b1 * WIN], pC[:, a * 512:a * 512 + (b1 - b0) * WIN], ACT.Copy)
                                    ins.then_inc(S["found"], 1)
                                act.wait_ge(S["mm_done"], g + 5)
                                act.wait_ge(S["dot_done"], g + 1)
                                nc.scalar.activation(z[:, n, :, :].rearrange("p t d -> p (t d)"), pZ[q][:, 0:QW], ACT.Copy).then_inc(S["z_copied"], 1)

                    @block.vector
                    def _(dve):
                        dve.wait_ge(S["const"], 2)
                        step(nc.vector.tensor_copy(win_f, win_i[:, :]))
                        step(nc.vector.tensor_scalar(win_f, win_f, float(NP - WIN), None, ALU.min))
                        nc.vector.tensor_copy(win_i[:, :], win_f).then_inc(S["prep"], 1)
                        step(nc.vector.tensor_scalar(win_p[:, :], win_f, part[:, 0:1], None, ALU.add))
                        step(nc.vector.tensor_copy(dstf, dst_i[:, :, :]))
                        step(nc.vector.tensor_scalar(tmp.bitcast(i32), src_i[:, :, :], P - 1, None, ALU.bitwise_and))
                        step(nc.vector.tensor_copy(lo[:, :, :], tmp.bitcast(i32)))
                        step(nc.vector.tensor_copy(key[:, :, :], src_i[:, :, :]))
                        step(nc.vector.tensor_tensor(key[:, :, :], key[:, :, :], lo[:, :, :], ALU.subtract))
                        step(nc.vector.tensor_scalar(key[:, :, :], key[:, :, :], WIN / P, 1.0, ALU.mult, ALU.add))
                        step(nc.vector.tensor_tensor(tmp, dstf, win_f.unsqueeze(2).broadcast_to([P, NSUP, CT_TILES]), ALU.subtract))
                        step(nc.vector.tensor_tensor(key[:, :, :], key[:, :, :], tmp, ALU.add))
                        good = eT[:, :, :].rearrange("p a n -> p (a n)")[:, 0:NT].rearrange("p (s j) -> p s j", s=NSUP)
                        step(nc.vector.tensor_scalar(good, tmp, float(WIN), None, ALU.is_lt))
                        step(nc.vector.tensor_scalar(tmp, tmp, 0.0, None, ALU.is_ge))
                        step(nc.vector.tensor_tensor(good, good, tmp, ALU.mult))
                        step(nc.vector.tensor_scalar(dstf, dstf, float(N), None, ALU.is_lt))
                        step(nc.vector.tensor_tensor(good, good, dstf, ALU.mult))
                        step(nc.vector.tensor_tensor(key[:, :, :], key[:, :, :], good, ALU.mult))
                        step(nc.vector.tensor_scalar(key[:, :, :], key[:, :, :], 1.0, None, ALU.subtract))
                        step(nc.vector.tensor_tensor(dstf, dstf, good, ALU.subtract))
                        nc.vector.tensor_reduce(small[:, 0:1], dstf.rearrange("p s j -> p (s j)"), AX.X, ALU.max).then_inc(S["fl_r"], 1)
                        dve.wait_ge(S["fl_t"], 1)
                        nc.vector.tensor_reduce(small[0:1, 1:2], pS[0:1, 0:P], AX.X, ALU.max).then_inc(S["fl_r"], 1)
                        dve.wait_ge(S["fl_b"], 1)
                        step(nc.vector.tensor_copy(flag[:, :], pS[:, P:P + 1]))
                        nc.vector.scalar_tensor_tensor(win_p[:, :], flag[:, 0:1].broadcast_to([P, NSUP]), -2.0 * NP, win_p[:, :],
                                                       ALU.mult, ALU.add).then_inc(S["prep"], 1)
                        dve.wait_ge(S["prep"], 2)
                        dve.sem_inc(S["dot_done"], 4)
                        dve.sem_inc(S["stored"], 1)
                        dve.sem_inc(S["score"], 1)

                        def edge_loop(general):
                            def make_dst_oh(h, par):
                                i = h * 2 + par
                                dve.wait_ge(in_ready[par], h * IN_INC + IN_INC)
                                dve.wait_ge(S["mm_done"], i * 2 + 2)
                                nc.vector.tensor_scalar(dst_oh[0:WIN, par, :], dst_row[0:WIN, par, :], win_p[0:WIN, bass.ds(i, 1)], None,
                                                        ALU.is_equal).then_inc(S["doh_ready"], 1)

                            def make_oh(i, n):
                                dve.wait_ge(S["oh_used"], i * CT_TILES + n + 1)
                                nc.vector.tensor_scalar(lo_oh[:, n % SLOTS, :], iota[:, 0:P], lo[:, bass.ds(i, 1), n:n + 1].squeeze(1), None, ALU.is_equal)
                                nc.vector.tensor_scalar(key_oh[:, n % SLOTS, :], iota[:, :], key[:, bass.ds(i, 1), n:n + 1].squeeze(1), None,
                                                        ALU.is_equal).then_inc(S["oh_ready"], 1)

                            def store(i):
                                at = dve.value_load(win_i[0:1, bass.ds(i, 1)], min_val=0, max_val=NP - WIN)
                                dve.wait_ge(S["found"], i + 2)
                                dve.wait_ge(S["stored"], i + 1)
                                v = counts[:, :, bass.ds(at, WIN)]
                                nc.vector.tensor_tensor(v, v, found[:, :].rearrange("p (b w) -> p b w", w=WIN), ALU.add).then_inc(S["stored"], 1)

                            def dot(h, par, q):
                                i, g, slot = h * 2 + par, h * 4 + (par * 2 + q), par * 2 + q
                                ready = k_ready if general else q_ready
                                dve.wait_ge(ready[slot], h * (16 * QT) + 16 * QT)
                                v = z[:, slot, :, :].rearrange("p t d -> p (t d)")
                                nc.vector.scalar_tensor_tensor(v, v, SLOPE, v, ALU.mult, ALU.max).then_inc(S["own"], 1)
                                dve.wait_ge(S["own"], g + 1)
                                if q == 0:
                                    dve.wait_ge(S["score"], i + 1)
                                for k in range(QT):
                                    n = q * QT + k
                                    ins = nc.vector.tensor_tensor_reduce(out=z[:, slot, k, :], in0=z[:, slot, k, :], in1=a_row[:, :], scale=1.0,
                                                                         scalar=0.0, op0=ALU.mult, op1=ALU.add, accum_out=dots[:, n:n + 1])
                                ins.then_inc(S["dot_done"], 1)

                            def copy_scores(i):
                                dve.wait_ge(S["dot_done"], i * 2 + 6)
                                nc.vector.tensor_copy(scores[:, bass.ds(i * CT_TILES, CT_TILES)], dots[:, :]).then_inc(S["score"], 1)

                            def supertile(h, par, early=False):
                                i = h * 2 + par
                                before = (h, 0) if par else (h - 1, 1)
                                make_dst_oh(h, par)
                                for n in range(CT_TILES):
                                    make_oh(i, n)
                                    if n == 2 and not (early and par == 0):
                                        store(i - 1)
                                    if n == 3 and not early:
                                        dot(h - 1, par, 1)
                                        copy_scores(i - 2)
                                    if n == 5 and not (early and par == 0):
                                        dot(*before, 0)

                            supertile(0, 0, early=True)
                            supertile(0, 1, early=True)
                            with dve.Fori(1, NSUP // 2) as h:
                                supertile(h, 0)
                                supertile(h, 1)
                            store(NSUP - 1)
                            dot(NSUP // 2 - 1, 0, 1)
                            copy_scores(NSUP - 2)
                            dot(NSUP // 2 - 1, 1, 0)
                            dot(NSUP // 2 - 1, 1, 1)
                            copy_scores(NSUP - 1)

                        general = dve.value_load(flag[0:1, 0:1], min_val=0, max_val=1)
                        with dve.If(general > 0):
                            edge_loop(True)
                        with dve.If(general < 1):
                            edge_loop(False)
                        dve.wait_ge(S["back"], 16)
                        nc.vector.tensor_scalar(scores[0:EP, :], scores[0:EP, :], a_bias[0:EP, 0:1], None, ALU.add)

                    @block.tensor
                    def _(pe):
                        pe.sem_inc(S["mm_done"], 4)
                        pe.sem_inc(S["oh_used"], SLOTS)
                        pe.wait_ge(S["w_in"], 48)
                        nc.tensor.transpose(pT[0][:, 0:D], weT[:, :], ident[:, :]).then_inc(S["we_tr"], 1)
                        pe.wait_ge(S["we_sb"], 1)
                        pe.wait_ge(S["const"], 3)
                        pe.wait_ge(S["fl_r"], 1)
                        nc.tensor.transpose(pS[0:1, 0:P], small[:, 0:1], ident[:, :]).then_inc(S["fl_t"], 1)
                        pe.wait_ge(S["fl_r"], 2)
                        nc.tensor.matmul(pS[:, P:P + 1], ones_row[0:1, :], small[0:1, 1:2], start=True, stop=True).then_inc(S["fl_b"], 1)

                        def group(h, par, q):
                            i, g = h * 2 + par, h * 4 + (par * 2 + q)
                            if q == 0:
                                pe.wait_ge(in_ready[par], h * IN_INC + IN_INC)
                            pe.wait_ge(S["eT_ready"], g + 1)
                            for k in range(QT):
                                ins = nc.tensor.transpose(pT[q][:, k * P:(k + 1) * P], e_in[:, par, q * QT + k, :], ident[:, :])
                            ins.then_inc(S["tr_done"], 1)
                            if q == 0:
                                pe.wait_ge(S["found"], i + 1)
                            for n in range(q * QT, (q + 1) * QT):
                                pe.wait_ge(S["oh_ready"], i * CT_TILES + n + 1)
                                for a, (b0, b1) in enumerate(HB):
                                    ins = nc.tensor.matmul(pC[:, a * 512:a * 512 + (b1 - b0) * WIN], lo_oh[:, n % SLOTS, :],
                                                           key_oh[:, n % SLOTS, b0 * WIN:b1 * WIN], start=(n == 0), stop=(n == CT_TILES - 1), skip_group_check=True)
                                ins.then_inc(S["oh_used"], 1)
                            pe.wait_ge(S["eT_ready"], g + 3)
                            pe.wait_ge(S["doh_ready"], i + 1)
                            pe.wait_ge(S["z_copied"], g + 1)
                            for k in range(QT):
                                nc.tensor.matmul(pZ[q][:, k * P:(k + 1) * P], eT[:, q, k * P:(k + 1) * P], weT[:, :], start=(k == 0), stop=False,
                                                 skip_group_check=True)
                            for k in range(QT):
                                n = q * QT + k
                                for t in range(3):
                                    ins = nc.tensor.matmul(pZ[q][:, k * P:(k + 1) * P], dst_oh[0:WIN, par, n:n + (P - 1) * CT_TILES + 1:CT_TILES],
                                                           k_win[0:WIN, par, t, :], start=False, stop=(t == 2), skip_group_check=True)
                            ins.then_inc(S["mm_done"], 1)

                        with pe.Fori(0, NSUP // 2) as h:
                            for par in range(2):
                                for q in range(2):
                                    group(h, par, q)
                end_stage()
                general_counts(flag, iota, key, lo, src_i, dst_i, z, e_in, dst_oh, key_oh, lo_oh, small, pC, HB)

        def general_counts(flag, iota, key, lo, src_i, dst_i, z, e_in, zeros, key_oh, lo_oh, small, pC, HB):
            NT = NSUP * CT_TILES
            hi, dstf = (z[:, k:k + 2, :, :].rearrange("p a t d -> p (a t d)")[:, 0:NT] for k in (0, 2))
            rel, good = (e_in[:, k, :, :].rearrange("p t d -> p (t d)")[:, 0:NT] for k in (0, 1))
            keys, los, srcs, dsts = (t[:, :, :].rearrange("p s j -> p (s j)") for t in (key, lo, src_i, dst_i))
            start = small[:, 2:3]
            zero = zeros[:, 0, :]
            S = {n: sem(f"c_{n}") for n in ("made", "used", "zeroed", "stored", "own")}
            step = Chain("c_dve", nc.vector)
            STEPS = 7
            GROUPS = NT // SLOTS
            with nc.Block() as block:
                @block.vector
                def _(dve):
                    with dve.If(dve.value_load(flag[0:1, 0:1], min_val=0, max_val=1) > 0):
                        nc.vector.memset(zero, 0.0).then_inc(S["zeroed"], 1)
                        nc.vector.memset(start, 0.0)
                        step(nc.vector.tensor_copy(hi, srcs))
                        step(nc.vector.tensor_tensor(hi, hi, los, ALU.subtract))
                        step(nc.vector.tensor_scalar(hi, hi, GWIN / P, 1.0, ALU.mult, ALU.add))
                        step(nc.vector.tensor_copy(dstf, dsts))
                        step(nc.vector.tensor_scalar(rel, dstf, float(N), None, ALU.is_lt))
                        step(nc.vector.scalar_tensor_tensor(dstf, dstf, 1.0, rel, ALU.add, ALU.mult))
                        step(nc.vector.tensor_scalar(dstf, dstf, 1.0, None, ALU.subtract))
                        dve.sem_inc(S["used"], 1)
                        dve.sem_inc(S["own"], 1)
                        with dve.Fori(0, NP // GWIN) as w:
                            def own(n, ins):
                                ins.then_inc(S["own"], 1)
                                dve.wait_ge(S["own"], w * STEPS + n + 1)

                            dve.wait_ge(S["own"], w * STEPS + 1)
                            own(1, nc.vector.tensor_scalar(rel, dstf, start, None, ALU.subtract))
                            own(2, nc.vector.tensor_scalar(good, rel, float(GWIN), None, ALU.is_lt))
                            own(3, nc.vector.scalar_tensor_tensor(keys, rel, 0.0, good, ALU.is_ge, ALU.mult))
                            own(4, nc.vector.tensor_tensor(good, rel, hi, ALU.add))
                            own(5, nc.vector.tensor_tensor(keys, keys, good, ALU.mult))
                            own(6, nc.vector.tensor_scalar(keys, keys, 1.0, None, ALU.subtract))
                            nc.vector.tensor_scalar(start, start, float(GWIN), None, ALU.add).then_inc(S["own"], 1)
                            with dve.Fori(0, GROUPS) as t:
                                dve.wait_ge(S["used"], w * GROUPS + t + 1)
                                for n in range(SLOTS):
                                    nc.vector.tensor_scalar(lo_oh[:, n, :], iota[:, 0:P], los[:, bass.ds(t * SLOTS + n, 1)], None, ALU.is_equal)
                                    ins = nc.vector.tensor_scalar(key_oh[:, n, 0:NB * GWIN], iota[:, 0:NB * GWIN], keys[:, bass.ds(t * SLOTS + n, 1)], None, ALU.is_equal)
                                ins.then_inc(S["made"], 1)
                            dve.wait_ge(S["used"], w * GROUPS + GROUPS + 1)
                            for a, (b0, b1) in enumerate(HB):
                                ins = nc.vector.tensor_copy(counts[:, b0:b1, bass.ds(w * GWIN, GWIN)],
                                                            pC[:, a * 512:a * 512 + (b1 - b0) * GWIN].rearrange("p (b w) -> p b w", w=GWIN))
                            ins.then_inc(S["stored"], 1)

                @block.tensor
                def _(pe):
                    with pe.If(pe.value_load(flag[0:1, 0:1], min_val=0, max_val=1) > 0):
                        pe.wait_ge(S["zeroed"], 1)
                        pe.sem_inc(S["stored"], 1)
                        with pe.Fori(0, NP // GWIN) as w:
                            pe.wait_ge(S["stored"], w + 1)
                            for a, (b0, b1) in enumerate(HB):
                                nc.tensor.matmul(pC[:, a * 512:a * 512 + (b1 - b0) * GWIN], zero[:, 0:P], zero[:, 0:(b1 - b0) * GWIN], start=True, stop=False,
                                                 skip_group_check=True)
                            with pe.Fori(0, GROUPS) as t:
                                pe.wait_ge(S["made"], w * GROUPS + t + 1)
                                for n in range(SLOTS):
                                    for a, (b0, b1) in enumerate(HB):
                                        ins = nc.tensor.matmul(pC[:, a * 512:a * 512 + (b1 - b0) * GWIN], lo_oh[:, n, :],
                                                               key_oh[:, n, b0 * GWIN:b1 * GWIN], start=False, stop=True, skip_group_check=True)
                                ins.then_inc(S["used"], 1)

        def edge_softmax(hN):
            HC = 25
            LS = 5
            with ExitStack() as s:
                dst_i = sb(s, "s_dst_i", [P, ET + 2], i32)
                dstF = sb(s, "s_dstF", [P, ET + 2], fp32)
                link = sb(s, "s_link", [P, ET + 1], fp32)
                pen = sb(s, "s_pen", [P, ET + 1], fp32)
                fwd = sb(s, "s_fwd", [P, ET], fp32)
                bwd = sb(s, "s_bwd", [P, ET], fp32)
                col = sb(s, "s_col", [P, 4], fp32)
                carry = sb(s, "s_carry", [P, 2], fp32)
                row = sb(s, "s_row", [1, 4, P], fp32)
                rowc = sb(s, "s_rowc", [1, 2, P + 1], fp32)
                lo = sb(s, "s_lo", [P, ET], fp32)
                hi = sb(s, "s_hi", [P, ET], fp32)
                iota = sb(s, "s_iota", [P, P], fp16)
                iota25 = sb(s, "s_iota25", [P, NB], fp32)
                alpha = sb(s, "s_alpha", [P, 3, ET], bf16)
                lo_oh = sb(s, "s_lo_oh", [P, 2, LS, P], bf16)
                hi_oh = sb(s, "s_hi_oh", [P, 2, HC, NB], bf16)
                hi_al = sb(s, "s_hi_al", [P, 2, HC, 3, NB], bf16)
                zero = sb(s, "s_zero", [P, P], bf16)
                nodes = sb(s, "s_nodes", [P, 3, NB], fp32)
                parts = sb(s, "s_parts", [3 * NB, P], fp32)
                pR = pb(s, "s_pR", [P, 512])
                pN = pb(s, "s_pN", [P, 512])
                pX = pb(s, "s_pX", [P, 512])
                idx_in, const, row_t, col_t = sem("s_idx_in"), sem("s_const"), sem("s_row_t"), sem("s_col_t")
                row_ready, rc_ready, c_ready = sem("s_row_ready"), sem("s_rc"), sem("s_c")
                hi_ready, lo_ready, hist = sem("s_hi_ready"), sem("s_lo_ready"), sem("s_hist")
                own, pad, zeroed, turned = sem("s_own"), sem("s_pad"), sem("s_zeroed"), sem("s_turned")
                step = Chain("s_dve", nc.vector)
                passes = [(0, "max"), (1, "max"), (0, "sum"), (1, "sum")]

                with nc.Block() as block:
                    @block.sync
                    def _(sp):
                        sp.wait_ge(pad, 1)
                        sp.dma_start(dst_i[0:EP, 1:ET + 1], T["dst"].rearrange("(p j) -> p j", p=EP)).then_inc(idx_in, 16)
                        sp.dma_start(dst_i[1:EP, 0:1], T["dst"][ET - 1:E - ET:ET].unsqueeze(1), allow_slow_non_contiguous=True).then_inc(idx_in, 16)
                        sp.dma_start(dst_i[0:EP - 1, ET + 1:ET + 2], T["dst"][ET:E:ET].unsqueeze(1), allow_slow_non_contiguous=True).then_inc(idx_in, 16)

                    @block.gpsimd
                    def _(pool):
                        nc.gpsimd.iota(iota[:, :], pattern=[[1, P]], base=0, channel_multiplier=0,
                                       allow_small_or_imprecise_dtypes=True).then_inc(const, 1)
                        nc.gpsimd.iota(iota25[:, :], pattern=[[1, NB]], base=0, channel_multiplier=0,
                                       allow_small_or_imprecise_dtypes=True).then_inc(const, 1)

                        def weigh(i, par):
                            v = slice(0, EP)
                            pool.wait_ge(own, i + 1)
                            for k in range(3):
                                ins = nc.gpsimd.tensor_tensor(hi_al[v, par, :, k, :], hi_oh[v, par, :, :],
                                                              alpha[v, k, bass.ds(i * HC, HC)].unsqueeze(2).broadcast_to([EP, HC, NB]), ALU.mult)
                            ins.then_inc(hi_ready, 1)

                        weigh(0, 0)
                        with pool.Fori(0, ET // HC // 2) as i:
                            for par in range(2):
                                pool.wait_ge(hist, i * (2 * HC // LS) + par * (HC // LS) + 2)
                                weigh(i * 2 + par + 1, 1 - par)

                    @block.vector
                    def _(dve):
                        nc.vector.memset(zero[:, :], 0.0).then_inc(zeroed, 1)
                        nc.vector.memset(dst_i[:, :], -1).then_inc(pad, 1)
                        dve.wait_ge(idx_in, 48)
                        v = slice(0, EP)
                        step(nc.vector.tensor_copy(dstF[v, :], dst_i[v, :]))
                        step(nc.vector.tensor_tensor(link[v, :], dstF[v, 0:ET + 1], dstF[v, 1:ET + 2], ALU.is_equal))
                        step(nc.vector.tensor_scalar(pen[v, :], link[v, :], BIG, BIG, ALU.mult, ALU.subtract))
                        step(nc.vector.tensor_reduce(col[v, 1:2], link[v, 0:ET], AX.X, ALU.min))
                        step(nc.vector.tensor_reduce(col[v, 2:3], link[v, 1:ET + 1], AX.X, ALU.min))
                        val = scores
                        for n, (back, kind) in enumerate(passes):
                            o = bwd if back else fwd
                            data = val[v, 0:ET]
                            gate = (pen if kind == "max" else link)[v, 1:ET + 1] if back else (pen if kind == "max" else link)[v, 0:ET]
                            dest = o[v, :]
                            if back:
                                data, gate, dest = data[:, ::-1], gate[:, ::-1], dest[:, ::-1]
                            ops = (ALU.add, ALU.max) if kind == "max" else (ALU.mult, ALU.add)
                            start = -BIG if kind == "max" else 0.0
                            step(nc.vector.tensor_tensor_scan(dest, gate, data, start, *ops))
                            step(nc.vector.tensor_copy(col[v, 0:1], o[v, 0:1] if back else o[v, ET - 1:ET]))
                            step(nc.vector.tensor_copy(col[v, 3:4], col[v, 2:3] if back else col[v, 1:2]))
                            nc.vector.tensor_scalar(col[v, 3:4], col[v, 3:4], BIG if kind == "max" else 1.0,
                                                    BIG if kind == "max" else 0.0, ALU.mult, ALU.subtract).then_inc(row_ready, 1)
                            dve.wait_ge(row_t, 2 * (n + 1))
                            step(nc.vector.tensor_copy(row[0:1, 0, v], pR[0:1, 0:EP]))
                            step(nc.vector.tensor_copy(row[0:1, 1, v], pR[0:1, P:P + EP]))
                            step(nc.vector.memset(rowc[0:1, 0, :], start))
                            rd, rg, ro = row[0:1, 0, v], row[0:1, 1, v], (rowc[0:1, 0, 0:EP] if back else rowc[0:1, 0, 1:EP + 1])
                            if back:
                                rd, rg, ro = rd[:, ::-1], rg[:, ::-1], ro[:, ::-1]
                            step(nc.vector.tensor_tensor_scan(ro, rg, rd, start, *ops))
                            nc.vector.tensor_copy(rowc[0:1, 1, v], rowc[0:1, 0, 1:EP + 1] if back else rowc[0:1, 0, 0:EP]).then_inc(rc_ready, 1)
                            dve.wait_ge(col_t, n + 1)
                            step(nc.vector.tensor_copy(carry[v, 0:1], pR[v, 2 * P:2 * P + 1]))
                            step(nc.vector.tensor_tensor_scan(dest, gate, data, carry[v, 0:1], *ops))
                            if n == 1:
                                step(nc.vector.tensor_tensor(fwd[v, :], fwd[v, :], bwd[v, :], ALU.max))
                                nc.vector.tensor_tensor(scores[v, :], scores[v, :], fwd[v, :], ALU.subtract).then_inc(c_ready, 1)
                                dve.wait_ge(c_ready, 2)
                        step(nc.vector.tensor_tensor(fwd[v, :], fwd[v, :], bwd[v, :], ALU.add))
                        step(nc.vector.tensor_tensor(fwd[v, :], fwd[v, :], scores[v, :], ALU.subtract))
                        step(nc.vector.reciprocal(bwd[v, :], fwd[v, :]))
                        step(nc.vector.tensor_tensor(fwd[v, :], scores[v, :], bwd[v, :], ALU.mult))
                        for k in range(3):
                            step(nc.vector.tensor_copy(alpha[v, k, :], fwd[v, :]))
                            if k < 2:
                                step(nc.vector.tensor_tensor(fwd[v, :], fwd[v, :], alpha[v, k, :], ALU.subtract))
                        step(nc.vector.tensor_scalar(dst_i[v, :], dst_i[v, :], P - 1, None, ALU.bitwise_and))
                        step(nc.vector.tensor_copy(lo[v, :], dst_i[v, 1:ET + 1]))
                        step(nc.vector.tensor_tensor(hi[v, :], dstF[v, 1:ET + 1], lo[v, :], ALU.subtract))
                        step(nc.vector.tensor_scalar(hi[v, :], hi[v, :], 1.0 / P, None, ALU.mult))
                        dve.wait_ge(const, 2)
                        def make_hi(i, par):
                            nc.vector.tensor_tensor(hi_oh[v, par, :, :], hi[v, bass.ds(i * HC, HC)].unsqueeze(2).broadcast_to([EP, HC, NB]),
                                                    iota25[v, :].unsqueeze(1).broadcast_to([EP, HC, NB]), ALU.is_equal).then_inc(own, 1)

                        def make_lo(i, u0):
                            for u in range(HC // LS):
                                dve.wait_ge(hist, i * (HC // LS) + u + 1)
                                for j in range(u * LS, (u + 1) * LS):
                                    ins = nc.vector.tensor_scalar(lo_oh[v, (u0 + u) % 2, j % LS, :], iota[v, :], lo[v, bass.ds(i * HC + j, 1)], None, ALU.is_equal)
                                ins.then_inc(lo_ready, 1)

                        make_hi(0, 0)
                        with dve.Fori(0, ET // HC // 2) as i:
                            for par in range(2):
                                dve.wait_ge(hi_ready, i * 2 + par + 1)
                                make_hi(i * 2 + par + 1, 1 - par)
                                make_lo(i * 2 + par, par * (HC // LS))
                        make_lo(ET // HC - 1, 0)
                        dve.wait_ge(hist, ET // LS + 2)
                        nc.vector.tensor_copy(parts[:, :], pN[0:3 * NB, 0:P]).then_inc(own, 1)
                        dve.wait_ge(turned, 1)
                        step(nc.vector.tensor_copy(nodes[:, :, :], pX[:, 0:3 * NB].rearrange("p (k b) -> p k b", k=3)))
                        step(nc.vector.tensor_tensor(nodes[:, 0, :], nodes[:, 0, :], nodes[:, 1, :], ALU.add))
                        step(nc.vector.tensor_tensor(alpha_sum[:, :], nodes[:, 0, :], nodes[:, 2, :], ALU.add))

                    @block.scalar
                    def _(act):
                        act.wait_ge(c_ready, 1)
                        nc.scalar.activation(scores[0:EP, :], scores[0:EP, :], ACT.Exp).then_inc(c_ready, 1)

                    @block.tensor
                    def _(pe):
                        v = slice(0, EP)
                        for n in range(4):
                            pe.wait_ge(row_ready, n + 1)
                            nc.tensor.transpose(pR[0:1, 0:EP], col[v, 0:1], ident[v, v]).then_inc(row_t, 1)
                            nc.tensor.transpose(pR[0:1, P:P + EP], col[v, 3:4], ident[v, v]).then_inc(row_t, 1)
                            pe.wait_ge(rc_ready, n + 1)
                            nc.tensor.transpose(pR[v, 2 * P:2 * P + 1], rowc[0:1, 1, v], ident[0:1, 0:1]).then_inc(col_t, 1)
                        pe.wait_ge(zeroed, 1)
                        nc.tensor.matmul(pN[0:3 * NB, 0:P], zero[:, 0:3 * NB], zero[:, :], start=True, stop=False, skip_group_check=True).then_inc(hist, 2)

                        def products(i, par):
                            for j in range(HC):
                                if j == 0:
                                    pe.wait_ge(hi_ready, i + 1)
                                if j % LS == 0:
                                    pe.wait_ge(lo_ready, i * (HC // LS) + j // LS + 1)
                                ins = nc.tensor.matmul(pN[0:3 * NB, 0:P], hi_al[v, par, j, :, :].rearrange("p k b -> p (k b)"),
                                                       lo_oh[v, (par * (HC // LS) + j // LS) % 2, j % LS, :], start=False, stop=True, skip_group_check=True)
                                if j % LS == LS - 1:
                                    ins.then_inc(hist, 1)

                        with pe.Fori(0, ET // HC // 2) as i:
                            products(i * 2, 0)
                            products(i * 2 + 1, 1)
                        products(ET // HC - 1, 0)
                        pe.wait_ge(own, ET // HC + 1)
                        nc.tensor.transpose(pX[:, 0:3 * NB], parts[:, :], ident[0:3 * NB, 0:3 * NB]).then_inc(turned, 1)

        def residual(tag, hN, first=False, last=False, loops=None):
            with ExitStack() as s:
                xN = sb(s, f"{tag}_x", [P, NB, D], fp32)
                vN = sb(s, f"{tag}_v", [P, NB, D], fp32)
                st = sb(s, f"{tag}_st", [P, 4, NB], fp32)
                pad, x_in, x_new, x_out = (sem(f"{tag}_{n}") for n in ("pad", "x_in", "x_new", "x_out"))
                norm = norm_sems(tag)
                step = Chain(f"{tag}_dve", nc.vector)
                flat = counts[:, :, :].rearrange("p b n -> p (b n)")
                own_block = NP + P
                with nc.Block() as block:
                    @block.sync
                    def _(sp):
                        if first:
                            sp.wait_ge(pad, 1)
                            load_x(sp, xN, x_in)
                            sp.dma_start(vN[:, :, :], node_view(v_table)).then_inc(x_in, 16)
                        else:
                            sp.dma_start(xN[:, :, :], node_view(x_dram)).then_inc(x_in, 16)
                        sp.wait_ge(x_new, 1)
                        if last:
                            sp.dma_start(out[0:FULL * P, :].rearrange("(b p) d -> p b d", p=P), xN[:, 0:FULL, :]).then_inc(x_out, 16)
                            sp.dma_start(out[FULL * P:N, :], xN[0:REST, FULL, :]).then_inc(x_out, 16)
                            sp.wait_ge(x_out, 32)
                        else:
                            sp.dma_start(node_view(x_dram), xN[:, :, :]).then_inc(x_out, 16)
                            sp.wait_ge(x_out, 16)

                    @block.scalar
                    def _(act):
                        if not last:
                            square_and_root(act, hN, vN, st, norm)

                    @block.vector
                    def _(dve):
                        if loops is not None:
                            v = flat[:, 0:(NB - 1) * own_block].rearrange("p (b n) -> p b n", n=own_block)[:, :, 0:P]
                            nc.vector.tensor_tensor(v, v, identb[:, :].unsqueeze(1).broadcast_to([P, NB - 1, P]), loops)
                            v = flat[:, (NB - 1) * own_block:NB * NP]
                            nc.vector.tensor_tensor(v, v, identb[:, :], loops)
                        if first:
                            nc.vector.memset(xN[:, FULL, :], 0.0).then_inc(pad, 1)
                            dve.wait_ge(x_in, 48)
                            step(nc.vector.tensor_tensor(vN[:, :, :], vN[:, :, :], alpha_sum[:, :].unsqueeze(2).broadcast_to([P, NB, D]), ALU.mult))
                            add = vN
                        else:
                            dve.wait_ge(x_in, 16)
                            add = hN
                        nc.vector.tensor_tensor(xN[:, :, :], xN[:, :, :], add[:, :, :], ALU.add).then_inc(x_new, 1)
                        dve.wait_ge(x_new, 1)
                        if not last:
                            layernorm_relu(step, dve, xN, hN, vN, st, norm, None)

        def bank_of(k, w):
            return k * w if k < 3 else 512 + (k - 3) * w

        def logit_range(step, dve, logit, rng, neg, S, pR, flag):
            step(nc.vector.tensor_reduce(rng[:, 0:1], logit, AX.X, ALU.max))
            step(nc.vector.tensor_scalar(neg, logit, -1.0, None, ALU.mult))
            nc.vector.tensor_reduce(rng[:, 1:2], neg, AX.X, ALU.max).then_inc(S["rng_r"], 1)
            dve.wait_ge(S["rng_t"], 1)
            nc.vector.tensor_reduce(rng[0:1, 2:4], pR[0:1, 0:2 * P].rearrange("p (t n) -> p t n", t=2), AX.X, ALU.max).then_inc(S["rng_s"], 1)
            dve.wait_ge(S["rng_b"], 1)
            step(nc.vector.tensor_copy(rng[:, 4:6], pR[:, 2 * P:2 * P + 2]))
            step(nc.vector.tensor_tensor(rng[:, 6:7], rng[:, 4:5], rng[:, 5:6], ALU.add))
            step(nc.vector.tensor_scalar(flag[:, :], rng[:, 6:7], SAFE_RANGE, None, ALU.is_gt))
            step(nc.vector.tensor_scalar(rng[:, 6:7], rng[:, 6:7], TINY, 2.0, ALU.max, ALU.mult))
            step(nc.vector.reciprocal(rng[:, 7:8], rng[:, 6:7]))

        def logit_range_pe(pe, rng, ones, S, pR):
            pe.wait_ge(S["rng_r"], 1)
            for t in range(2):
                ins = nc.tensor.transpose(pR[0:1, t * P:(t + 1) * P], rng[:, t:t + 1], ident[:, :])
            ins.then_inc(S["rng_t"], 1)
            pe.wait_ge(S["rng_s"], 1)
            nc.tensor.matmul(pR[:, 2 * P:2 * P + 2], ones[0:1, :], rng[0:1, 2:4], start=True, stop=True).then_inc(S["rng_b"], 1)

        def gat(layer, hN):
            tag = f"g{layer}"
            wide = D + 2
            with ExitStack() as s:
                val = sb(s, f"{tag}_val", [P, NB, D + 1], fp32)
                acc = sb(s, f"{tag}_acc", [P, NP], fp32)
                e2 = sb(s, f"{tag}_e2", [P, 2, CHUNK], fp32)
                w_ext = scores[:, 0:wide]
                a_col = sb(s, f"{tag}_a", [P, 2], fp32)
                b_row = scores[:, wide:wide + D]
                ones = scores[:, wide + D:wide + D + P]
                al = sb(s, f"{tag}_al", [P, 2, NB], fp32)
                al2 = sb(s, f"{tag}_al2", [P, NB], fp32)
                ap = sb(s, f"{tag}_ap", [P, NB], fp32)
                amax = sb(s, f"{tag}_amax", [P, NB], fp32)
                m = sb(s, f"{tag}_m", [P, NB], fp32)
                R = sb(s, f"{tag}_R", [P, 2, NB + GB], fp32)
                rng = sb(s, f"{tag}_rng", [P, 8], fp32)
                flag = sb(s, f"{tag}_flag", [P, 1], i32)
                z = sb(s, f"{tag}_z", [P, GB], fp32)
                rz = sb(s, f"{tag}_rz", [P, GB], fp32)
                hT = acc[:, 0:2 * CHUNK].rearrange("p (t n) -> p t n", t=2)
                wT = acc[:, 2 * CHUNK:2 * CHUNK + D]
                diag = acc[:, 0:2 * CHUNK].rearrange("p (t b m) -> p t b m", t=2, b=GB)
                e1 = acc[:, 2 * CHUNK:(2 + SLOTS) * CHUNK].rearrange("p (t n) -> p t n", t=SLOTS)
                e1_slots = [e1[:, k, :] for k in range(SLOTS)] + [sb(s, f"{tag}_e1", [P, CHUNK], fp32)[:, :]]
                r2 = sb(s, f"{tag}_r2", [P, CHUNK], fp32)
                pR = pb(s, f"{tag}_pR", [P, 2, 1536])
                pO = pb(s, f"{tag}_pO", [P, 1024])

                S = {n: sem(f"{tag}_{n}") for n in ("w_in", "const", "w_tr", "w_sb", "wa", "wa_sb", "tr", "tr_sb", "lin", "lin_sb",
                                                     "rng_r", "rng_t", "rng_s", "rng_b")}
                step = Chain(f"{tag}_dve", nc.vector)

                def result(g, k):
                    o = k * wide if k < 3 else (k - 3) * wide
                    bank = (pO[:, 0:512] if k < 3 else pO[:, 512:1024]) if g % 2 == 0 else (pR[:, 0, 1024:1536] if k < 3 else pR[:, 1, 1024:1536])
                    return bank, o

                with nc.Block() as block:
                    @block.sync
                    def _(sp):
                        sp.dma_start(w_ext[:, 0:D], T["L1_gnn_W"][layer, :, :]).then_inc(S["w_in"], 16)
                        sp.dma_start(a_col[:, 0:1], T["L1_gnn_a_src"][layer, :].unsqueeze(1)).then_inc(S["w_in"], 16)
                        sp.dma_start(a_col[:, 1:2], T["L1_gnn_a_dst"][layer, :].unsqueeze(1)).then_inc(S["w_in"], 16)
                        sp.dma_start(b_row[:, :], T["L1_gnn_b"][layer, :].unsqueeze(0).broadcast_to([P, D])).then_inc(S["w_in"], 16)

                    @block.gpsimd
                    def _(pool):
                        nc.gpsimd.memset(ones[:, :], 1.0).then_inc(S["const"], 1)
                        nc.gpsimd.memset(val[:, :, D:D + 1], 1.0).then_inc(S["const"], 1)
                        nc.gpsimd.memset(R[:, :, NB:NB + GB], 0.0).then_inc(S["const"], 1)

                    @block.scalar
                    def _(act):
                        def copy_hT(g):
                            act.wait_ge(S["tr"], g + 1)
                            if g >= 2:
                                act.wait_ge(S["lin"], g - 1)
                            nc.scalar.activation(hT[:, g % 2, :], pR[:, g % 2, 0:CHUNK], ACT.Copy).then_inc(S["tr_sb"], 1)

                        copy_hT(0)
                        copy_hT(1)
                        act.wait_ge(S["w_tr"], 1)
                        nc.scalar.activation(wT, pO[:, 0:D], ACT.Copy).then_inc(S["w_sb"], 1)
                        act.wait_ge(S["wa"], 1)
                        nc.scalar.activation(w_ext[:, D:D + 2], pO[:, 0:2], ACT.Copy).then_inc(S["wa_sb"], 1)
                        for g in range(2, NG):
                            copy_hT(g)

                    @block.vector
                    def _(dve):
                        for g in range(NG):
                            dve.wait_ge(S["lin"], g + 1)
                            for k0, k1 in ((0, 3), (3, GB)):
                                bank, _o = result(g, k0)
                                o = bank[:, 0:(k1 - k0) * wide].rearrange("p (b w) -> p b w", w=wide)
                                nc.vector.tensor_copy(val[:, g * GB + k0:g * GB + k1, 0:D], o[:, :, 0:D])
                                ins = nc.vector.tensor_copy(al[:, :, g * GB + k0:g * GB + k1], o[:, :, D:D + 2].rearrange("p b t -> p t b"))
                            ins.then_inc(S["lin_sb"], 1)
                        dve.wait_ge(S["lin_sb"], NG)
                        step(nc.vector.tensor_scalar(al2[:, :], al[:, 0, :], SLOPE, None, ALU.mult))
                        logit_range(step, dve, al[:, 0, :], rng, ap[:, :], S, pR[:, 0, :], flag)
                        nc.vector.tensor_copy(amax[:, :], rng[:, 4:5].broadcast_to([P, NB]))

                    @block.tensor
                    def _(pe):
                        def turn(g):
                            if g >= 2:
                                pe.wait_ge(S["tr_sb"], g - 1)
                            for k in range(GB):
                                ins = nc.tensor.transpose(pR[:, g % 2, k * P:(k + 1) * P], hN[:, g * GB + k, :], ident[:, :])
                            ins.then_inc(S["tr"], 1)

                        turn(0)
                        turn(1)
                        pe.wait_ge(S["w_in"], 64)
                        nc.tensor.transpose(pO[:, 0:D], w_ext[:, 0:D], ident[:, :]).then_inc(S["w_tr"], 1)
                        pe.wait_ge(S["w_sb"], 1)
                        nc.tensor.matmul(pO[:, 0:2], wT, a_col[:, :], start=True, stop=True).then_inc(S["wa"], 1)
                        pe.wait_ge(S["wa_sb"], 1)
                        for g in range(NG):
                            pe.wait_ge(S["tr_sb"], g + 1)
                            if g >= 2:
                                pe.wait_ge(S["lin_sb"], g - 1)
                            for k in range(GB):
                                bank, o = result(g, k)
                                ins = nc.tensor.matmul(bank[:, o:o + wide], hT[:, g % 2, k * P:(k + 1) * P], w_ext[:, :], start=True, stop=True)
                            ins.then_inc(S["lin"], 1)
                            if g + 2 < NG:
                                turn(g + 2)
                        pe.wait_ge(S["const"], 3)
                        logit_range_pe(pe, rng, ones, S, pR[:, 0, :])
                end_stage()

                destination_maxima(tag, acc, ap, al, amax, rng, pR, flag)

                end_stage()

                own_shift_weights(tag, hN, val, diag, e1, e2, al, al2, amax, m, R, z, rz, b_row, ones, flag, pR, pO)
                end_stage()
                one_shift_weights(tag, hN, val, diag, e1_slots, e2, r2, al, al2, m, R, z, rz, rng, b_row, ones, flag, pR, pO)

        def own_shift_weights(tag, hN, val, diag, e1, e2, al, al2, amax, m, R, z, rz, b_row, ones, flag, pR, pO):
            S = {n: sem(f"{tag}m_{n}") for n in ("diag", "r_ready", "e_ready", "m_done", "p_ready", "p_used", "o_free", "z_own", "relu")}
            step = Chain(f"{tag}m_dve", nc.vector)

            with nc.Block() as block:
                @block.scalar
                def _(act):
                    with act.If(act.value_load(flag[0:1, 0:1], min_val=0, max_val=1) > 0):
                        def exponentials(c, par):
                            for b in range(NB):
                                if b == 0:
                                    act.wait_ge(S["r_ready"], c + 1)
                                last = b - SLOTS + NB if b >= SLOTS else max(x for x in range(NB) if x % SLOTS == b % SLOTS)
                                act.wait_ge(S["p_used"], c * NB + last + 1)
                                nc.scalar.activation(e1[:, b % SLOTS, :], pR[:, par, 0:CHUNK], ACT.Exp, bias=al[:, 0, b:b + 1])
                                act.wait_ge(S["m_done"], c * NB + (b + 1 if b >= 2 else 2 - b))
                                nc.scalar.activation(e2[:, b % 2, :], pR[:, par, CHUNK:2 * CHUNK], ACT.Exp, bias=al2[:, b:b + 1]).then_inc(S["e_ready"], 1)

                        exponentials(0, 0)
                        with act.Fori(0, NG // 2) as i:
                            exponentials(i * 2 + 1, 1)
                            exponentials(i * 2 + 2, 0)

                @block.vector
                def _(dve):
                    with dve.If(dve.value_load(flag[0:1, 0:1], min_val=0, max_val=1) > 0):
                        step(nc.vector.tensor_tensor(amax[:, :], amax[:, :], al[:, 1, :], ALU.add))
                        step(nc.vector.scalar_tensor_tensor(m[:, :], amax[:, :], SLOPE, amax[:, :], ALU.mult, ALU.max))
                        step(nc.vector.tensor_tensor(R[:, 0, 0:NB], al[:, 1, :], m[:, :], ALU.subtract))
                        step(nc.vector.scalar_tensor_tensor(R[:, 1, 0:NB], al[:, 1, :], SLOPE, m[:, :], ALU.mult, ALU.subtract))
                        dve.sem_inc(S["m_done"], 2)

                        def make_diag(c):
                            for t in range(2):
                                ins = nc.vector.tensor_tensor(diag[:, t, :, :], ident[:, :].unsqueeze(1).broadcast_to([P, GB, P]),
                                                              R[:, t, bass.ds(c * GB, GB)].unsqueeze(2).broadcast_to([P, GB, P]), ALU.mult)
                            ins.then_inc(S["diag"], 1)

                        def weights(c, b):
                            dve.wait_ge(S["e_ready"], c * NB + b + 1)
                            v = e1[:, b % SLOTS, :]
                            nc.vector.tensor_tensor(v, v, e2[:, b % 2, :], ALU.max).then_inc(S["m_done"], 1)
                            dve.wait_ge(S["m_done"], c * NB + b + 3)
                            nc.vector.scalar_tensor_tensor(v, v, CLAMP, counts[:, b, bass.ds(c * CHUNK, CHUNK)], ALU.min, ALU.mult).then_inc(S["p_ready"], 1)

                        def normalise(c):
                            dve.wait_ge(S["p_used"], c * NB + NB)
                            for k0, k1 in ((0, 3), (3, GB)):
                                o = pO[:, bank_of(k0, D + 1):bank_of(k0, D + 1) + (k1 - k0) * (D + 1)].rearrange("p (b w) -> p b w", w=D + 1)
                                ins = nc.vector.tensor_scalar(z[:, k0:k1].unsqueeze(2), o[:, :, D:D + 1], TINY, None, ALU.max)
                            ins.then_inc(S["z_own"], 1)
                            dve.wait_ge(S["z_own"], c * 2 - 1)
                            nc.vector.reciprocal(rz[:, :], z[:, :]).then_inc(S["z_own"], 1)
                            dve.wait_ge(S["z_own"], c * 2)
                            for k in range(GB):
                                o = pO[:, bank_of(k, D + 1):bank_of(k, D + 1) + D]
                                ins = nc.vector.scalar_tensor_tensor(hN[:, bass.ds((c - 1) * GB + k, 1), :].squeeze(1), o, rz[:, k:k + 1], b_row[:, :],
                                                                     ALU.mult, ALU.add)
                            ins.then_inc(S["o_free"], 1)

                        def relu(c):
                            v = hN[:, bass.ds((c - 1) * GB, GB), :]
                            nc.vector.tensor_scalar(v, v, 0.0, None, ALU.max).then_inc(S["relu"], 1)

                        make_diag(0)
                        for b in range(NB):
                            weights(0, b)
                            if b == 12:
                                make_diag(1)
                        with dve.Fori(1, NG) as c:
                            for b in range(NB):
                                weights(c, b)
                                if b == 1:
                                    normalise(c)
                                if b == 3:
                                    dve.wait_ge(S["o_free"], c)
                                    relu(c)
                                if b == 12:
                                    dve.wait_ge(S["r_ready"], c + 1)
                                    make_diag(c + 1)
                        normalise(NG)
                        dve.wait_ge(S["o_free"], NG)
                        relu(NG)

                @block.tensor
                def _(pe):
                    with pe.If(pe.value_load(flag[0:1, 0:1], min_val=0, max_val=1) > 0):
                        def spread(c, par):
                            pe.wait_ge(S["diag"], c + 1)
                            bank = pR[:, par, :]
                            d = diag[:, :, :, :].rearrange("p t b m -> p (t b m)")
                            for a, z0 in ((0, 512), (512, 1024), (1024, 2 * CHUNK)):
                                ins = nc.tensor.matmul(bank[:, a:z0], ones[:, :], d[:, a:z0], start=True, stop=True)
                            ins.then_inc(S["r_ready"], 1)

                        def products(c, b):
                            pe.wait_ge(S["p_ready"], c * NB + b + 1)
                            for k in range(GB):
                                ins = nc.tensor.matmul(pO[:, bank_of(k, D + 1):bank_of(k, D + 1) + D + 1], e1[:, b % SLOTS, k * P:(k + 1) * P],
                                                       val[:, b, :], start=(b == 0 and k in (0, 3)), stop=(b == NB - 1), skip_group_check=True)
                            ins.then_inc(S["p_used"], 1)

                        pe.sem_inc(S["p_used"], NB)
                        spread(0, 0)
                        for b in range(NB):
                            products(0, b)
                            if b == 14:
                                spread(1, 1)
                        with pe.Fori(0, NG // 2) as i:
                            for c, par in ((i * 2 + 1, 0), (i * 2 + 2, 1)):
                                pe.wait_ge(S["o_free"], c)
                                for b in range(NB):
                                    products(c, b)
                                    if b == 14:
                                        spread(c + 1, par)

        GAT_SLOTS = [b % 4 if b < 16 else (b - 16) % 3 for b in range(NB)]
        ON_POOL = [b for b in range(NB) if b % 2]
        ON_DVE = [b for b in range(NB) if b not in ON_POOL]

        def before(b):
            same = [x for x in range(NB) if GAT_SLOTS[x] == GAT_SLOTS[b]]
            return max([x + NB for x in same if x < b] or same)

        def one_shift_weights(tag, hN, val, diag, e1, e2, r2, al, al2, m, R, z, rz, rng, b_row, ones, flag, pR, pO):
            S = {n: sem(f"{tag}f_{n}") for n in ("args", "exps", "diag", "r_ready", "e_ready", "m_done", "p_dve", "p_pool", "p_used",
                                                 "o_free", "z_own", "relu", "r2", "h")}
            sums = diag[:, :, :, :].rearrange("p t b m -> p (t b m)")[:, 0:GB * (D + 1)].rearrange("p (b w) -> p b w", b=GB)
            step = Chain(f"{tag}f_dve", nc.vector)
            ones_if = lambda engine: engine.If(engine.value_load(flag[0:1, 0:1], min_val=0, max_val=1) < 1)
            NDVE, NPOOL = len(ON_DVE), len(ON_POOL)
            with nc.Block() as block:
                @block.scalar
                def _(act):
                    with ones_if(act):
                        act.wait_ge(S["args"], 1)
                        nc.scalar.activation(al2[:, :], al[:, 0, :], ACT.Exp, scale=SLOPE)
                        nc.scalar.activation(R[:, :, 0:NB], R[:, :, 0:NB], ACT.Exp).then_inc(S["exps"], 1)
                        act.wait_ge(S["exps"], 1)
                        nc.scalar.activation(al[:, 0, :], al[:, 0, :], ACT.Exp).then_inc(S["exps"], 1)
                        act.wait_ge(S["exps"], 2)

                        def copy_sums(c):
                            act.wait_ge(S["p_used"], c * NB + NB)
                            for k0, k1 in ((0, 3), (3, GB)):
                                o = pO[:, bank_of(k0, D + 1):bank_of(k0, D + 1) + (k1 - k0) * (D + 1)]
                                ins = nc.scalar.activation(sums[:, k0:k1, :].rearrange("p b w -> p (b w)"), o, ACT.Copy)
                            ins.then_inc(S["o_free"], 1)

                        def second(c, par, first=False):
                            act.wait_ge(S["r_ready"], c + 1)
                            act.wait_ge(S["e_ready"], c * NB + 1)
                            nc.scalar.activation(r2[:, :], pR[:, par, CHUNK:2 * CHUNK], ACT.Copy).then_inc(S["r2"], 1)
                            act.wait_ge(S["r2"], c + 1)
                            for b in range(NB):
                                act.wait_ge(S["m_done"], c * NB + (b + 1 if b >= 2 else 2 - b))
                                nc.scalar.activation(e2[:, b % 2, :], r2[:, :], ACT.Copy, scale=al2[:, b:b + 1]).then_inc(S["e_ready"], 1)
                                if b == 2 and not first:
                                    copy_sums(c)

                        act.sem_inc(S["e_ready"], 1)
                        second(0, 0, first=True)
                        with act.Fori(0, NG // 2) as i:
                            second(i * 2 + 1, 1)
                            second(i * 2 + 2, 0)
                        copy_sums(NG)

                @block.gpsimd
                def _(pool):
                    with ones_if(pool):
                        def weigh(c):
                            for n, b in enumerate(ON_POOL):
                                pool.wait_ge(S["m_done"], c * NB + b + 3)
                                v = e1[GAT_SLOTS[b]]
                                nc.gpsimd.tensor_tensor(v, v, counts[:, b, bass.ds(c * CHUNK, CHUNK)], ALU.mult).then_inc(S["p_pool"], 1)

                        with pool.Fori(0, NG) as c:
                            weigh(c)

                @block.vector
                def _(dve):
                    with ones_if(dve):
                        step(nc.vector.tensor_scalar(al[:, 0, :], al[:, 0, :], rng[:, 4:5], None, ALU.subtract))
                        step(nc.vector.tensor_scalar(al[:, 1, :], al[:, 1, :], rng[:, 4:5], None, ALU.add))
                        step(nc.vector.scalar_tensor_tensor(m[:, :], al[:, 1, :], SLOPE, al[:, 1, :], ALU.mult, ALU.max))
                        step(nc.vector.tensor_tensor(R[:, 0, 0:NB], al[:, 1, :], m[:, :], ALU.subtract))
                        nc.vector.scalar_tensor_tensor(R[:, 1, 0:NB], al[:, 1, :], SLOPE, m[:, :], ALU.mult, ALU.subtract).then_inc(S["args"], 1)
                        dve.sem_inc(S["m_done"], 2)
                        dve.wait_ge(S["exps"], 2)

                        def make_diag(c):
                            for t in range(2):
                                ins = nc.vector.tensor_tensor(diag[:, t, :, :], ident[:, :].unsqueeze(1).broadcast_to([P, GB, P]),
                                                              R[:, t, bass.ds(c * GB, GB)].unsqueeze(2).broadcast_to([P, GB, P]), ALU.mult)
                            ins.then_inc(S["diag"], 1)

                        def maximum(c, par, b):
                            dve.wait_ge(S["e_ready"], c * NB + b + 2)
                            dve.wait_ge(S["p_used"], c * NB + before(b) + 1)
                            nc.vector.scalar_tensor_tensor(e1[GAT_SLOTS[b]], pR[:, par, 0:CHUNK], al[:, 0, b:b + 1], e2[:, b % 2, :],
                                                           ALU.mult, ALU.max).then_inc(S["m_done"], 1)

                        def weigh(c, b):
                            if b in ON_DVE:
                                dve.wait_ge(S["m_done"], c * NB + b + 3)
                                v = e1[GAT_SLOTS[b]]
                                nc.vector.tensor_tensor(v, v, counts[:, b, bass.ds(c * CHUNK, CHUNK)], ALU.mult).then_inc(S["p_dve"], 1)

                        def normalise(c):
                            dve.wait_ge(S["o_free"], c)
                            nc.vector.tensor_scalar(z[:, :].unsqueeze(2), sums[:, :, D:D + 1], TINY, None, ALU.max).then_inc(S["z_own"], 1)
                            dve.wait_ge(S["z_own"], c * 2 - 1)
                            nc.vector.reciprocal(rz[:, :], z[:, :]).then_inc(S["z_own"], 1)
                            dve.wait_ge(S["z_own"], c * 2)
                            for k in range(GB):
                                ins = nc.vector.scalar_tensor_tensor(hN[:, bass.ds((c - 1) * GB + k, 1), :].squeeze(1), sums[:, k, 0:D], rz[:, k:k + 1], b_row[:, :],
                                                                     ALU.mult, ALU.add)
                            ins.then_inc(S["h"], 1)

                        def relu(c):
                            v = hN[:, bass.ds((c - 1) * GB, GB), :]
                            nc.vector.tensor_scalar(v, v, 0.0, None, ALU.max).then_inc(S["relu"], 1)

                        def chunk(c, par, first=False):
                            for b in range(NB):
                                maximum(c, par, b)
                                if b:
                                    weigh(c, b - 1)
                                if b == 5 and not first:
                                    normalise(c)
                                if b == 7 and not first:
                                    dve.wait_ge(S["h"], c)
                                    relu(c)
                                if b == 12:
                                    if not first:
                                        dve.wait_ge(S["r_ready"], c + 1)
                                    make_diag(c + 1)
                            weigh(c, NB - 1)

                        make_diag(0)
                        chunk(0, 0, first=True)
                        with dve.Fori(0, NG // 2) as i:
                            chunk(i * 2 + 1, 1)
                            chunk(i * 2 + 2, 0)
                        normalise(NG)
                        dve.wait_ge(S["h"], NG)
                        relu(NG)

                @block.tensor
                def _(pe):
                    with ones_if(pe):
                        PIECES = ((0, 512), (512, 1024), (1024, 2 * CHUNK))

                        def spread(c, par, pieces=PIECES):
                            pe.wait_ge(S["diag"], c + 1)
                            bank = pR[:, par, :]
                            d = diag[:, :, :, :].rearrange("p t b m -> p (t b m)")
                            for a, z0 in pieces:
                                ins = nc.tensor.matmul(bank[:, a:z0], ones[:, :], d[:, a:z0], start=True, stop=True)
                            if pieces[-1] == PIECES[-1]:
                                ins.then_inc(S["r_ready"], 1)

                        def products(c, b):
                            if b in ON_POOL:
                                pe.wait_ge(S["p_pool"], c * NPOOL + ON_POOL.index(b) + 1)
                            else:
                                pe.wait_ge(S["p_dve"], c * NDVE + ON_DVE.index(b) + 1)
                            for k in range(GB):
                                ins = nc.tensor.matmul(pO[:, bank_of(k, D + 1):bank_of(k, D + 1) + D + 1], e1[GAT_SLOTS[b]][:, k * P:(k + 1) * P],
                                                       val[:, b, :], start=(b == 0 and k in (0, 3)), stop=(b == NB - 1), skip_group_check=True)
                            ins.then_inc(S["p_used"], 1)

                        pe.sem_inc(S["p_used"], NB)
                        spread(0, 0)
                        for b in range(NB):
                            products(0, b)
                            if b in (13, 16, 19):
                                spread(1, 1, PIECES[(b - 13) // 3:(b - 13) // 3 + 1])
                        with pe.Fori(0, NG // 2) as i:
                            for c, par in ((i * 2 + 1, 0), (i * 2 + 2, 1)):
                                pe.wait_ge(S["o_free"], c)
                                for b in range(NB):
                                    products(c, b)
                                    if b in (13, 16, 19):
                                        spread(c + 1, par, PIECES[(b - 13) // 3:(b - 13) // 3 + 1])

        def destination_maxima(tag, acc, ap, al, amax, rng, pR, flag):
            S = {n: sem(f"{tag}x_{n}") for n in ("own", "ready", "turned", "reduced")}
            step = Chain(f"{tag}x_dve", nc.vector)
            with nc.Block() as block:
                @block.vector
                def _(dve):
                    with dve.If(dve.value_load(flag[0:1, 0:1], min_val=0, max_val=1) > 0):
                        step(nc.vector.tensor_scalar(ap[:, :], al[:, 0, :], rng[:, 5:6], rng[:, 7:8], ALU.add, ALU.mult))
                        step(nc.vector.tensor_scalar(ap[:, :], ap[:, :], 0.5, None, ALU.add))
                        nc.vector.memset(acc[:, :], 0.0).then_inc(S["own"], 1)
                        with dve.Fori(0, NB) as b:
                            dve.wait_ge(S["own"], b + 1)
                            nc.vector.scalar_tensor_tensor(acc[:, :], counts[:, bass.ds(b, 1), :].squeeze(1), ap[:, bass.ds(b, 1)],
                                                           acc[:, :], ALU.min, ALU.max).then_inc(S["own"], 1)
                        for g in range(NG):
                            dve.wait_ge(S["turned"], g + 1)
                            nc.vector.tensor_reduce(amax[:, g * GB:(g + 1) * GB], pR[:, 0, 0:CHUNK].rearrange("p (b n) -> p b n", b=GB), AX.X,
                                                    ALU.max).then_inc(S["reduced"], 1)
                        dve.wait_ge(S["reduced"], NG)
                        step(nc.vector.tensor_scalar(amax[:, :], amax[:, :], 0.5, rng[:, 6:7], ALU.subtract, ALU.mult))
                        step(nc.vector.tensor_scalar(amax[:, :], amax[:, :], rng[:, 5:6], None, ALU.subtract))

                @block.tensor
                def _(pe):
                    with pe.If(pe.value_load(flag[0:1, 0:1], min_val=0, max_val=1) > 0):
                        pe.wait_ge(S["own"], NB + 1)
                        for g in range(NG):
                            if g:
                                pe.wait_ge(S["reduced"], g)
                            for k in range(GB):
                                ins = nc.tensor.transpose(pR[:, 0, k * P:(k + 1) * P], acc[:, (g * GB + k) * P:(g * GB + k + 1) * P], ident[:, :])
                            ins.then_inc(S["turned"], 1)

        def local_attention(hN):
            tag = "l2"
            WD = D + 1
            with ExitStack() as s:
                val = sb(s, f"{tag}_val", [P, NB, WD], fp32)
                space = sb(s, f"{tag}_space", [P, (3 * NB * WD + 1) // 2], fp32)
                acc = space[:, 0:NP]
                parts = space[:, :].bitcast(bf16)[:, 0:3 * NB * WD].rearrange("p (b t w) -> p b t w", b=NB, t=3)
                turn = sb(s, f"{tag}_turn", [P, 3, CHUNK], bf16)
                e2 = space[:, NP:NP + CHUNK]
                turn32 = turn[:, :, :].rearrange("p t n -> p (t n)").bitcast(fp32)
                ones = turn32[:, 0:P]
                w_row = turn32[:, P:3 * P].rearrange("p (t d) -> p t d", t=2)
                al = sb(s, f"{tag}_al", [P, NB], fp32)
                A = sb(s, f"{tag}_A", [P, NB], fp32)
                ap = sb(s, f"{tag}_ap", [P, NB], fp32)
                amax = sb(s, f"{tag}_amax", [P, NB], fp32)
                rng = sb(s, f"{tag}_rng", [P, 8], fp32)
                flag = sb(s, f"{tag}_flag", [P, 1], i32)
                fin = scores[:, 0:2 * (WD + 2)].rearrange("p (t w) -> p t w", t=2)
                pA = pb(s, f"{tag}_pA", [P, 1024])
                pB = pb(s, f"{tag}_pB", [P, 1024])
                pC = pb(s, f"{tag}_pC", [P, 1024])
                pO = pb(s, f"{tag}_pO", [P, 1024])
                S = {n: sem(f"{tag}_{n}") for n in ("w_in", "const", "tanh", "rng_r", "rng_t", "rng_s", "rng_b")}
                step = Chain(f"{tag}_dve", nc.vector)
                a3 = space[:, 0:NP].rearrange("p (b d) -> p b d", b=NB)
                with nc.Block() as block:
                    @block.sync
                    def _(sp):
                        sp.dma_start(w_row[:, 0, :], T["L2_gnn_high_atts"].broadcast_to([P, D])).then_inc(S["w_in"], 16)
                        sp.dma_start(w_row[:, 1, :], T["L2_gnn_diff_atts"].broadcast_to([P, D])).then_inc(S["w_in"], 16)

                    @block.gpsimd
                    def _(pool):
                        nc.gpsimd.memset(ones[:, :], 1.0).then_inc(S["const"], 1)
                        nc.gpsimd.memset(val[:, :, D:WD], 1.0)

                    @block.scalar
                    def _(act):
                        nc.scalar.activation(val[:, :, 0:D], hN[:, :, :], ACT.Tanh).then_inc(S["tanh"], 1)

                    @block.vector
                    def _(dve):
                        dve.wait_ge(S["w_in"], 32)
                        step(nc.vector.scalar_tensor_tensor(w_row[:, 0, :], w_row[:, 1, :], -0.5, w_row[:, 0, :], ALU.mult, ALU.add))
                        dve.wait_ge(S["tanh"], 1)
                        step(nc.vector.tensor_tensor(a3, val[:, :, 0:D], w_row[:, 0, :].unsqueeze(1).broadcast_to([P, NB, D]), ALU.mult))
                        step(nc.vector.tensor_reduce(al[:, :], a3, AX.X, ALU.add))
                        logit_range(step, dve, al[:, :], rng, ap[:, :], S, pC[:, :], flag)

                    @block.tensor
                    def _(pe):
                        pe.wait_ge(S["const"], 1)
                        logit_range_pe(pe, rng, ones, S, pC[:, :])
                end_stage()
                one_shift(hN, tag, val, parts, turn, fin, al, A, rng, flag, (pA, pB, pC), pO)
                end_stage()
                own_shifts(hN, tag, val, acc, e2, ones, al, ap, amax, rng, flag, pA, pB, pC, pO)

        def one_shift(hN, tag, val, parts, turn, fin, al, A, rng, flag, pTurn, pO):
            WD = D + 1
            U = NG
            S = {n: sem(f"{tag}f_{n}") for n in ("A", "left", "w", "turned", "copied", "used", "read", "own", "done")}
            step = Chain(f"{tag}f_dve", nc.vector)
            with nc.Block() as block:
                @block.scalar
                def _(act):
                    with act.If(act.value_load(flag[0:1, 0:1], min_val=0, max_val=1) < 1):
                        act.wait_ge(S["A"], 1)
                        nc.scalar.activation(A[:, :], al[:, :], ACT.Exp).then_inc(S["A"], 1)
                        act.sem_inc(S["copied"], 2)
                        for t in range(3):
                            for g in range(NG):
                                act.wait_ge(S["left"], t * NG + g + 1)
                                nc.scalar.activation(parts[:, g * GB:(g + 1) * GB, t, :], val[:, g * GB:(g + 1) * GB, :], ACT.Copy).then_inc(S["w"], 1)

                        def copies(b):
                            for g in range(U):
                                act.wait_ge(S["turned"], b * U + g + 1)
                                act.wait_ge(S["used"], b * U + g + 1)
                                nc.scalar.activation(turn[:, g % 3, :], pTurn[g % 3][:, 0:CHUNK], ACT.Copy).then_inc(S["copied"], 1)

                        with act.Fori(0, NB) as b:
                            copies(b)
                        for g in range(NG):
                            act.wait_ge(S["done"], (g + 1) * GB)
                            v = hN[:, g * GB:(g + 1) * GB, :]
                            nc.scalar.activation(v, v, ACT.Tanh)

                @block.vector
                def _(dve):
                    with dve.If(dve.value_load(flag[0:1, 0:1], min_val=0, max_val=1) < 1):
                        nc.vector.tensor_scalar(al[:, :], al[:, :], rng[:, 4:5], None, ALU.subtract).then_inc(S["A"], 1)
                        dve.sem_inc(S["read"], 2)
                        dve.wait_ge(S["A"], 2)
                        for g in range(NG):
                            v = val[:, g * GB:(g + 1) * GB, :]
                            nc.vector.tensor_tensor(v, v, A[:, g * GB:(g + 1) * GB].unsqueeze(2).broadcast_to([P, GB, WD]), ALU.mult).then_inc(S["left"], 1)
                        for t in range(2):
                            for g in range(NG):
                                v = val[:, g * GB:(g + 1) * GB, :]
                                dve.wait_ge(S["w"], t * NG + g + 1)
                                nc.vector.tensor_tensor(v, v, parts[:, g * GB:(g + 1) * GB, t, :], ALU.subtract).then_inc(S["left"], 1)

                        def finish(b, par):
                            def own(n, ins):
                                ins.then_inc(S["own"], 1)
                                dve.wait_ge(S["own"], b * 4 + n)

                            dve.wait_ge(S["used"], b * U + U + 2)
                            o = pO[:, par * 512:par * 512 + 3 * WD].rearrange("p (t w) -> p t w", t=3)
                            t = fin[:, par, :]
                            own(1, nc.vector.tensor_reduce(t[:, 0:WD], o.rearrange("p t w -> p w t"), AX.X, ALU.add))
                            own(2, nc.vector.tensor_scalar(t[:, WD:WD + 1], t[:, D:WD], TINY, None, ALU.max))
                            own(3, nc.vector.reciprocal(t[:, WD + 1:WD + 2], t[:, WD:WD + 1]))
                            dve.sem_inc(S["read"], 1)
                            own(4, nc.vector.tensor_scalar(hN[:, bass.ds(b, 1), :].squeeze(1), t[:, 0:D], t[:, WD + 1:WD + 2], None, ALU.mult))
                            dve.sem_inc(S["done"], 1)

                        with dve.Fori(0, NB // 2) as i:
                            finish(i * 2, 0)
                            finish(i * 2 + 1, 1)
                        finish(NB - 1, 0)

                @block.tensor
                def _(pe):
                    with pe.If(pe.value_load(flag[0:1, 0:1], min_val=0, max_val=1) < 1):
                        pe.sem_inc(S["used"], 2)

                        def turned(b, g):
                            pe.wait_ge(S["copied"], b * U + g + 1)
                            for k in range(GB):
                                c = g * GB + k
                                src = counts[:, b, c * P:(c + 1) * P] if isinstance(b, int) else counts[:, bass.ds(b, 1), c * P:(c + 1) * P].squeeze(1)
                                ins = nc.tensor.matmul(pTurn[g % 3][:, k * P:(k + 1) * P], src, identb[:, :], start=True, stop=True)
                            ins.then_inc(S["turned"], 1)

                        def sources(b, par, last=False):
                            for g in range(U):
                                if g + 1 < U:
                                    turned(b, g + 1)
                                elif not last:
                                    turned(b + 1, 0)
                                if g == 0:
                                    pe.wait_ge(S["read"], b + 1)
                                pe.wait_ge(S["w"], 2 * NG + g + 1)
                                pe.wait_ge(S["copied"], b * U + g + 3)
                                for k in range(GB):
                                    ins = nc.tensor.matmul(pO[:, par * 512:par * 512 + 3 * WD], turn[:, g % 3, k * P:(k + 1) * P],
                                                           parts[:, g * GB + k, :, :].rearrange("p t w -> p (t w)"), start=(g == 0 and k == 0),
                                                           stop=(g == U - 1 and k == GB - 1), skip_group_check=True)
                                ins.then_inc(S["used"], 1)

                        turned(0, 0)
                        with pe.Fori(0, NB // 2) as i:
                            sources(i * 2, 0)
                            sources(i * 2 + 1, 1)
                        sources(NB - 1, 0, last=True)

        def own_shifts(hN, tag, val, acc, e2, ones, al, ap, amax, rng, flag, pA, pB, pC, pO):
            e1 = acc[:, 2 * CHUNK:(2 + SLOTS) * CHUNK].rearrange("p (t n) -> p t n", t=SLOTS)
            diag = acc[:, 0:CHUNK].rearrange("p (b m) -> p b m", b=GB)
            z, rz = ap[:, 0:GB], ap[:, GB:2 * GB]
            S = {n: sem(f"{tag}o_{n}") for n in ("acc_ready", "acc_t", "acc_m", "diag_ready", "r_ready", "e_ready", "p_ready", "p_used",
                                                  "o_free", "c_ready", "c_used", "tanh")}
            step = Chain(f"{tag}o_dve", nc.vector)
            with nc.Block() as block:
                @block.scalar
                def _(act):
                    with act.If(act.value_load(flag[0:1, 0:1], min_val=0, max_val=1) > 0):
                        act.sem_inc(S["e_ready"], 1)
                        act.sem_inc(S["tanh"], 1)
                        with act.Fori(0, NG) as c:
                            for b in range(NB):
                                if b == 0:
                                    act.wait_ge(S["r_ready"], c + 1)
                                last = b - SLOTS + NB if b >= SLOTS else max(x for x in range(NB) if x % SLOTS == b % SLOTS)
                                act.wait_ge(S["p_used"], c * NB + last + 1)
                                nc.scalar.activation(e1[:, b % SLOTS, :], pA[:, 0:CHUNK], ACT.Exp, bias=al[:, b:b + 1]).then_inc(S["e_ready"], 1)
                            act.wait_ge(S["o_free"], c + 2)
                            nc.scalar.activation(hN[:, bass.ds(c * GB, GB), :], e2[:, :].rearrange("p (b d) -> p b d", b=GB), ACT.Tanh).then_inc(S["tanh"], 1)

                @block.vector
                def _(dve):
                    with dve.If(dve.value_load(flag[0:1, 0:1], min_val=0, max_val=1) > 0):
                        step(nc.vector.tensor_scalar(ap[:, :], al[:, :], rng[:, 5:6], rng[:, 7:8], ALU.add, ALU.mult))
                        step(nc.vector.tensor_scalar(ap[:, :], ap[:, :], 0.5, None, ALU.add))
                        step(nc.vector.memset(acc, 0.0))
                        dve.sem_inc(S["c_used"], 1)
                        with dve.Fori(0, NB) as b:
                            for c in range(NG):
                                dve.wait_ge(S["c_ready"], b * NG + c + 1)
                                dve.wait_ge(S["c_used"], b * NG + c + 1)
                                v = acc[:, c * CHUNK:(c + 1) * CHUNK]
                                nc.vector.scalar_tensor_tensor(v, (pO if c % 2 else pC)[:, 0:CHUNK], ap[:, bass.ds(b, 1)], v,
                                                               ALU.min, ALU.max).then_inc(S["c_used"], 1)
                        dve.wait_ge(S["c_used"], NB * NG + 1)
                        dve.sem_inc(S["acc_ready"], 1)
                        for g in range(NG):
                            dve.wait_ge(S["acc_t"], g + 1)
                            nc.vector.tensor_reduce(amax[:, g * GB:(g + 1) * GB], pA[:, 0:CHUNK].rearrange("p (b n) -> p b n", b=GB), AX.X,
                                                    ALU.max).then_inc(S["acc_m"], 1)
                        dve.wait_ge(S["acc_m"], NG)
                        step(nc.vector.tensor_scalar(amax[:, :], amax[:, :], 0.5, rng[:, 6:7], ALU.subtract, ALU.mult))
                        step(nc.vector.tensor_scalar(amax[:, :], amax[:, :], rng[:, 5:6], -1.0, ALU.subtract, ALU.mult))
                        dve.sem_inc(S["o_free"], 1)
                        with dve.Fori(0, NG) as c:
                            nc.vector.tensor_tensor(diag, ident[:, :].unsqueeze(1).broadcast_to([P, GB, P]),
                                                    amax[:, bass.ds(c * GB, GB)].unsqueeze(2).broadcast_to([P, GB, P]), ALU.mult).then_inc(S["diag_ready"], 1)
                            for b in range(NB):
                                dve.wait_ge(S["e_ready"], c * NB + b + 2)
                                v = e1[:, b % SLOTS, :]
                                dve.wait_ge(S["c_ready"], c * NB + (NB * NG + b + 1))
                                nc.vector.scalar_tensor_tensor(v, v, CLAMP, (pB if b % 2 else pC)[:, 0:CHUNK], ALU.min, ALU.mult).then_inc(S["p_ready"], 1)
                            dve.wait_ge(S["p_used"], c * NB + 2 * NB)
                            dve.wait_ge(S["tanh"], c + 1)
                            for k0, k1 in ((0, 3), (3, GB)):
                                o = pO[:, bank_of(k0, D + 1):bank_of(k0, D + 1) + (k1 - k0) * (D + 1)].rearrange("p (b w) -> p b w", w=D + 1)
                                nc.vector.tensor_scalar(z[:, k0:k1].unsqueeze(2), o[:, :, D:D + 1], TINY, None, ALU.max).then_inc(S["acc_m"], 1)
                            dve.wait_ge(S["acc_m"], c * 3 + NG + 2)
                            nc.vector.reciprocal(rz, z).then_inc(S["acc_m"], 1)
                            dve.wait_ge(S["acc_m"], c * 3 + NG + 3)
                            for k in range(GB):
                                o = pO[:, bank_of(k, D + 1):bank_of(k, D + 1) + D]
                                ins = nc.vector.tensor_scalar(e2[:, k * D:(k + 1) * D], o, rz[:, k:k + 1], None, ALU.mult)
                            ins.then_inc(S["o_free"], 1)

                @block.tensor
                def _(pe):
                    with pe.If(pe.value_load(flag[0:1, 0:1], min_val=0, max_val=1) > 0):
                        def turned(b, c, bank):
                            for k in range(GB):
                                src = (counts[:, c * GB + k, bass.ds(b * P, P)] if isinstance(c, int) else
                                       counts[:, bass.ds(c * GB + k, 1), b * P:(b + 1) * P].squeeze(1))
                                ins = nc.tensor.matmul(bank[:, k * P:(k + 1) * P], src, identb[:, :], start=True, stop=True)
                            ins.then_inc(S["c_ready"], 1)

                        with pe.Fori(0, NB) as b:
                            for c in range(NG):
                                pe.wait_ge(S["c_used"], b * NG + (c if c >= 1 else 1))
                                turned(b, c, pO if c % 2 else pC)
                        pe.wait_ge(S["acc_ready"], 1)
                        for g in range(NG):
                            if g:
                                pe.wait_ge(S["acc_m"], g)
                            for k in range(GB):
                                ins = nc.tensor.transpose(pA[:, k * P:(k + 1) * P], acc[:, (g * GB + k) * P:(g * GB + k + 1) * P], ident[:, :])
                            ins.then_inc(S["acc_t"], 1)
                        pe.sem_inc(S["p_used"], NB)
                        with pe.Fori(0, NG) as c:
                            pe.wait_ge(S["diag_ready"], c + 1)
                            pe.wait_ge(S["e_ready"], c * NB + 1)
                            nc.tensor.matmul(pA[:, 0:512], ones[:, :], diag[:, 0:4, :].rearrange("p b m -> p (b m)"), start=True, stop=True)
                            nc.tensor.matmul(pA[:, 512:CHUNK], ones[:, :], diag[:, 4, :], start=True, stop=True).then_inc(S["r_ready"], 1)
                            pe.wait_ge(S["o_free"], c + 1)
                            for b in range(NB):
                                if b == 0:
                                    turned(0, c, pC)
                                else:
                                    pe.wait_ge(S["p_ready"], c * NB + b)
                                if b + 1 < NB:
                                    turned(b + 1, c, pC if b % 2 else pB)
                                pe.wait_ge(S["p_ready"], c * NB + b + 1)
                                for k in range(GB):
                                    ins = nc.tensor.matmul(pO[:, bank_of(k, D + 1):bank_of(k, D + 1) + D + 1], e1[:, b % SLOTS, k * P:(k + 1) * P],
                                                           val[:, b, :], start=(b == 0 and k in (0, 3)), stop=(b == NB - 1), skip_group_check=True)
                                ins.then_inc(S["p_used"], 1)

        def gin(hN):
            L = 3
            HW = CHUNK // 2
            names_ = ("b1", "bn_mean", "bn_var", "gamma", "beta", "b2")
            B1, MEAN, VAR, GAMMA, BETA, B2 = (slice(L * k, L * k + L) for k in range(6))
            with ExitStack() as s:
                first = sb(s, "i_first", [P, NB, 3, D], bf16)
                extra = sb(s, "i_extra", [P, 2 * GB, 3, D], bf16)
                in_hN = hN[:, :, :].rearrange("p b d -> p (b d)").bitcast(bf16)[:, 0:3 * GB * 3 * D].rearrange("p (b t d) -> p b t d", b=3 * GB, t=3)
                w = sb(s, "i_w", [P, L, 2, D], fp32)
                cols = sb(s, "i_cols", [P, 6 * L], fp32)
                t1 = sb(s, "i_t1", [P, CHUNK], fp32)
                rows = t1[0:6 * L, 0:D]
                z = sb(s, "i_z", [P, CHUNK], fp32)
                rest = z[:, :].rearrange("p (b d) -> p b d", b=GB)
                pZ = [pb(s, f"i_pZ{k}", [P, 1024]) for k in range(2)]
                pM = pb(s, "i_pM", [P, 1024])
                pT = pb(s, "i_pT", [P, 1024])
                names = ("in", "cols_t", "cols_c", "sd", "sd_d", "tr", "tr_used", "h_split", "agg", "z_ready", "m1", "m1_act", "m2", "h_new", "bn")
                S = {n: sem(f"i_{n}") for n in names}
                step = Chain("i_dve", nc.vector)

                def group(l, g):
                    if l % 2 == 0:
                        return first[:, g * GB:(g + 1) * GB, :, :]
                    return in_hN[:, g * GB:(g + 1) * GB, :, :] if g < 3 else extra[:, (g - 3) * GB:(g - 2) * GB, :, :]

                def halves(bank):
                    return bank[:, :].rearrange("p (h n) -> p h n", h=2)[:, :, 0:HW]

                with nc.Block() as block:
                    @block.sync
                    def _(sp):
                        for k, n in enumerate(names_):
                            sp.dma_start(rows[L * k:L * k + L, :], T[f"L3_gnn_{n}"]).then_inc(S["in"], 16)
                        sp.dma_start(w[:, :, 0, :], T["L3_gnn_W1"].rearrange("l i o -> i l o")).then_inc(S["in"], 16)
                        sp.dma_start(w[:, :, 1, :], T["L3_gnn_W2"].rearrange("l i o -> i l o")).then_inc(S["in"], 16)

                    @block.tensor
                    def _(pe):
                        pe.wait_ge(S["in"], 16 * 8)
                        nc.tensor.transpose(pT[:, 0:6 * L], rows, ident[0:6 * L, 0:6 * L]).then_inc(S["cols_t"], 1)
                        pe.wait_ge(S["cols_c"], 1)
                        def first_product(l, n):
                            pe.wait_ge(S["z_ready"], n + 3)
                            for h in range(2):
                                ins = nc.tensor.matmul(pM[:, h * 512:h * 512 + HW], w[:, l, 0, :], z[:, h * HW:(h + 1) * HW], start=True, stop=True)
                            ins.then_inc(S["m1"], 1)

                        def second_product(l, n):
                            pe.wait_ge(S["m1_act"], n + 1)
                            for h in range(2):
                                ins = nc.tensor.matmul(pM[:, h * 512:h * 512 + HW], w[:, l, 1, :], t1[:, h * HW:(h + 1) * HW], start=True, stop=True)
                            ins.then_inc(S["m2"], 1)

                        def turn_back(n):
                            pe.wait_ge(S["h_new"], n + 1)
                            pe.wait_ge(S["tr_used"], n + 1)
                            for k in range(GB):
                                ins = nc.tensor.transpose(pT[:, k * P:(k + 1) * P], t1[:, k * P:(k + 1) * P], ident[:, :])
                            ins.then_inc(S["tr"], 1)

                        def aggregate(l, c, n, par, before=None):
                            pe.wait_ge(S["z_ready"], n + 1)
                            for b in range(NB):
                                if isinstance(c, int) and b % GB == 0:
                                    pe.wait_ge(S["h_split"], l * NG + b // GB + 1)
                                for t in range(3):
                                    for h in range(2):
                                        ins = nc.tensor.matmul(pZ[par][:, h * 512:h * 512 + HW], group(l, b // GB)[:, b % GB, t, :],
                                                               counts[:, b, bass.ds(c * CHUNK + h * HW, HW)],
                                                               start=(b == 0 and t == 0), stop=(b == NB - 1 and t == 2), skip_group_check=True)
                                if before is not None and b == 2:
                                    first_product(before, n - 1)
                                if before is not None and b == 6:
                                    second_product(before, n - 1)
                                if before is not None and b == 10:
                                    turn_back(n - 1)
                            ins.then_inc(S["agg"], 1)

                        for l in range(L):
                            base = l * NG
                            aggregate(l, 0, base, l % 2, l - 1 if l else None)
                            with pe.Fori(0, NG // 2) as i:
                                aggregate(l, i * 2 + 1, i * 2 + (base + 1), (l + 1) % 2, l)
                                aggregate(l, i * 2 + 2, i * 2 + (base + 2), l % 2, l)
                        n = L * NG - 1
                        first_product(L - 1, n)
                        second_product(L - 1, n)
                        turn_back(n)

                    @block.scalar
                    def _(act):
                        act.wait_ge(S["sd"], 1)
                        nc.scalar.activation(cols[:, VAR], cols[:, VAR], ACT.Sqrt).then_inc(S["sd_d"], 1)
                        act.wait_ge(S["bn"], 1)
                        for l in range(L):
                            for c in range(NG):
                                n = l * NG + c
                                act.wait_ge(S["m1"], n + 1)
                                if n:
                                    act.wait_ge(S["tr"], n)
                                nc.scalar.activation(t1[:, :].rearrange("p (h n) -> p h n", h=2), halves(pM), ACT.Relu, bias=cols[:, BETA][:, l:l + 1],
                                                     scale=cols[:, GAMMA][:, l:l + 1]).then_inc(S["m1_act"], 1)
                                act.wait_ge(S["m2"], n + 1)
                                nc.scalar.activation(t1[:, :].rearrange("p (h n) -> p h n", h=2), halves(pM), ACT.Relu,
                                                     bias=cols[:, B2][:, l:l + 1]).then_inc(S["h_new"], 1)

                    @block.vector
                    def _(dve):
                        def split(l, g, source):
                            o = group(l, g)
                            step(nc.vector.tensor_copy(o[:, :, 0, :], source))
                            step(nc.vector.tensor_tensor(rest, source, o[:, :, 0, :], ALU.subtract))
                            step(nc.vector.tensor_copy(o[:, :, 1, :], rest))
                            step(nc.vector.tensor_tensor(rest, rest, o[:, :, 1, :], ALU.subtract))
                            nc.vector.tensor_copy(o[:, :, 2, :], rest).then_inc(S["h_split"], 1)

                        dve.sem_inc(S["z_ready"], 2)
                        dve.sem_inc(S["tr_used"], 1)
                        split(0, 0, hN[:, 0:GB, :])
                        dve.wait_ge(S["cols_t"], 1)
                        nc.vector.tensor_copy(cols[:, :], pT[:, 0:6 * L]).then_inc(S["cols_c"], 1)
                        dve.wait_ge(S["cols_c"], 1)
                        for g in range(1, NG):
                            dve.wait_ge(S["h_split"], g)
                            split(0, g, hN[:, g * GB:(g + 1) * GB, :])
                        nc.vector.tensor_scalar(cols[:, VAR], cols[:, VAR], EPS, None, ALU.add).then_inc(S["sd"], 1)
                        dve.wait_ge(S["sd_d"], 1)
                        step(nc.vector.reciprocal(cols[:, VAR], cols[:, VAR]))
                        step(nc.vector.tensor_tensor(cols[:, GAMMA], cols[:, GAMMA], cols[:, VAR], ALU.mult))
                        step(nc.vector.tensor_tensor(cols[:, B1], cols[:, B1], cols[:, MEAN], ALU.subtract))
                        step(nc.vector.tensor_tensor(cols[:, B1], cols[:, B1], cols[:, GAMMA], ALU.mult))
                        nc.vector.tensor_tensor(cols[:, BETA], cols[:, BETA], cols[:, B1], ALU.add).then_inc(S["bn"], 1)
                        dve.wait_ge(S["h_split"], NG)
                        for l in range(L):
                            for c in range(NG):
                                n = l * NG + c
                                dve.wait_ge(S["agg"], n + 1)
                                nc.vector.tensor_copy(z[:, :].rearrange("p (h n) -> p h n", h=2), halves(pZ[n % 2])).then_inc(S["z_ready"], 1)
                                dve.wait_ge(S["tr"], n + 1)
                                turned = pT[:, 0:CHUNK].rearrange("p (b d) -> p b d", b=GB)
                                if l < L - 1:
                                    split(l + 1, c, turned)
                                    dve.wait_ge(S["h_split"], n + NG + 1)
                                    dve.sem_inc(S["tr_used"], 1)
                                else:
                                    nc.vector.tensor_copy(hN[:, c * GB:(c + 1) * GB, :], turned).then_inc(S["tr_used"], 1)
                        dve.wait_ge(S["tr_used"], L * NG + 1)


        with ExitStack() as s:
            src_i = sb(s, "src_i", [P, NSUP, CT_TILES], i32)
            dst_i = sb(s, "dst_i", [P, NSUP, CT_TILES], i32)
            win_i = sb(s, "win_i", [P, NSUP], i32)
            tables(src_i, dst_i, win_i)
            end_stage()
            if stop >= 2:
                edges(src_i, dst_i, win_i)
                end_stage()
        alpha_sum = sb(ctx, "alpha_sum", [P, NB], fp32)
        hN = sb(ctx, "hN", [P, NB, D], fp32)
        stages = [lambda: edge_softmax(hN), lambda: residual("r0", hN, first=True, loops=ALU.add),
                  lambda: gat(0, hN), lambda: gat(1, hN), lambda: gat(2, hN),
                  lambda: residual("r1", hN, loops=ALU.subtract), lambda: local_attention(hN), lambda: residual("r2", hN, loops=ALU.add),
                  lambda: gin(hN), lambda: residual("r3", hN, last=True)]
        for stage in stages[0:max(0, stop - 2)]:
            stage()
            end_stage()


_INS = ['x', 'src', 'dst', 'edge_attr_128', 'L0_gnn_Wq_w', 'L0_gnn_Wq_b', 'L0_gnn_Wk_w', 'L0_gnn_Wk_b', 'L0_gnn_Wv_w',
        'L0_gnn_Wv_b', 'L0_gnn_We_w', 'L0_gnn_We_b', 'L0_gnn_a_w', 'L0_gnn_a_b', 'L1_gnn_W', 'L1_gnn_a_src',
        'L1_gnn_a_dst', 'L1_gnn_b', 'L2_gnn_high_atts', 'L2_gnn_diff_atts', 'L3_gnn_W1', 'L3_gnn_b1', 'L3_gnn_gamma',
        'L3_gnn_beta', 'L3_gnn_bn_mean', 'L3_gnn_bn_var', 'L3_gnn_W2', 'L3_gnn_b2']


def kernel(**inputs):
    import concourse.bacc as bacc
    from concourse.bass_utils import run_bass_kernel_spmd

    nc = bacc.Bacc("TRN2", target_bir_lowering=False, num_devices=1)
    arrays, aps = {}, {}
    for name in _INS:
        a = np.ascontiguousarray(inputs[name])
        arrays[f"in_{name}"] = a
        aps[name] = nc.dram_tensor(f"in_{name}", a.shape, mybir.dt.from_np(a.dtype), kind="ExternalInput").ap()
    out = nc.dram_tensor("out_x", (N, D), fp32, kind="ExternalOutput").ap()
    build(nc, aps, out)
    r = run_bass_kernel_spmd(nc, [arrays], core_ids=[0])
    return r.results[0]["out_x"]
```
